# Optimizing a Trainium2 kernel written in Bass

```python
import numpy as np
import jax
import jax.numpy as jnp

def _softmax(x, axis=-1):
    return jax.nn.softmax(x, axis=axis)

def _gelu(x):
    return jax.nn.gelu(x, approximate=True)

def _silu(x):
    return jax.nn.silu(x)

def _sigmoid(x):
    return jax.nn.sigmoid(x)

def _layernorm(x, axis=-1, eps=1e-05):
    m = jnp.mean(x, axis=axis, keepdims=True)
    v = jnp.var(x, axis=axis, keepdims=True)
    return (x - m) / jnp.sqrt(v + eps)

def _scatter_add(tgt, idx, src, axis=0):
    return tgt.at[idx].add(src)

def _segment_sum(src, seg, n):
    return jax.ops.segment_sum(src, seg, n)
kernel_name = 'mk_flamingo_gated_d2_seqx_r8_13758d'

def setup_inputs(seed: int=0):
    np.random.seed(seed)
    _w = jnp.asarray

    def _rec_inputs():
        import jax
        import jax.numpy as jnp
        _rk = jax.random.key(seed)
        x = 7.22e-05 + 1 * jax.random.normal(jax.random.fold_in(_rk, 1), (32, 64, 512), jnp.float32)
        _lenS = 64 - jax.random.randint(jax.random.fold_in(_rk, 7), (32,), 0, max(1, 64 // 4) + 1, jnp.int32)
        _lenS2 = 64 - jax.random.randint(jax.random.fold_in(_rk, 8), (32,), 0, max(1, 64 // 4) + 1, jnp.int32)
        _ctx_4096P = jax.random.normal(jax.random.fold_in(_rk, 11), (32, 16, 512), jnp.float32)
        _ctx_4096c = jax.random.dirichlet(jax.random.fold_in(_rk, 511), 0.3 * jnp.ones((16,), jnp.float32), (32, 64))
        _ctx_4096t = jnp.einsum('bsk,bkd->bsd', _ctx_4096c, _ctx_4096P)
        _ctx_4096t = _ctx_4096t * jax.lax.rsqrt(jnp.mean(jnp.square(_ctx_4096t)) + 1e-12) * 0.953939
        ctx_4096 = 4.13588e-05 + 0.999923 * (_ctx_4096t + 0.3 * jax.random.normal(jax.random.fold_in(_rk, 611), (32, 64, 512), jnp.float32))
        _g = jax.random.normal(jax.random.fold_in(_rk, 9001), (2, 2), jnp.float32)
        _g = jnp.sign(_g) * jnp.maximum(jnp.abs(_g), 1.0) + (_g == 0) * 1.0
        g_xattn = _g[0]
        g_ffn = _g[1]
        return (x, ctx_4096, g_xattn, g_ffn)
    x, ctx_4096, g_xattn, g_ffn = _rec_inputs()

    def _L0_xattn_setup():
        import jax, jax.numpy as jnp
        import numpy as np
        HEADS = 8
        WINDOW = 16

        def _pointwise(W, b, t):
            return jnp.einsum('oc,bct->bot', W, t) + b[None, :, None]
        key = jax.random.key(seed)
        ks = jax.random.split(key, 10)
        B, C, T = (4, 64, 512)
        s = 0.02
        return {'x': jax.random.normal(ks[0], (B, C, T), jnp.float32), 'cond': jax.random.normal(ks[1], (B, C, T), jnp.float32), 'Wq': jax.random.normal(ks[2], (C, C), jnp.float32) * s, 'bq': jnp.zeros((C,), jnp.float32), 'Wk': jax.random.normal(ks[3], (C, C), jnp.float32) * s, 'bk': jnp.zeros((C,), jnp.float32), 'Wv': jax.random.normal(ks[4], (C, C), jnp.float32) * s, 'bv': jnp.zeros((C,), jnp.float32), 'Wo': jax.random.normal(ks[5], (C, C), jnp.float32) * s, 'bo': jnp.zeros((C,), jnp.float32)}
    _L0_xattn_all = _L0_xattn_setup()
    _L0_xattn_in = {k: v for k, v in _L0_xattn_all.items() if k in ('Wq', 'bq', 'Wk', 'bk', 'Wv', 'bv', 'Wo', 'bo')}
    del _L0_xattn_all

    def _L0_ffn_setup():
        import jax, jax.numpy as jnp
        import numpy as np
        HIDDEN = 512
        MOE_INTER = 128
        SHARED_INTER = 512
        NUM_EXPERTS = 16
        TOP_K = 2

        def _moe_forward(x, gate_w, w_gate_up, w_down, shared_w_gate_up, shared_w_down):
            orig_shape = x.shape
            x2 = x.reshape(-1, orig_shape[-1])
            gu_s = x2 @ shared_w_gate_up.T
            g_s, u_s = jnp.split(gu_s, 2, axis=-1)
            shared_out = jax.nn.silu(g_s) * u_s @ shared_w_down.T
            logits = x2 @ gate_w.T
            probs = jax.nn.softmax(logits, axis=-1)
            topk_vals, topk_idx = jax.lax.top_k(probs, TOP_K)
            topk_vals = topk_vals / jnp.sum(topk_vals, axis=-1, keepdims=True)
            combine = jnp.sum(jax.nn.one_hot(topk_idx, NUM_EXPERTS, dtype=x2.dtype) * topk_vals[..., None], axis=1)
            gu = jnp.einsum('th,eih->eti', x2, w_gate_up)
            g, u = jnp.split(gu, 2, axis=-1)
            act = jax.nn.silu(g) * u
            out_e = jnp.einsum('eti,ehi->eth', act, w_down)
            moe_out = jnp.einsum('eth,te->th', out_e, combine)
            return (moe_out + shared_out).reshape(orig_shape)
        key = jax.random.key(seed)
        ks = jax.random.split(key, 6)
        s = 0.02
        hidden_states = jax.random.normal(ks[0], (2, 256, HIDDEN), dtype=jnp.float32)
        gate_w = jax.random.normal(ks[1], (NUM_EXPERTS, HIDDEN), dtype=jnp.float32) * s
        w_gate_up = jax.random.normal(ks[2], (NUM_EXPERTS, 2 * MOE_INTER, HIDDEN), dtype=jnp.float32) * s
        w_down = jax.random.normal(ks[3], (NUM_EXPERTS, HIDDEN, MOE_INTER), dtype=jnp.float32) * s
        shared_w_gate_up = jax.random.normal(ks[4], (2 * SHARED_INTER, HIDDEN), dtype=jnp.float32) * s
        shared_w_down = jax.random.normal(ks[5], (HIDDEN, SHARED_INTER), dtype=jnp.float32) * s
        return {'hidden_states': hidden_states, 'gate_w': gate_w, 'w_gate_up': w_gate_up, 'w_down': w_down, 'shared_w_gate_up': shared_w_gate_up, 'shared_w_down': shared_w_down}
    _L0_ffn_all = _L0_ffn_setup()
    _L0_ffn_in = {k: v for k, v in _L0_ffn_all.items() if k in ('gate_w', 'w_gate_up', 'w_down', 'shared_w_gate_up', 'shared_w_down')}
    del _L0_ffn_all

    def _L1_xattn_setup():
        import jax, jax.numpy as jnp
        import numpy as np
        NUM_HEADS = 8

        def _proj(W, b, x):
            return jnp.einsum('oi,bil->bol', W, x) + b[:, None]
        key = jax.random.key(seed)
        ks = jax.random.split(key, 11)
        B, D, L = (16, 64, 512)
        s = 1.0 / np.sqrt(D).astype(np.float32)
        return {'x_query': jax.random.normal(ks[0], (B, D, L), jnp.float32), 'x_key': jax.random.normal(ks[1], (B, D, L), jnp.float32), 'x_value': jax.random.normal(ks[2], (B, D, L), jnp.float32), 'Wq': jax.random.normal(ks[3], (D, D), jnp.float32) * s, 'bq': jax.random.normal(ks[4], (D,), jnp.float32) * 0.01, 'Wk': jax.random.normal(ks[5], (D, D), jnp.float32) * s, 'bk': jax.random.normal(ks[6], (D,), jnp.float32) * 0.01, 'Wv': jax.random.normal(ks[7], (D, D), jnp.float32) * s, 'bv': jax.random.normal(ks[8], (D,), jnp.float32) * 0.01, 'Wo': jax.random.normal(ks[9], (D, D), jnp.float32) * s, 'bo': jax.random.normal(ks[10], (D,), jnp.float32) * 0.01}
    _L1_xattn_all = _L1_xattn_setup()
    _L1_xattn_in = {k: v for k, v in _L1_xattn_all.items() if k in ('Wq', 'bq', 'Wk', 'bk', 'Wv', 'bv', 'Wo', 'bo')}
    del _L1_xattn_all

    def _L1_ffn_setup():
        import jax, jax.numpy as jnp
        import numpy as np
        B_L, B_H = (4, 8)
        LIN_SLOPE, LIN_INTER, EST_T = (1.0, 0.0, 64.0)
        BATCH, SEQ, IN_F, OUT_F = (4, 256, 512, 512)
        MAX_BITS = 8

        def dequant_kbit(qweight, lut, bit):
            O, I32 = (qweight.shape[1], qweight.shape[2])
            shifts = jnp.arange(32, dtype=jnp.int32)
            idx = jnp.zeros((O, I32 * 32), dtype=jnp.int32)
            for p in range(bit):
                bits = (qweight[p][:, :, None] >> shifts & 1).reshape(O, I32 * 32)
                idx = idx | bits << p
            return jnp.take_along_axis(lut, idx, axis=1)
        key = jax.random.key(seed)
        k = jax.random.split(key, 5)
        x = jax.random.normal(k[0], (BATCH, SEQ, IN_F), dtype=jnp.float32)
        qweight = jax.random.randint(k[1], (MAX_BITS, OUT_F, IN_F // 32), 0, 2147483647, dtype=jnp.int32)
        lut4 = jax.random.normal(k[2], (OUT_F, 2 ** B_L), dtype=jnp.float32) * 0.02
        lut8 = jax.random.normal(k[3], (OUT_F, 2 ** B_H), dtype=jnp.float32) * 0.02
        bias = jax.random.normal(k[4], (OUT_F,), dtype=jnp.float32) * 0.01
        return {'x': x, 'qweight': qweight, 'lut4': lut4, 'lut8': lut8, 'bias': bias}
    _L1_ffn_all = _L1_ffn_setup()
    _L1_ffn_in = {k: v for k, v in _L1_ffn_all.items() if k in ('qweight', 'lut4', 'lut8', 'bias')}
    del _L1_ffn_all
    return {'x': x, 'ctx_4096': ctx_4096, 'g_xattn': g_xattn, 'g_ffn': g_ffn, 'L0_xattn_Wq': _L0_xattn_in['Wq'], 'L0_xattn_bq': _L0_xattn_in['bq'], 'L0_xattn_Wk': _L0_xattn_in['Wk'], 'L0_xattn_bk': _L0_xattn_in['bk'], 'L0_xattn_Wv': _L0_xattn_in['Wv'], 'L0_xattn_bv': _L0_xattn_in['bv'], 'L0_xattn_Wo': _L0_xattn_in['Wo'], 'L0_xattn_bo': _L0_xattn_in['bo'], 'L0_ffn_gate_w': _L0_ffn_in['gate_w'], 'L0_ffn_w_gate_up': _L0_ffn_in['w_gate_up'], 'L0_ffn_w_down': _L0_ffn_in['w_down'], 'L0_ffn_shared_w_gate_up': _L0_ffn_in['shared_w_gate_up'], 'L0_ffn_shared_w_down': _L0_ffn_in['shared_w_down'], 'L1_xattn_Wq': _L1_xattn_in['Wq'], 'L1_xattn_bq': _L1_xattn_in['bq'], 'L1_xattn_Wk': _L1_xattn_in['Wk'], 'L1_xattn_bk': _L1_xattn_in['bk'], 'L1_xattn_Wv': _L1_xattn_in['Wv'], 'L1_xattn_bv': _L1_xattn_in['bv'], 'L1_xattn_Wo': _L1_xattn_in['Wo'], 'L1_xattn_bo': _L1_xattn_in['bo'], 'L1_ffn_qweight': _L1_ffn_in['qweight'], 'L1_ffn_lut4': _L1_ffn_in['lut4'], 'L1_ffn_lut8': _L1_ffn_in['lut8'], 'L1_ffn_bias': _L1_ffn_in['bias']}

def reference(x, ctx_4096, g_xattn, g_ffn, L0_xattn_Wq, L0_xattn_bq, L0_xattn_Wk, L0_xattn_bk, L0_xattn_Wv, L0_xattn_bv, L0_xattn_Wo, L0_xattn_bo, L0_ffn_gate_w, L0_ffn_w_gate_up, L0_ffn_w_down, L0_ffn_shared_w_gate_up, L0_ffn_shared_w_down, L1_xattn_Wq, L1_xattn_bq, L1_xattn_Wk, L1_xattn_bk, L1_xattn_Wv, L1_xattn_bv, L1_xattn_Wo, L1_xattn_bo, L1_ffn_qweight, L1_ffn_lut4, L1_ffn_lut8, L1_ffn_bias):
    import jax
    import jax.numpy as jnp

    def _L0_xattn_ref(x, cond, Wq, bq, Wk, bk, Wv, bv, Wo, bo):
        import jax, jax.numpy as jnp
        import numpy as np
        HEADS = 8
        WINDOW = 16

        def _pointwise(W, b, t):
            return jnp.einsum('oc,bct->bot', W, t) + b[None, :, None]
        B, C, T = x.shape
        H, W = (HEADS, WINDOW)
        hd = C // H
        scale = hd ** (-0.5)
        pad_left = W // 2
        pad_right = W - pad_left - 1
        q = _pointwise(Wq, bq, x)
        k = _pointwise(Wk, bk, cond)
        v = _pointwise(Wv, bv, cond)
        k = jnp.pad(k, ((0, 0), (0, 0), (pad_left, pad_right)))
        v = jnp.pad(v, ((0, 0), (0, 0), (pad_left, pad_right)))
        idx = jnp.arange(T)[:, None] + jnp.arange(W)[None, :]
        k_win = k[:, :, idx].reshape(B, H, hd, T, W)
        v_win = v[:, :, idx].reshape(B, H, hd, T, W)
        qh = q.reshape(B, H, hd, T)
        dots = jnp.einsum('bhdt,bhdtw->bhtw', qh, k_win) * scale
        attn = jax.nn.softmax(dots, axis=-1)
        out = jnp.einsum('bhtw,bhdtw->bhdt', attn, v_win)
        out = out.reshape(B, C, T)
        return _pointwise(Wo, bo, out)

    def _L0_ffn_ref(hidden_states, gate_w, w_gate_up, w_down, shared_w_gate_up, shared_w_down):
        import jax, jax.numpy as jnp
        import numpy as np
        HIDDEN = 512
        MOE_INTER = 128
        SHARED_INTER = 512
        NUM_EXPERTS = 16
        TOP_K = 2

        def _moe_forward(x, gate_w, w_gate_up, w_down, shared_w_gate_up, shared_w_down):
            orig_shape = x.shape
            x2 = x.reshape(-1, orig_shape[-1])
            gu_s = x2 @ shared_w_gate_up.T
            g_s, u_s = jnp.split(gu_s, 2, axis=-1)
            shared_out = jax.nn.silu(g_s) * u_s @ shared_w_down.T
            logits = x2 @ gate_w.T
            probs = jax.nn.softmax(logits, axis=-1)
            topk_vals, topk_idx = jax.lax.top_k(probs, TOP_K)
            topk_vals = topk_vals / jnp.sum(topk_vals, axis=-1, keepdims=True)
            combine = jnp.sum(jax.nn.one_hot(topk_idx, NUM_EXPERTS, dtype=x2.dtype) * topk_vals[..., None], axis=1)
            gu = jnp.einsum('th,eih->eti', x2, w_gate_up)
            g, u = jnp.split(gu, 2, axis=-1)
            act = jax.nn.silu(g) * u
            out_e = jnp.einsum('eti,ehi->eth', act, w_down)
            moe_out = jnp.einsum('eth,te->th', out_e, combine)
            return (moe_out + shared_out).reshape(orig_shape)
        return _moe_forward(hidden_states, gate_w, w_gate_up, w_down, shared_w_gate_up, shared_w_down)

    def _L1_xattn_ref(x_query, x_key, x_value, Wq, bq, Wk, bk, Wv, bv, Wo, bo):
        import jax, jax.numpy as jnp
        import numpy as np
        NUM_HEADS = 8

        def _proj(W, b, x):
            return jnp.einsum('oi,bil->bol', W, x) + b[:, None]
        B, D, L = x_query.shape
        h = NUM_HEADS
        Lh = L // h
        q = _proj(Wq, bq, x_query)
        k = _proj(Wk, bk, x_key)
        v = _proj(Wv, bv, x_value)
        qh = q.reshape(B, D, h, Lh).transpose(2, 0, 1, 3)
        kh = k.reshape(B, D, h, Lh).transpose(2, 0, 1, 3)
        vh = v.reshape(B, D, h, Lh).transpose(2, 0, 1, 3)
        scale = 1.0 / jnp.sqrt(jnp.asarray(Lh, x_query.dtype))
        scores = jnp.einsum('hbdk,hbek->hbde', qh, kh) * scale
        p = jax.nn.softmax(scores, axis=-1)
        xh = jnp.einsum('hbde,hbek->hbdk', p, vh)
        x = xh.transpose(1, 2, 0, 3).reshape(B, D, L)
        return _proj(Wo, bo, x)

    def _L1_ffn_ref(x, qweight, lut4, lut8, bias):
        import jax, jax.numpy as jnp
        import numpy as np
        B_L, B_H = (4, 8)
        LIN_SLOPE, LIN_INTER, EST_T = (1.0, 0.0, 64.0)
        BATCH, SEQ, IN_F, OUT_F = (4, 256, 512, 512)
        MAX_BITS = 8

        def dequant_kbit(qweight, lut, bit):
            O, I32 = (qweight.shape[1], qweight.shape[2])
            shifts = jnp.arange(32, dtype=jnp.int32)
            idx = jnp.zeros((O, I32 * 32), dtype=jnp.int32)
            for p in range(bit):
                bits = (qweight[p][:, :, None] >> shifts & 1).reshape(O, I32 * 32)
                idx = idx | bits << p
            return jnp.take_along_axis(lut, idx, axis=1)
        e = jnp.linalg.norm(x, axis=-1) * LIN_SLOPE + LIN_INTER
        mask = e > EST_T
        w_l = dequant_kbit(qweight, lut4, B_L)
        w_h = dequant_kbit(qweight, lut8, B_H)
        y_l = jnp.einsum('bsi,oi->bso', x, w_l)
        y_h = jnp.einsum('bsi,oi->bso', x, w_h)
        y = jnp.where(mask[..., None], y_h, y_l) + bias
        return y
    x = x + jnp.tanh(g_xattn[0]) * _L0_xattn_ref(_layernorm(x, axis=-1), ctx_4096, L0_xattn_Wq, L0_xattn_bq, L0_xattn_Wk, L0_xattn_bk, L0_xattn_Wv, L0_xattn_bv, L0_xattn_Wo, L0_xattn_bo)
    x = x + jnp.tanh(g_ffn[0]) * _L0_ffn_ref(_layernorm(x, axis=-1), L0_ffn_gate_w, L0_ffn_w_gate_up, L0_ffn_w_down, L0_ffn_shared_w_gate_up, L0_ffn_shared_w_down)
    x = x + jnp.tanh(g_xattn[1]) * _L1_xattn_ref(_layernorm(x, axis=-1), ctx_4096, ctx_4096, L1_xattn_Wq, L1_xattn_bq, L1_xattn_Wk, L1_xattn_bk, L1_xattn_Wv, L1_xattn_bv, L1_xattn_Wo, L1_xattn_bo)
    x = x + jnp.tanh(g_ffn[1]) * _L1_ffn_ref(_layernorm(x, axis=-1), L1_ffn_qweight, L1_ffn_lut4, L1_ffn_lut8, L1_ffn_bias)
    return x

_drawn_inputs = setup_inputs


def setup_inputs(seed=0):
    import zlib

    import numpy as np

    out = dict(_drawn_inputs(seed))
    spreads = {'g_ffn': (-1.0, 0.6),
     'L0_xattn_bq': (0.0, 0.8),
     'L0_xattn_bk': (0.0, 0.8),
     'L0_xattn_bv': (0.0, 0.752),
     'L0_xattn_bo': (0.0, 0.1)}
    factors = {'L0_xattn_Wq': 8.0,
     'L0_xattn_Wk': 8.0,
     'L0_xattn_Wv': 8.0,
     'L0_xattn_Wo': 4.133,
     'L0_ffn_gate_w': 4.55,
     'L0_ffn_w_gate_up': 4.263,
     'L0_ffn_w_down': 4.265,
     'L1_xattn_bq': 49.58,
     'L1_xattn_bk': 42.31,
     'L1_xattn_bv': 64.0,
     'L1_xattn_bo': 5.88,
     'L1_ffn_bias': 7.576,
     'L0_ffn_shared_w_gate_up': 2.778,
     'L0_ffn_shared_w_down': 2.772}
    for name, (base, spread) in spreads.items():
        noise = np.random.default_rng([zlib.crc32(name.encode()), seed]).standard_normal(out[name].shape)
        drawn = base * np.exp(spread * noise) if base else spread * noise
        out[name] = jnp.asarray(drawn.astype(out[name].dtype))
    for name, factor in factors.items():
        out[name] = (out[name] * factor).astype(out[name].dtype)
    return out
```

```python
from contextlib import ExitStack

import concourse.bass as bass
from concourse import mybir

P = 128
B, C, T = 32, 64, 512
TILES = B * C // P
TC = T // P
HEADS0, WINDOW = 8, 16
HD = C // HEADS0
GROUPS = 2 * HEADS0
LEFT = WINDOW // 2
PADDED = T + WINDOW - 1
HEADS1 = 8
LH = T // HEADS1
EXPERTS, EI, SI = 16, 128, 512
SLOT_TILES = 48
SLOTS = SLOT_TILES * P
UNROLL = 3
CODES = 16
EPS = 1e-5
WORK = 10750

ALU = mybir.AluOpType
ACT = mybir.ActivationFunctionType
AX = mybir.AxisListType
F32, I32, U32 = mybir.dt.float32, mybir.dt.int32, mybir.dt.uint32

POOL_W = (2, 6, 10, 14)
DVE_W = tuple(w for w in range(WINDOW) if w not in POOL_W)
ZD, ZP = 4, 2
PAIRS = WINDOW // 2
A_LINKS = 3
R_LINKS = 4


def later(i):
    return not (isinstance(i, int) and i == 0)


def build(nc, a):
    ctx = ExitStack()
    with ctx:
        def sb(name, shape, dt=F32):
            return ctx.enter_context(nc.sbuf_tensor(name, shape, dt))

        def sem(name):
            return ctx.enter_context(nc.semaphore(name))

        X = sb("X", [P, TILES, T])
        w_att = sb("w_att", [P, 9, P])
        bias_att = sb("bias_att", [P, 8])
        ident = sb("ident", [P, P])
        gates = sb("gates", [P, 4])
        gbias = sb("gbias", [P, 2])
        consts = sb("consts", [P, 2])
        stats = sb("stats", [P, 6])
        mv = sb("mv", [P, 2])
        veps = sb("veps", [P, 1])
        held = sb("held", [P, 1])
        rstd = sb("rstd", [P, 1])
        ctx_t = sb("ctx_t", [P, T])
        xn = sb("xn", [P, T])
        xo = sb("xo", [P, T])
        onehot = sb("onehot", [P, TILES + 1, 2, EXPERTS])
        margin = sb("margin", [P, TILES])
        comb = sb("comb", [P, 2, TILES])
        slot_of = sb("slot_of", [P, TILES, 2], U32)
        cols = sb("cols", [P, 4], U32)
        w_exp = sb("w_exp", [P, EXPERTS, TC * 2 * EI + T])
        w_gu = w_exp[:, :, 0:TC * 2 * EI].rearrange("p e (k n) -> p e k n", k=TC)
        w_dn = w_exp[:, :, TC * 2 * EI:]
        work = sb("work", [P, WORK])
        ps = ctx.enter_context(nc.psum_tensor("ps", [P, 8, 512], F32))

        used = {}

        def carve(area, key, n):
            at = used.get(key, 0)
            used[key] = at + n
            assert used[key] <= area.shape[1], (key, used[key])
            return area[:, at:at + n]

        w_shared = sb("w_shared", [P, TC * 2 * SI + 4 * T])
        w_sgu = w_shared[:, 0:TC * 2 * SI].rearrange("p (k n) -> p k n", k=TC)
        w_sdn = w_shared[:, TC * 2 * SI:].rearrange("p (k n) -> p k n", k=4)

        w1 = lambda n: carve(work, 1, n)
        q = w1(T)
        k_pad = w1(PADDED + 1)
        v_pad = w1(PADDED + 1)
        z = [w1(T) for _ in range(ZD + ZP)]
        diff = w1(TC * WINDOW * GROUPS)
        pexp = [w1(T) for _ in range(2)]
        x2 = w1(T)
        x2T = w1(T)
        th = w1(T)
        act = th
        w_router = w1(TC * EXPERTS).rearrange("p (k e) -> p k e", k=TC)
        head_sum = w1(GROUPS)
        iota16 = w1(EXPERTS)
        smax = w1(TC * GROUPS)
        ssum = w1(TC * GROUPS)
        srec = w1(TC * GROUPS)
        lg = w1(EXPERTS)
        top = w1(8)
        topi = w1(8).bitcast(U32)
        topf = w1(2)
        actT = x2T

        w2 = lambda n: carve(work, 2, n)
        tri = w2(P)
        ones = w2(P)
        chosen = w2((TILES + 1) * EXPERTS).rearrange("p (i e) -> p i e", e=EXPERTS)
        prod = w2(TILES * 2 * EXPERTS).rearrange("p (i k e) -> p i k e", k=2, e=EXPERTS)
        pos = w2(TILES * 2)
        base = w2(TILES * 2)
        posi = w2(TILES * 2).bitcast(I32)
        rowi = w2(TILES * 2).bitcast(I32)
        tili = w2(TILES * 2).bitcast(I32)
        rowf = w2(TILES * 2)
        tilf = w2(TILES * 2)
        cnt = w2(EXPERTS)
        cnti = w2(EXPERTS).bitcast(I32)
        cum = [w2(EXPERTS) for _ in range(2)]
        ntile = w2(EXPERTS)
        first = w2(EXPERTS)
        token = w2(TILES).bitcast(I32)
        ids = w2(SLOT_TILES).bitcast(U32)
        zeros48 = w2(SLOT_TILES).bitcast(U32)
        slot_no = w2(SLOT_TILES)
        exp_of = w2(SLOT_TILES)
        exp_id = w2(SLOT_TILES).bitcast(I32)
        at_most = prod[0:1].rearrange("p i k e -> p (i k e)")
        e1 = w2(TILES)
        den = w2(TILES)
        lut = w2(4 * CODES).rearrange("p (o c) -> p o c", o=4)
        words = w2(4 * 4 * 16).bitcast(I32).rearrange("p (b o w) -> p b o w", b=4, o=4)
        xg = [w2(T) for _ in range(UNROLL)]
        xT = [w2(T) for _ in range(UNROLL)]
        th2 = [w2(EI) for _ in range(UNROLL)]
        act2 = [w2(EI) for _ in range(UNROLL)]
        act2T = [w2(EI) for _ in range(UNROLL)]
        ysb = [w2(T) for _ in range(UNROLL)]
        w2s = lambda n: carve(w_shared, "2s", n)
        code = w2s(4 * T).rearrange("p (o i) -> p o i", o=4)
        picked = w2s(4 * T).rearrange("p (o i) -> p o i", o=4)
        codes = w2s(CODES)
        bits = picked.rearrange("p o i -> p (o i)").bitcast(I32).rearrange("p (o w s) -> p o w s", o=4, w=16)
        w3 = lambda n: carve(w_exp.rearrange("p e n -> p (e n)"), 3, n)
        wl = work[:, WORK - 4 * T:WORK].rearrange("p (o i) -> p o i", o=4)
        assert used[2] <= WORK - 4 * T, used
        wlT = w3(4 * T).rearrange("p (k o) -> p k o", k=4)
        yg = [w3(T) for _ in range(2)]
        qT = w3(T)
        kT = w3(T)
        vv = [w3(T) for _ in range(2)]
        pr = w3(T)
        prT = w3(T)
        xh = w3(T)
        xf = w3(T)
        xfT = w3(T)
        obuf = w3(T)
        m3 = w3(8)
        s3 = w3(8)
        r3 = w3(8)
        bqk = w3(2 * P).rearrange("p (a o) -> p a o", a=2)
        brow = w3(T)
        orow = w3(P)

        x2_rows = nc.dram_tensor("x2_rows", [B * C, T], F32, kind="Internal").ap()
        ids_dram = nc.dram_tensor("ids_dram", [SLOTS, 1], U32, kind="Internal").ap()
        y_slots = nc.dram_tensor("y_slots", [SLOTS, T], F32, kind="Internal").ap()
        ids_rows = ids_dram.rearrange("(r s) o -> r (s o)", s=SLOT_TILES)
        y_rows = y_slots.rearrange("(r s) d -> r s d", s=SLOT_TILES)
        x_rows = a["x"].rearrange("b c t -> (b c) t")
        c_rows = a["ctx"].rearrange("b c t -> (b c) t")
        o_rows = a["out"].rearrange("b c t -> (b c) t")

        S = {}
        for name in """zeroed small_loaded shared_loaded iota_done ident_done gates_done gbias_done x_loaded ctx_loaded
                experts_loaded stats_ready veps_ready rstd_ready normed projected copied zd_ready zp_ready qk_done
                scores_read diff_read exp_done prob_ready pexp_ready expanded z2_ready pair_summed wo_done xo_ready
                x1_ready a_link x2_stored x2_turned x2T_ready logits_done logits_read r_link routed g_done u_done
                tanh_done act_ready act_turned actT_ready down_done ffn_added
                c_link tri_ready ranked slots_ready e1_done comb_done ids_zeroed ids_scattered ids_loaded tables_loaded
                experts_known codes_ready picked_ready added
                y_col wl_turned wlT_ready const3_loaded const3_zeroed y1_gathered y2_gathered mixed qkT_done
                qk3_ready v_done pv_ready halves_ready half_mixed top_ready s3_done d_link d3_ready e3_done p3_ready pT_done av_done
                xh_ready wo3_done xo3_ready x3_ready xf_turned xfT_ready y3_done out_ready out_stored""".split():
            S[name] = sem(name)
        for u in range(UNROLL):
            for name in "gathered turned xT_ready gu_done th2_done act2_ready act2_turned act2T_ready dn_done ysb_ready y_stored col_ready".split():
                S[f"{name}{u}"] = sem(f"{name}{u}")
        s = type("Sems", (), S)

        def S_(name):
            return S[name]


        N_SM = 2 * 9 + 2 * 8 + 2
        block = ctx.enter_context(nc.Block())

        @block.sync
        def _(sp):
            small = 0

            def load(dst, src, sm=s.small_loaded):
                sp.dma_start(dst, src).then_inc(sm, 16)

            load(X[:, 0, :], x_rows[0:P, :], s.x_loaded)
            load(ctx_t[:, :], c_rows[0:P, :], s.ctx_loaded)
            sp.wait_ge(s.zeroed, 1)
            mats = ["wq0", "wk0", "wv0", "wo0", "wq1", "wk1", "wv1", "wv1", "wo1"]
            for n, name in enumerate(mats):
                for h in range(2):
                    c = (1 - h) if n == 7 else h
                    load(w_att[h * C:(h + 1) * C, n, c * C:(c + 1) * C], a[name])
                    small += 1
            for n, name in enumerate(["bq0", "bk0", "bv0", "bo0", "bq1", "bk1", "bv1", "bo1"]):
                for h in range(2):
                    load(bias_att[h * C:(h + 1) * C, n:n + 1], a[name].rearrange("(c o) -> c o", o=1))
                    small += 1
            load(gates[:, 0:4], a["gate4"].partition_broadcast(P))
            load(w_router, a["w_router"])
            small += 2
            assert small == N_SM
            load(w_sgu, a["w_sgu"], s.shared_loaded)
            load(w_sdn, a["w_sdn"], s.shared_loaded)

            def phase1(i):
                sp.wait_ge(s.x_loaded, 16 * (i + 1))
                sp.dma_start(X[:, bass.ds(i + 1, 1), :], x_rows[bass.ds((i + 1) * P, P), :]).then_inc(s.x_loaded, 16)
                sp.dma_start(w_exp[:, bass.ds(i, 1), 0:TC * 2 * EI],
                             a["w_gu"][bass.ds(i * P, P), :]).then_inc(s.experts_loaded, 16)
                sp.dma_start(w_exp[:, bass.ds(i, 1), TC * 2 * EI:],
                             a["w_dn"][bass.ds(i * P, P), :]).then_inc(s.experts_loaded, 16)
                sp.wait_ge(s.projected, 3 * (i + 1))
                sp.dma_start(ctx_t[:, :], c_rows[bass.ds((i + 1) * P, P), :]).then_inc(s.ctx_loaded, 16)
                store_x2(i)

            def store_x2(i):
                sp.wait_ge(s.normed, 2 * i + 2)
                sp.dma_start(x2_rows[bass.ds(i * P, P), :], x2).then_inc(s.x2_stored, 16)

            with sp.Fori(0, TILES - 1) as i:
                phase1(i)
            last = TILES - 1
            sp.dma_start(w_exp[:, last, 0:TC * 2 * EI], a["w_gu"][last * P:, :]).then_inc(s.experts_loaded, 16)
            sp.dma_start(w_exp[:, last, TC * 2 * EI:], a["w_dn"][last * P:, :]).then_inc(s.experts_loaded, 16)
            store_x2(last)
            sp.wait_ge(s.projected, 3 * TILES)
            sp.dma_start(ctx_t[:, :], c_rows[0:P, :]).then_inc(s.ctx_loaded, 16)
            sp.wait_ge(s.ffn_added, TILES)
            load(lut, a["lut4"], s.tables_loaded)
            load(words, a["words"], s.tables_loaded)
            sp.wait_ge(s.tri_ready, 5)
            load(ids_rows, zeros48, s.ids_zeroed)
            sp.wait_ge(s.ids_scattered, 16 * 2 * TILES)
            load(ids, ids_rows, s.ids_loaded)
            with sp.Fori(0, SLOT_TILES // UNROLL) as it:
                for u in range(UNROLL):
                    sp.wait_ge(S_(f"ysb_ready{u}"), it + 1)
                    sp.dma_start(y_rows[:, bass.ds(UNROLL * it + u, 1), :], ysb[u]).then_inc(S_(f"y_stored{u}"), 16)
            sp.wait_ge(s.const3_zeroed, 1)
            for h in range(2):
                for n, name in enumerate(["bq1", "bk1"]):
                    load(bqk[:, n, h * C:(h + 1) * C], a[name].partition_broadcast(P), s.const3_loaded)
            load(brow[0:1, :], a["bias"].rearrange("(r o) -> r o", r=1), s.const3_loaded)

            def out_tile(i):
                sp.wait_ge(s.out_ready, i + 1)
                sp.dma_start(o_rows[bass.ds(i * P, P), :], obuf).then_inc(s.out_stored, 16)

            with sp.Fori(0, TILES - 1) as i:
                sp.wait_ge(s.qkT_done, 2 * (i + 1))
                sp.wait_ge(s.v_done, 2 * (i + 1))
                sp.dma_start(ctx_t[:, :], c_rows[bass.ds((i + 1) * P, P), :]).then_inc(s.ctx_loaded, 16)
                out_tile(i)
            out_tile(last)
            sp.wait_ge(s.out_stored, 16 * TILES)
            sp.wait_ge(s.x2_stored, 16 * TILES)

        @block.gpsimd
        def _(pool):
            pool.memset(w_att[:, :, :], 0.0).then_inc(s.zeroed, 1)
            pool.memset(consts[:, 0:1], -0.5).then_inc(s.iota_done, 1)
            pool.memset(k_pad, 0.0).then_inc(s.iota_done, 1)
            pool.memset(v_pad, 0.0).then_inc(s.iota_done, 1)
            pool.memset(onehot[:, TILES, :, :], 0.0).then_inc(s.iota_done, 1)
            pool.iota(iota16, pattern=[[1, EXPERTS]], base=0, channel_multiplier=0,
                      allow_small_or_imprecise_dtypes=True).then_inc(s.iota_done, 1)
            pool.memset(ident[:, :], 0.0).then_inc(s.ident_done, 1)
            pool.memset(head_sum, 1.0).then_inc(s.ident_done, 1)
            pool.wait_ge(s.ident_done, 2)
            pool.affine_select(out=ident[:, :], in_=ident[:, :], compare_op=ALU.not_equal, fill=1.0, base=0,
                               pattern=[[-1, P]], channel_multiplier=1).then_inc(s.ident_done, 1)
            pool.affine_select(out=head_sum, in_=head_sum, compare_op=ALU.is_ge, fill=0.0, base=0,
                               pattern=[[-HD, GROUPS]], channel_multiplier=1).then_inc(s.ident_done, 1)
            pool.wait_ge(s.ident_done, 4)
            pool.affine_select(out=head_sum, in_=head_sum, compare_op=ALU.is_ge, fill=0.0, base=HD - 1,
                               pattern=[[HD, GROUPS]], channel_multiplier=-1).then_inc(s.ident_done, 1)

            def root(n):
                pool.wait_ge(s.stats_ready, 1)
                pool.sem_clear(s.stats_ready)
                pool.tensor_scalar(veps[:, :], mv[:, 1:2], EPS, None, ALU.add).then_inc(s.veps_ready, 1)
                pool.wait_ge(s.veps_ready, n + 1)
                pool.tensor_tensor(rstd[:, :], veps[:, :], consts[:, 0:1], ALU.pow).then_inc(s.rstd_ready, 1)

            def phase1(i):
                root(2 * i)
                pool.wait_ge(s.copied, 3 * i + 2)
                for n, w in enumerate(POOL_W):
                    if n >= ZP:
                        pool.wait_ge(s.qk_done, WINDOW * i + POOL_W[n - ZP] + 1)
                    else:
                        if later(i):
                            pool.wait_ge(s.wo_done, PAIRS * i)
                    pool.tensor_tensor(z[ZD + n % ZP], q, k_pad[:, w:w + T], ALU.mult).then_inc(s.zp_ready, 1)
                for k in range(PAIRS):
                    pool.wait_ge(s.z2_ready, WINDOW * i + 2 * k + 2)
                    if k >= ZP:
                        pool.wait_ge(s.wo_done, PAIRS * i + k - ZP + 1)
                    else:
                        pool.wait_ge(s.qk_done, WINDOW * (i + 1))
                    pool.tensor_tensor(z[ZD + k % ZP], z[2 * k % ZD], z[(2 * k + 1) % ZD],
                                       ALU.add).then_inc(s.pair_summed, 1)
                root(2 * i + 1)

            phase1(0)
            with pool.Fori(1, TILES) as i:
                phase1(i)

            pool.wait_ge(s.ffn_added, TILES)
            pool.wait_ge(s.x2_stored, 16 * TILES)
            pool.memset(ones, 1.0).then_inc(s.tri_ready, 1)
            pool.memset(tri, 1.0).then_inc(s.tri_ready, 1)
            pool.iota(token, pattern=[[P, TILES]], base=0, channel_multiplier=1).then_inc(s.tri_ready, 1)
            pool.iota(slot_no, pattern=[[1, SLOT_TILES]], base=0, channel_multiplier=0,
                      allow_small_or_imprecise_dtypes=True).then_inc(s.tri_ready, 1)
            pool.memset(zeros48, 0).then_inc(s.tri_ready, 1)
            pool.iota(codes, pattern=[[1, CODES]], base=0, channel_multiplier=0,
                      allow_small_or_imprecise_dtypes=True).then_inc(s.tri_ready, 1)
            pool.wait_ge(s.tri_ready, 6)
            pool.affine_select(out=tri, in_=tri, compare_op=ALU.is_ge, fill=0.0, base=-1,
                               pattern=[[1, P]], channel_multiplier=-1).then_inc(s.tri_ready, 1)
            pool.wait_ge(s.slots_ready, 1)
            pool.wait_ge(s.ids_zeroed, 16)
            for i in range(TILES):
                for k in range(2):
                    pool.indirect_dma_start(out=ids_dram, out_offset=bass.IndirectOffsetOnAxis(ap=slot_of[:, i, k:k + 1], axis=0),
                                            in_=token[:, i:i + 1], in_offset=None).then_inc(s.ids_scattered, 16)
            pool.memset(wl, 0.0).then_inc(s.added, 1)
            pool.wait_ge(s.ids_loaded, 16)
            def expert_turn(it):
                for u in range(UNROLL):
                    if later(it):
                        pool.wait_ge(S_(f"gathered{u}"), 16 * it)
                    if later(it):
                        pool.wait_ge(S_(f"turned{u}"), it)
                    pool.tensor_copy(cols[:, u:u + 1], ids[:, bass.ds(UNROLL * it + u, 1)]).then_inc(S_(f"col_ready{u}"), 1)
                    pool.wait_ge(S_(f"col_ready{u}"), 1)
                    pool.sem_clear(S_(f"col_ready{u}"))
                    pool.indirect_dma_start(out=xg[u], out_offset=None, in_=x2_rows,
                                            in_offset=bass.IndirectOffsetOnAxis(ap=cols[:, u:u + 1], axis=0)
                                            ).then_inc(S_(f"gathered{u}"), 16)
                pool.wait_ge(s.picked_ready, it + 1)
                pool.wait_ge(s.added, it + 1)
                pool.tensor_tensor(wl, wl, picked, ALU.add).then_inc(s.added, 1)

            expert_turn(0)
            with pool.Fori(1, SLOT_TILES // UNROLL) as it:
                expert_turn(it)
            for u in range(UNROLL):
                pool.wait_ge(S_(f"y_stored{u}"), 16 * (SLOT_TILES // UNROLL))
                pool.wait_ge(S_(f"dn_done{u}"), SLOT_TILES // UNROLL)
            pool.memset(orow[0:1, :], 1.0).then_inc(s.const3_zeroed, 1)

            def gather_tile(i):
                for k in range(2):
                    gathered = (s.y1_gathered, s.y2_gathered)[k]
                    if later(i):
                        pool.wait_ge(gathered, 16 * i)
                    pool.wait_ge(s.normed, 2 * TILES + 2 * i)
                    pool.tensor_copy(cols[:, k:k + 1], slot_of[:, bass.ds(i, 1), k]).then_inc(s.y_col, 1)
                    pool.wait_ge(s.y_col, 1)
                    pool.sem_clear(s.y_col)
                    pool.indirect_dma_start(out=yg[k], out_offset=None, in_=y_slots,
                                            in_offset=bass.IndirectOffsetOnAxis(ap=cols[:, k:k + 1], axis=0)
                                            ).then_inc(gathered, 16)
                root(2 * TILES + 2 * i)
                root(2 * TILES + 2 * i + 1)

            gather_tile(0)
            with pool.Fori(1, TILES) as i:
                gather_tile(i)
        @block.scalar
        def _(act_e):
            sc = act_e
            sc.wait_ge(s.small_loaded, 16 * N_SM)
            sc.activation(gates[:, :], gates[:, :], ACT.Tanh).then_inc(s.gates_done, 1)

            def turned(i):
                sc.wait_ge(s.x2_turned, i + 1)
                sc.activation(x2T, ps[:, 7, :], ACT.Copy).then_inc(s.x2T_ready, 1)

            def attention(i):
                for n, dst in enumerate((q, k_pad[:, LEFT:LEFT + T], v_pad[:, LEFT:LEFT + T])):
                    sc.wait_ge(s.projected, 3 * i + n + 1)
                    sc.activation(dst, ps[:, (0, 1, 4)[n], :], ACT.Identity,
                                  bias=bias_att[:, n:n + 1]).then_inc(s.copied, 1)

            def gate(i):
                sc.wait_ge(s.g_done, i + 1)
                sc.activation(th, ps[:, 2, :], ACT.Tanh, scale=0.5).then_inc(s.tanh_done, 1)

            def act_copy(i):
                sc.wait_ge(s.act_turned, i + 1)
                sc.activation(actT, ps[:, 7, :], ACT.Copy).then_inc(s.actT_ready, 1)

            def expand(i):
                sc.wait_ge(s.diff_read, i + 1)
                sc.activation(diff, diff, ACT.Exp, scale=HD ** -0.5).then_inc(s.exp_done, 1)
                sc.wait_ge(s.prob_ready, i + 1)
                pw = diff.rearrange("p (j w g) -> p j w g", j=TC, w=WINDOW)
                for w in range(WINDOW):
                    if w >= 2:
                        sc.wait_ge(s.expanded, WINDOW * i + w - 1)
                    sc.activation(pexp[w % 2].rearrange("p (j g d) -> p j g d", j=TC, g=GROUPS),
                                  pw[:, :, w, :].unsqueeze(3).broadcast_to([P, TC, GROUPS, HD]),
                                  ACT.Copy).then_inc(s.pexp_ready, 1)
                sc.wait_ge(s.wo_done, PAIRS * (i + 1))
                sc.activation(xo[:, :], ps[:, 6, :], ACT.Identity, bias=gbias[:, 0:1],
                              scale=gates[:, 0:1]).then_inc(s.xo_ready, 1)

            sc.wait_ge(s.iota_done, 5)
            sc.wait_ge(s.gbias_done, 1)
            attention(0)
            expand(0)
            with sc.Fori(1, TILES) as i:
                turned(i - 1)
                attention(i)
                gate(i - 1)
                act_copy(i - 1)
                expand(i)
            turned(TILES - 1)
            gate(TILES - 1)
            act_copy(TILES - 1)
            sc.wait_ge(s.slots_ready, 1)
            sc.activation(e1, margin[:, :], ACT.Exp).then_inc(s.e1_done, 1)
            def expert_turn(it):
                for u in range(UNROLL):
                    sc.wait_ge(S_(f"turned{u}"), it + 1)
                    sc.activation(xT[u], ps[:, u, :], ACT.Copy).then_inc(S_(f"xT_ready{u}"), 1)
                for u in range(UNROLL):
                    sc.wait_ge(S_(f"gu_done{u}"), it + 1)
                    sc.activation(th2[u], ps[:, u, 0:EI], ACT.Tanh, scale=0.5).then_inc(S_(f"th2_done{u}"), 1)
                for u in range(UNROLL):
                    sc.wait_ge(S_(f"act2_turned{u}"), it + 1)
                    sc.activation(act2T[u], ps[:, u, 0:EI], ACT.Copy).then_inc(S_(f"act2T_ready{u}"), 1)
                for u in range(UNROLL):
                    sc.wait_ge(S_(f"dn_done{u}"), it + 1)
                    if later(it):
                        sc.wait_ge(S_(f"y_stored{u}"), 16 * it)
                    sc.activation(ysb[u], ps[:, 3 + u, :], ACT.Copy).then_inc(S_(f"ysb_ready{u}"), 1)

            expert_turn(0)
            with sc.Fori(1, SLOT_TILES // UNROLL) as it:
                expert_turn(it)
            for k in range(4):
                sc.wait_ge(s.wl_turned, k + 1)
                sc.activation(wlT[:, k, :], ps[:, k, :], ACT.Copy).then_inc(s.wlT_ready, 1)

            def attend(i):
                for n in range(2):
                    sc.wait_ge(s.v_done, 2 * i + n + 1)
                    sc.activation(vv[n], ps[:, 2 + n, :], ACT.Identity, bias=bias_att[:, 6:7]).then_inc(s.pv_ready, 1)
                sc.wait_ge(s.d3_ready, i + 1)
                sc.activation(pr, pr, ACT.Exp, scale=LH ** -0.5).then_inc(s.e3_done, 1)
                sc.wait_ge(s.pT_done, i + 1)
                sc.activation(prT, ps[:, 4, :], ACT.Copy).then_inc(s.pv_ready, 1)
                sc.wait_ge(s.av_done, i + 1)
                sc.activation(xh.rearrange("p (j f t) -> p f j t", f=2, t=LH),
                              ps[:, 2:4, 0:4 * LH].rearrange("p f (j t) -> p f j t", t=LH), ACT.Copy).then_inc(s.xh_ready, 1)
                sc.wait_ge(s.wo3_done, i + 1)
                sc.activation(xo[:, :], ps[:, 5, :], ACT.Identity, bias=gbias[:, 1:2],
                              scale=gates[:, 1:2]).then_inc(s.xo3_ready, 1)

            def ffn_turn(i):
                sc.wait_ge(s.xf_turned, i + 1)
                sc.activation(xfT, ps[:, 6, :], ACT.Copy).then_inc(s.xfT_ready, 1)

            attend(0)
            with sc.Fori(1, TILES) as i:
                ffn_turn(i - 1)
                attend(i)
            ffn_turn(TILES - 1)

        @block.vector
        def _(dve):
            dve.wait_ge(s.gates_done, 1)
            for n in range(2):
                dve.tensor_tensor(gbias[:, n:n + 1], bias_att[:, 4 * n + 3:4 * n + 4], gates[:, n:n + 1],
                                  ALU.mult).then_inc(s.gbias_done, 1) if n else \
                    dve.tensor_tensor(gbias[:, 0:1], bias_att[:, 3:4], gates[:, 0:1], ALU.mult)

            def statistics(src):
                dve.bn_stats(stats[:, :], src).then_inc(s.halves_ready, 1)
                dve.wait_ge(s.halves_ready, 1)
                dve.sem_clear(s.halves_ready)
                dve.bn_aggr(mv[:, :], stats[:, :]).then_inc(s.stats_ready, 1)

            def normalise(n, src, out):
                dve.wait_ge(s.rstd_ready, n + 1)
                dve.tensor_scalar(out, src, mv[:, 0:1], rstd[:, :], ALU.subtract, ALU.mult).then_inc(s.normed, 1)

            def row_tile(i):
                return X[:, bass.ds(i, 1), :].squeeze(1)

            sc4 = ps[:, 0:2, :].rearrange("p b (j w g) -> p (b j) w g", j=2, w=WINDOW)
            d4 = diff.rearrange("p (j w g) -> p j w g", j=TC, w=WINDOW)

            def per_group(t):
                return t.rearrange("p (j g) -> p j g", j=TC).unsqueeze(2).broadcast_to([P, TC, WINDOW, GROUPS])

            def products(i):
                dve.wait_ge(s.copied, 3 * i + 2)
                for n, w in enumerate(DVE_W):
                    if n >= ZD:
                        dve.wait_ge(s.qk_done, WINDOW * i + DVE_W[n - ZD] + 1)
                    else:
                        if later(i):
                            dve.wait_ge(s.pair_summed, PAIRS * i)
                    dve.tensor_tensor(z[n % ZD], q, k_pad[:, w:w + T], ALU.mult).then_inc(s.zd_ready, 1)

            def softmax(i):
                n = A_LINKS * i
                dve.wait_ge(s.qk_done, WINDOW * (i + 1))
                dve.tensor_reduce(smax, sc4.rearrange("p j w g -> p j g w"), AX.X, ALU.max).then_inc(s.a_link, 1)
                dve.wait_ge(s.a_link, n + 1)
                dve.tensor_tensor(d4, sc4, per_group(smax), ALU.subtract).then_inc(s.diff_read, 1)
                dve.wait_ge(s.exp_done, i + 1)
                dve.tensor_reduce(ssum, d4.rearrange("p j w g -> p j g w"), AX.X, ALU.add).then_inc(s.a_link, 1)
                dve.wait_ge(s.a_link, n + 2)
                dve.reciprocal(srec, ssum).then_inc(s.a_link, 1)
                dve.wait_ge(s.a_link, n + 3)
                dve.tensor_tensor(d4, d4, per_group(srec), ALU.mult).then_inc(s.prob_ready, 1)

            def values(i):
                dve.wait_ge(s.copied, 3 * (i + 1))
                for w in range(WINDOW):
                    dve.wait_ge(s.expanded, WINDOW * i + w + 1)
                    if w >= ZD:
                        dve.wait_ge(s.pair_summed, PAIRS * i + (w - ZD) // 2 + 1)
                    dve.tensor_tensor(z[w % ZD], ps[:, 4 + w % 2, :], v_pad[:, w:w + T],
                                      ALU.mult).then_inc(s.z2_ready, 1)

            def residual(i):
                dve.wait_ge(s.xo_ready, i + 1)
                dve.tensor_tensor(X[:, bass.ds(i, 1), :], X[:, bass.ds(i, 1), :], xo[:, :].unsqueeze(1),
                                  ALU.add).then_inc(s.x1_ready, 1)
                dve.wait_ge(s.x1_ready, 1)
                dve.sem_clear(s.x1_ready)
                statistics(row_tile(i))
                if later(i):
                    dve.wait_ge(s.x2_stored, 16 * i)
                    dve.wait_ge(s.x2_turned, i)
                normalise(2 * i + 1, row_tile(i), x2)

            def start(i):
                dve.wait_ge(s.x_loaded, 16 * (i + 1))
                dve.tensor_copy(held[:, :], consts[:, 0:1])
                statistics(row_tile(i))
                normalise(2 * i, row_tile(i), xn[:, :])

            def router(i):
                n = R_LINKS * i
                dve.wait_ge(s.logits_done, i + 1)
                dve.tensor_copy(lg, ps[:, 7, 0:EXPERTS]).then_inc(s.logits_read, 1)
                dve.wait_ge(s.logits_read, i + 1)
                dve.tensor_copy(held[:, :], lg[:, 0:1])
                dve.max(top, lg).then_inc(s.top_ready, 1)
                dve.wait_ge(s.top_ready, 1)
                dve.sem_clear(s.top_ready)
                dve.max_index(topi, top, lg).then_inc(s.r_link, 1)
                dve.wait_ge(s.r_link, n + 1)
                dve.tensor_copy(topf, topi[:, 0:2]).then_inc(s.r_link, 1)
                dve.tensor_tensor(margin[:, bass.ds(i, 1)], top[:, 1:2], top[:, 0:1], ALU.subtract).then_inc(s.r_link, 1)
                dve.wait_ge(s.r_link, n + 3)
                for k in range(2):
                    dve.tensor_scalar(onehot[:, bass.ds(i, 1), k, :].squeeze(1), iota16, topf[:, k:k + 1], None,
                                      ALU.is_equal).then_inc(s.r_link if k else s.routed, 1)

            def gating(i):
                dve.wait_ge(s.tanh_done, i + 1)
                dve.scalar_tensor_tensor(th, th, 1.0, ps[:, 2, :], ALU.add, ALU.mult).then_inc(s.u_done, 1)
                dve.wait_ge(s.u_done, 2 * (i + 1))
                dve.scalar_tensor_tensor(act, th, 0.5, ps[:, 3, :], ALU.mult, ALU.mult).then_inc(s.act_ready, 1)

            def add_ffn(i):
                dve.wait_ge(s.down_done, i + 1)
                dve.scalar_tensor_tensor(X[:, bass.ds(i, 1), :], ps[:, 7:8, :], gates[:, 2:3], X[:, bass.ds(i, 1), :],
                                         ALU.mult, ALU.add).then_inc(s.ffn_added, 1)

            dve.wait_ge(s.iota_done, 5)
            start(0)
            products(0)
            softmax(0)
            values(0)
            residual(0)
            with dve.Fori(1, TILES) as i:
                start(i)
                router(i - 1)
                products(i)
                gating(i - 1)
                softmax(i)
                add_ffn(i - 1)
                values(i)
                residual(i)
            router(TILES - 1)
            gating(TILES - 1)
            add_ffn(TILES - 1)

            links = [0]

            def link(ins):
                links[0] += 1
                ins.then_inc(s.c_link, 1)
                dve.wait_ge(s.c_link, links[0])

            dve.wait_ge(s.r_link, R_LINKS * TILES)
            dve.wait_ge(s.routed, TILES)
            dve.wait_ge(s.tri_ready, 7)
            link(dve.tensor_tensor(chosen, onehot[:, :, 0, :], onehot[:, :, 1, :], ALU.add))
            dve.wait_ge(s.ranked, 1)
            rank = ps[:, 0, 0:(TILES + 1) * EXPERTS].rearrange("p (i e) -> p i e", e=EXPERTS)
            link(dve.tensor_scalar(cnt, rank[:, TILES, :], float(P - 1), None, ALU.add))
            link(dve.tensor_copy(cnti, cnt))
            link(dve.tensor_scalar(cnti, cnti, 7, None, ALU.logical_shift_right))
            link(dve.tensor_copy(ntile, cnti))
            src = ntile
            for n, d in enumerate((1, 2, 4, 8)):
                dst = cum[n % 2]
                dve.tensor_copy(dst[:, 0:d], src[:, 0:d])
                link(dve.tensor_tensor(dst[:, d:], src[:, d:], src[:, 0:EXPERTS - d], ALU.add))
                src = dst
            link(dve.tensor_tensor(first, src, ntile, ALU.subtract))
            link(dve.tensor_tensor(prod, onehot[:, 0:TILES, :, :],
                                   rank[:, 0:TILES, :].unsqueeze(2).broadcast_to([P, TILES, 2, EXPERTS]), ALU.mult))
            link(dve.tensor_reduce(pos, prod, AX.X, ALU.add))
            link(dve.tensor_tensor(prod, onehot[:, 0:TILES, :, :].rearrange("p i k e -> p (i k) e"),
                                   first.unsqueeze(1).broadcast_to([P, 2 * TILES, EXPERTS]), ALU.mult))
            link(dve.tensor_reduce(base, prod, AX.X, ALU.add))
            link(dve.tensor_copy(posi, pos))
            dve.tensor_scalar(rowi, posi, P - 1, None, ALU.bitwise_and)
            link(dve.tensor_scalar(tili, posi, 7, None, ALU.logical_shift_right))
            dve.tensor_copy(rowf, rowi)
            link(dve.tensor_copy(tilf, tili))
            link(dve.tensor_tensor(base, base, tilf, ALU.add))
            dve.scalar_tensor_tensor(slot_of[:, :, :].rearrange("p i k -> p (i k)"), rowf, float(SLOT_TILES), base,
                                     ALU.mult, ALU.add).then_inc(s.slots_ready, 1)
            am = at_most[:, 0:SLOT_TILES // 2 * EXPERTS].rearrange("p (s e) -> p s e", e=EXPERTS)
            half = 24
            for n in range(2):
                hs = slice(n * half, (n + 1) * half)
                am = at_most[:, 0:half * EXPERTS].rearrange("p (s e) -> p s e", e=EXPERTS)
                link(dve.tensor_tensor(am, first[0:1, :].unsqueeze(1).broadcast_to([1, half, EXPERTS]),
                                       slot_no[0:1, hs].unsqueeze(2).broadcast_to([1, half, EXPERTS]), ALU.is_le))
                link(dve.tensor_reduce(exp_of[0:1, hs], am, AX.X, ALU.add))
            dve.tensor_scalar(exp_id[0:1, :], exp_of[0:1, :], -1.0, None, ALU.add).then_inc(s.experts_known, 1)
            dve.wait_ge(s.e1_done, 1)
            link(dve.tensor_scalar(den, e1, 1.0, None, ALU.add))
            link(dve.reciprocal(den, den))
            dve.tensor_scalar(comb[:, 0, :], den, gates[:, 2:3], None, ALU.mult)
            link(dve.scalar_tensor_tensor(comb[:, 1, :], e1, gates[:, 2:3], den, ALU.mult, ALU.mult))
            dve.wait_ge(s.tables_loaded, 32)
            for b in range(4):
                for sh in range(32):
                    ins = dve.tensor_scalar(bits[:, :, :, sh], words[:, b, :, :], sh, 1, ALU.logical_shift_right, ALU.bitwise_and)
                link(ins)
                flat = bits.rearrange("p o w s -> p (o w s)")
                cf = code.rearrange("p o i -> p (o i)")
                if b == 0:
                    link(dve.tensor_copy(cf, flat))
                else:
                    link(dve.scalar_tensor_tensor(cf, flat, float(1 << b), cf, ALU.mult, ALU.add))

            def expert_turn(it):
                for u in range(UNROLL):
                    dve.wait_ge(S_(f"th2_done{u}"), it + 1)
                    dve.scalar_tensor_tensor(th2[u], th2[u], 1.0, ps[:, u, 0:EI], ALU.add, ALU.mult).then_inc(S_(f"act2_ready{u}"), 1)
                    dve.wait_ge(S_(f"act2_ready{u}"), 2 * it + 1)
                    dve.scalar_tensor_tensor(act2[u], th2[u], 0.5, ps[:, u, EI:2 * EI], ALU.mult, ALU.mult).then_inc(S_(f"act2_ready{u}"), 1)
                dve.wait_ge(s.added, it + 1)
                dve.scalar_tensor_tensor(picked, code, codes[:, bass.ds(it, 1)],
                                         lut[:, :, bass.ds(it, 1)].broadcast_to([P, 4, T]),
                                         ALU.is_equal, ALU.mult).then_inc(s.picked_ready, 1)

            expert_turn(0)
            with dve.Fori(1, SLOT_TILES // UNROLL) as it:
                expert_turn(it)
            dve.wait_ge(s.const3_loaded, 16 * 5)

            def mix(i):
                for k in range(2):
                    if k:
                        dve.wait_ge(s.half_mixed, 1)
                        dve.sem_clear(s.half_mixed)
                    dve.wait_ge((s.y1_gathered, s.y2_gathered)[k], 16 * (i + 1))
                    dve.scalar_tensor_tensor(X[:, bass.ds(i, 1), :], yg[k].unsqueeze(1), comb[:, k, bass.ds(i, 1)],
                                             X[:, bass.ds(i, 1), :], ALU.mult, ALU.add).then_inc(s.half_mixed, 1)
                dve.wait_ge(s.half_mixed, 1)
                dve.sem_clear(s.half_mixed)
                statistics(row_tile(i))
                normalise(2 * TILES + 2 * i, row_tile(i), xn[:, :])

            def attend(i):
                n = 3 * i
                for m, dst in enumerate((qT, kT)):
                    dve.wait_ge(s.qkT_done, 2 * i + m + 1)
                    dve.tensor_tensor(dst.rearrange("p (j o) -> p j o", j=TC), ps[:, m, :].rearrange("p (j o) -> p j o", j=TC),
                                      bqk[:, m, :].unsqueeze(1).broadcast_to([P, TC, P]), ALU.add).then_inc(s.qk3_ready, 1)
                s3v = ps[:, 0:2, 0:4 * C].rearrange("p f (j e) -> p f j e", e=C)
                d3v = pr.rearrange("p (j f e) -> p f j e", f=2, e=C)
                bc = lambda t: t.rearrange("p (f j) -> p f j", f=2).unsqueeze(3).broadcast_to([P, 2, 4, C])
                dve.wait_ge(s.s3_done, i + 1)
                dve.tensor_reduce(m3, s3v, AX.X, ALU.max).then_inc(s.d_link, 1)
                dve.wait_ge(s.d_link, n + 1)
                dve.tensor_tensor(d3v, s3v, bc(m3), ALU.subtract).then_inc(s.d3_ready, 1)
                dve.wait_ge(s.e3_done, i + 1)
                dve.tensor_reduce(s3, d3v, AX.X, ALU.add).then_inc(s.d_link, 1)
                dve.wait_ge(s.d_link, n + 2)
                dve.reciprocal(r3, s3).then_inc(s.d_link, 1)
                dve.wait_ge(s.d_link, n + 3)
                dve.tensor_tensor(d3v, d3v, bc(r3), ALU.mult).then_inc(s.p3_ready, 1)

            def residual3(i):
                dve.wait_ge(s.xo3_ready, i + 1)
                dve.tensor_tensor(X[:, bass.ds(i, 1), :], X[:, bass.ds(i, 1), :], xo[:, :].unsqueeze(1),
                                  ALU.add).then_inc(s.x1_ready, 1)
                dve.wait_ge(s.x1_ready, 1)
                dve.sem_clear(s.x1_ready)
                statistics(row_tile(i))
                if later(i):
                    dve.wait_ge(s.xf_turned, i)
                normalise(2 * TILES + 2 * i + 1, row_tile(i), xf)

            def finish(i):
                dve.wait_ge(s.y3_done, i + 1)
                if later(i):
                    dve.wait_ge(s.out_stored, 16 * i)
                dve.scalar_tensor_tensor(obuf.unsqueeze(1), ps[:, 7:8, :], gates[:, 3:4], X[:, bass.ds(i, 1), :],
                                         ALU.mult, ALU.add).then_inc(s.out_ready, 1)

            mix(0)
            attend(0)
            residual3(0)
            mix(1)
            attend(1)
            finish(0)
            residual3(1)
            with dve.Fori(2, TILES) as i:
                mix(i)
                attend(i)
                finish(i - 1)
                residual3(i)
            finish(TILES - 1)

        @block.tensor
        def _(pe):
            def mm(out, lhsT, rhs, start=True, stop=True, **kw):
                return pe.matmul(out, lhsT, rhs, start=start, stop=stop, **kw)

            def turn4(out, src, done):
                for j in range(4):
                    ins = pe.transpose(out[:, j * P:(j + 1) * P], src[:, j * P:(j + 1) * P], ident[:, :])
                ins.then_inc(done, 1)

            def project(i):
                pe.wait_ge(s.normed, 2 * i + 1)
                if later(i):
                    pe.wait_ge(s.diff_read, i)
                mm(ps[:, 0, :], w_att[:, 0, :], xn[:, :]).then_inc(s.projected, 1)
                pe.wait_ge(s.ctx_loaded, 16 * (i + 1))
                mm(ps[:, 1, :], w_att[:, 1, :], ctx_t[:, :]).then_inc(s.projected, 1)
                if later(i):
                    pe.wait_ge(s.z2_ready, WINDOW * i)
                mm(ps[:, 4, :], w_att[:, 2, :], ctx_t[:, :]).then_inc(s.projected, 1)

            def qk(i, w):
                if w in POOL_W:
                    pe.wait_ge(s.zp_ready, len(POOL_W) * i + POOL_W.index(w) + 1)
                    zz = z[ZD + POOL_W.index(w) % ZP]
                else:
                    pe.wait_ge(s.zd_ready, len(DVE_W) * i + DVE_W.index(w) + 1)
                    zz = z[DVE_W.index(w) % ZD]
                if w == 0:
                    pe.wait_ge(s.copied, 3 * i + 2)
                for j in range(TC):
                    at = ((j % 2) * WINDOW + w) * GROUPS
                    ins = mm(ps[:, j // 2, at:at + GROUPS], zz[:, j * P:(j + 1) * P], head_sum)
                ins.then_inc(s.qk_done, 1)

            def turn_x2(i):
                pe.wait_ge(s.normed, 2 * i + 2)
                turn4(ps[:, 7, :], x2, s.x2_turned)

            def route(i):
                pe.wait_ge(s.x2T_ready, i + 1)
                for k in range(TC):
                    ins = mm(ps[:, 7, 0:EXPERTS], x2T[:, k * P:(k + 1) * P], w_router[:, k, :], k == 0, k == TC - 1)
                ins.then_inc(s.logits_done, 1)

            def gate_up(i, n):
                half, k = divmod(n, TC)
                ins = mm(ps[:, 2 + half, :], x2T[:, k * P:(k + 1) * P], w_sgu[:, k, half * SI:(half + 1) * SI], k == 0, k == TC - 1)
                if k == TC - 1:
                    ins.then_inc(s.u_done if half else s.g_done, 1)

            def turn_act(i):
                pe.wait_ge(s.act_ready, i + 1)
                pe.wait_ge(s.logits_read, i + 1)
                turn4(ps[:, 7, :], act, s.act_turned)

            def down(i):
                pe.wait_ge(s.actT_ready, i + 1)
                for k in range(4):
                    ins = mm(ps[:, 7, :], actT[:, k * P:(k + 1) * P], w_sdn[:, k, :], k == 0, k == 3)
                ins.then_inc(s.down_done, 1)

            def attention(i):
                def wo(k):
                    pe.wait_ge(s.pair_summed, PAIRS * i + k + 1)
                    if k == 0:
                        if later(i):
                            pe.wait_ge(s.xo_ready, i)
                    mm(ps[:, 6, :], w_att[:, 3, :], z[ZD + k % ZP], k == 0, k == PAIRS - 1).then_inc(s.wo_done, 1)

                for w in range(WINDOW):
                    pe.wait_ge(s.pexp_ready, WINDOW * i + w + 1)
                    if w >= 2:
                        pe.wait_ge(s.z2_ready, WINDOW * i + w - 1)
                    else:
                        pe.wait_ge(s.copied, 3 * (i + 1))
                    turn4(ps[:, 4 + w % 2, :], pexp[w % 2], s.expanded)
                    if w % 2 and w >= 3:
                        wo(w // 2 - 1)
                wo(PAIRS - 1)

            pe.wait_ge(s.small_loaded, 16 * N_SM)
            pe.wait_ge(s.ident_done, 5)
            project(0)
            for w in range(WINDOW):
                qk(0, w)
            attention(0)
            pe.wait_ge(s.shared_loaded, 32)
            with pe.Fori(1, TILES) as i:
                turn_x2(i - 1)
                project(i)
                route(i - 1)
                for w in range(WINDOW):
                    qk(i, w)
                    if w % 2:
                        gate_up(i - 1, w // 2)
                turn_act(i - 1)
                down(i - 1)
                attention(i)
            turn_x2(TILES - 1)
            route(TILES - 1)
            for n in range(2 * TC):
                gate_up(TILES - 1, n)
            turn_act(TILES - 1)
            down(TILES - 1)

            pe.wait_ge(s.tri_ready, 7)
            pe.wait_ge(s.c_link, 1)
            flat = chosen.rearrange("p i e -> p (i e)")
            mm(ps[:, 0, 0:(TILES + 1) * EXPERTS], tri, flat, True, False)
            for i in range(TILES):
                ins = mm(ps[:, 0, (i + 1) * EXPERTS:(TILES + 1) * EXPERTS], ones,
                         chosen[:, i:i + 1, :].broadcast_to([P, TILES - i, EXPERTS]), False, i == TILES - 1)
            ins.then_inc(s.ranked, 1)
            pe.wait_ge(s.experts_known, 1)
            pe.wait_ge(s.experts_loaded, 16 * 2 * EXPERTS)
            def expert_turn(it):
                for u in range(UNROLL):
                    pe.wait_ge(S_(f"gathered{u}"), 16 * (it + 1))
                    if later(it):
                        pe.wait_ge(S_(f"act2T_ready{u}"), it)
                    turn4(ps[:, u, :], xg[u], S_(f"turned{u}"))
                e = []
                for u in range(UNROLL):
                    e.append(pe.value_load(exp_id[0:1, bass.ds(UNROLL * it + u, 1)], min_val=0, max_val=EXPERTS - 1))
                    pe.wait_ge(S_(f"xT_ready{u}"), it + 1)
                    for k in range(TC):
                        ins = mm(ps[:, u, 0:2 * EI], xT[u][:, k * P:(k + 1) * P],
                                 w_gu[:, bass.ds(e[u], 1), k, :], k == 0, k == TC - 1)
                    ins.then_inc(S_(f"gu_done{u}"), 1)
                for u in range(UNROLL):
                    pe.wait_ge(S_(f"act2_ready{u}"), 2 * it + 2)
                    pe.transpose(ps[:, u, 0:EI], act2[u], ident[:, :]).then_inc(S_(f"act2_turned{u}"), 1)
                for u in range(UNROLL):
                    pe.wait_ge(S_(f"act2T_ready{u}"), it + 1)
                    if later(it):
                        pe.wait_ge(S_(f"ysb_ready{u}"), it)
                    mm(ps[:, 3 + u, :], act2T[u], w_dn[:, bass.ds(e[u], 1), :]).then_inc(S_(f"dn_done{u}"), 1)

            expert_turn(0)
            with pe.Fori(1, SLOT_TILES // UNROLL) as it:
                expert_turn(it)
            pe.wait_ge(s.added, 1 + CODES)
            pe.wait_ge(S_("ysb_ready0"), SLOT_TILES // UNROLL)
            for k in range(4):
                for o in range(4):
                    ins = pe.transpose(ps[:, k, o * P:(o + 1) * P], wl[:, o, k * P:(k + 1) * P], ident[:, :])
                ins.then_inc(s.wl_turned, 1)
            pe.wait_ge(s.wlT_ready, 4)
            pe.wait_ge(s.const3_loaded, 16 * 5)

            def qkv(i):
                pe.wait_ge(s.normed, 2 * TILES + 2 * i + 1)
                if later(i):
                    pe.wait_ge(s.d3_ready, i)
                for j in range(TC):
                    ins = mm(ps[:, 0, j * P:(j + 1) * P], xn[:, j * P:(j + 1) * P], w_att[:, 4, :])
                ins.then_inc(s.qkT_done, 1)
                pe.wait_ge(s.ctx_loaded, 16 * (TILES + 1 + i))
                for j in range(TC):
                    ins = mm(ps[:, 1, j * P:(j + 1) * P], ctx_t[:, j * P:(j + 1) * P], w_att[:, 5, :])
                ins.then_inc(s.qkT_done, 1)
                if later(i):
                    pe.wait_ge(s.xh_ready, i)
                for n in range(2):
                    mm(ps[:, 2 + n, :], w_att[:, 6 + n, :], ctx_t[:, :]).then_inc(s.v_done, 1)

            def scores(i):
                pe.wait_ge(s.qk3_ready, 2)
                pe.sem_clear(s.qk3_ready)
                for f in range(2):
                    rows = slice(f * LH, (f + 1) * LH)
                    for b in range(2):
                        for j in range(TC):
                            at = slice(j * P + b * C, j * P + (b + 1) * C)
                            ins = mm(ps[b * C:(b + 1) * C, f, j * C:(j + 1) * C], qT[rows, at], kT[rows, at])
                ins.then_inc(s.s3_done, 1)

            def weighted(i):
                pe.wait_ge(s.p3_ready, i + 1)
                turn4(ps[:, 4, :], pr, s.pT_done)
                pe.wait_ge(s.pv_ready, 3)
                pe.sem_clear(s.pv_ready)
                for f in range(2):
                    rows = slice(f * C, (f + 1) * C)
                    for b in range(2):
                        v = vv[0 if b == f else 1]
                        for j in range(TC):
                            ins = mm(ps[b * C:(b + 1) * C, 2 + f, j * LH:(j + 1) * LH],
                                     prT[rows, j * P + b * C:j * P + (b + 1) * C],
                                     v[rows, (2 * j + f) * LH:(2 * j + f + 1) * LH])
                ins.then_inc(s.av_done, 1)
                pe.wait_ge(s.xh_ready, i + 1)
                if later(i):
                    pe.wait_ge(s.xo3_ready, i)
                mm(ps[:, 5, :], w_att[:, 8, :], xh).then_inc(s.wo3_done, 1)

            def turn_xf(i):
                pe.wait_ge(s.normed, 2 * TILES + 2 * i + 2)
                turn4(ps[:, 6, :], xf, s.xf_turned)

            def linear(i):
                pe.wait_ge(s.xfT_ready, i + 1)
                mm(ps[:, 7, :], orow[0:1, :], brow[0:1, :], True, False)
                for k in range(4):
                    ins = mm(ps[:, 7, :], xfT[:, k * P:(k + 1) * P], wlT[:, k, :], False, k == 3)
                ins.then_inc(s.y3_done, 1)

            qkv(0)
            scores(0)
            weighted(0)
            with pe.Fori(1, TILES) as i:
                turn_xf(i - 1)
                qkv(i)
                scores(i)
                linear(i - 1)
                weighted(i)
            turn_xf(TILES - 1)
            linear(TILES - 1)


_NAMES = ["x", "ctx", "gate4", "wq0", "wk0", "wv0", "wo0", "wq1", "wk1", "wv1", "wo1", "bq0", "bk0", "bv0", "bo0",
          "bq1", "bk1", "bv1", "bo1", "w_router", "w_sgu", "w_sdn", "w_gu", "w_dn", "lut4", "words", "bias"]


def kernel(**inputs):
    import numpy as np
    import concourse.bacc as bacc
    from concourse.bass_utils import run_bass_kernel_spmd as run

    v = {k: np.asarray(t) for k, t in inputs.items()}

    def by_rows(w, chunks):
        return w.T.reshape(chunks, P, w.shape[0]).transpose(1, 0, 2)

    laid = {"x": v["x"], "ctx": v["ctx_4096"], "gate4": np.concatenate([v["g_xattn"], v["g_ffn"]])}
    for layer in range(2):
        for m in "qkvo":
            laid[f"w{m}{layer}"] = v[f"L{layer}_xattn_W{m}"].T
            laid[f"b{m}{layer}"] = v[f"L{layer}_xattn_b{m}"]
    laid["w_router"] = by_rows(v["L0_ffn_gate_w"], TC)
    laid["w_sgu"] = by_rows(v["L0_ffn_shared_w_gate_up"], TC)
    laid["w_sdn"] = by_rows(v["L0_ffn_shared_w_down"], 4)
    gu = v["L0_ffn_w_gate_up"].transpose(0, 2, 1).reshape(EXPERTS, TC, P, 2 * EI).transpose(0, 2, 1, 3)
    laid["w_gu"] = gu.reshape(EXPERTS * P, TC * 2 * EI)
    laid["w_dn"] = v["L0_ffn_w_down"].transpose(0, 2, 1).reshape(EXPERTS * P, T)
    laid["lut4"] = v["L1_ffn_lut4"].reshape(4, P, CODES).transpose(1, 0, 2)
    laid["words"] = v["L1_ffn_qweight"][0:4].reshape(4, 4, P, T // 32).transpose(2, 0, 1, 3)
    laid["bias"] = v["L1_ffn_bias"]

    nc = bacc.Bacc("TRN2", target_bir_lowering=False, num_devices=1)
    arrays, aps = {}, {}
    for name in _NAMES:
        t = np.ascontiguousarray(laid[name])
        arrays[f"in_{name}"] = t
        aps[name] = nc.dram_tensor(f"in_{name}", t.shape, mybir.dt.from_np(t.dtype), kind="ExternalInput").ap()
    aps["out"] = nc.dram_tensor("out_0", (B, C, T), F32, kind="ExternalOutput").ap()
    build(nc, aps)
    r = run(nc, [arrays], core_ids=[0])
    return r.results[0]["out_0"]
```

```python
from contextlib import ExitStack

import concourse.bass as bass
from concourse import mybir

P = 128
B, C, T = 32, 64, 512
TILES = B * C // P
TC = T // P
HEADS0, WINDOW = 8, 16
HD = C // HEADS0
GROUPS = 2 * HEADS0
LEFT = WINDOW // 2
PADDED = T + WINDOW - 1
HEADS1 = 8
LH = T // HEADS1
EXPERTS, EI, SI = 16, 128, 512
SLOT_TILES = 48
SLOTS = SLOT_TILES * P
UNROLL = 3
CODES = 16
EPS = 1e-5
WORK = 10750

ALU = mybir.AluOpType
ACT = mybir.ActivationFunctionType
AX = mybir.AxisListType
F32, I32, U32 = mybir.dt.float32, mybir.dt.int32, mybir.dt.uint32

CT = 64
CHUNKS = T // CT
HALO = CT + WINDOW - 1
PAIRS = WINDOW // 2
QK_POOL, AV_POOL = (2, 5), (1, 4, 6)
QK_DVE = tuple(c for c in range(PAIRS) if c not in QK_POOL)
AV_DVE = tuple(c for c in range(PAIRS) if c not in AV_POOL)
N_DVE, N_POOL = len(QK_DVE) + len(AV_DVE), len(QK_POOL) + len(AV_POOL)
SD, SP_ = 3, 2
NZ = 3
A_LINKS = 3
R_LINKS = 4
LATE_EXPERTS = 5


def later(i):
    return not (isinstance(i, int) and i == 0)


def build(nc, a):
    ctx = ExitStack()
    with ctx:
        def sb(name, shape, dt=F32):
            return ctx.enter_context(nc.sbuf_tensor(name, shape, dt))

        def sem(name):
            return ctx.enter_context(nc.semaphore(name))

        X = sb("X", [P, TILES, T])
        w_att = sb("w_att", [P, 9, P])
        bias_att = sb("bias_att", [P, 8])
        ident = sb("ident", [P, P])
        gates = sb("gates", [P, 4])
        gbias = sb("gbias", [P, 2])
        consts = sb("consts", [P, 2])
        stats = sb("stats", [P, 6])
        mv = sb("mv", [P, 2])
        veps = sb("veps", [P, 1])
        held = sb("held", [P, 1])
        rstd = sb("rstd", [P, 1])
        ctx_t = sb("ctx_t", [P, T])
        xn = sb("xn", [P, T])
        xo = sb("xo", [P, T])
        onehot = sb("onehot", [P, TILES + 1, 2, EXPERTS])
        margin = sb("margin", [P, TILES])
        comb = sb("comb", [P, 2, TILES])
        slot_of = sb("slot_of", [P, TILES, 2], U32)
        cols = sb("cols", [P, 4], U32)
        w_exp = sb("w_exp", [P, EXPERTS, TC * 2 * EI + T])
        w_gu = w_exp[:, :, 0:TC * 2 * EI].rearrange("p e (k n) -> p e k n", k=TC)
        w_dn = w_exp[:, :, TC * 2 * EI:]
        work = sb("work", [P, WORK])
        ps = ctx.enter_context(nc.psum_tensor("ps", [P, 8, 512], F32))

        used = {}

        def carve(area, key, n):
            at = used.get(key, 0)
            used[key] = at + n
            assert used[key] <= area.shape[1], (key, used[key])
            return area[:, at:at + n]

        w_shared = sb("w_shared", [P, TC * 2 * SI + 4 * T])
        w_sgu = w_shared[:, 0:TC * 2 * SI].rearrange("p (k n) -> p k n", k=TC)
        w_sdn = w_shared[:, TC * 2 * SI:].rearrange("p (k n) -> p k n", k=4)

        w1 = lambda n: carve(work, 1, n)
        late = w_exp[:, EXPERTS - LATE_EXPERTS:, :].rearrange("p e n -> p (e n)")
        w1l = lambda n: carve(late, "1l", n)
        q = w1(T)
        k_pad = w1(PADDED + 1)
        v_pad = w1(PADDED + 1)
        q2 = w1(HD * CT)
        k2 = w1(HD * HALO)
        v2 = w1(HD * HALO)
        diff = w1(WINDOW * CT)
        x2 = w1(T)
        x2T = w1(T)
        th = w1(T)
        act = th
        w_router = w1(TC * EXPERTS).rearrange("p (k e) -> p k e", k=TC)
        iota16 = w1(EXPERTS)
        smax = w1(CT)
        ssum = w1(CT)
        srec = w1(CT)
        lg = w1(EXPERTS)
        top = w1(8)
        topi = w1(8).bitcast(U32)
        topf = w1(2)
        actT = x2T
        o2 = w1(T)
        oT = w1(T)
        zd = [w1l(2 * HD * CT) for _ in range(NZ)]
        sd = [w1l(HD * CT) for _ in range(SD)]
        zp = [w1l(2 * HD * CT) for _ in range(NZ)]
        sp_ = [w1(HD * CT) for _ in range(SP_)]

        w2 = lambda n: carve(work, 2, n)
        tri = w2(P)
        ones = w2(P)
        chosen = w2((TILES + 1) * EXPERTS).rearrange("p (i e) -> p i e", e=EXPERTS)
        prod = w2(TILES * 2 * EXPERTS).rearrange("p (i k e) -> p i k e", k=2, e=EXPERTS)
        pos = w2(TILES * 2)
        base = w2(TILES * 2)
        posi = w2(TILES * 2).bitcast(I32)
        rowi = w2(TILES * 2).bitcast(I32)
        tili = w2(TILES * 2).bitcast(I32)
        rowf = w2(TILES * 2)
        tilf = w2(TILES * 2)
        cnt = w2(EXPERTS)
        cnti = w2(EXPERTS).bitcast(I32)
        cum = [w2(EXPERTS) for _ in range(2)]
        ntile = w2(EXPERTS)
        first = w2(EXPERTS)
        token = w2(TILES).bitcast(I32)
        ids = w2(SLOT_TILES).bitcast(U32)
        zeros48 = w2(SLOT_TILES).bitcast(U32)
        slot_no = w2(SLOT_TILES)
        exp_of = w2(SLOT_TILES)
        exp_id = w2(SLOT_TILES).bitcast(I32)
        at_most = prod[0:1].rearrange("p i k e -> p (i k e)")
        e1 = w2(TILES)
        den = w2(TILES)
        lut = w2(4 * CODES).rearrange("p (o c) -> p o c", o=4)
        words = w2(4 * 4 * 16).bitcast(I32).rearrange("p (b o w) -> p b o w", b=4, o=4)
        xg = [w2(T) for _ in range(UNROLL)]
        xT = [w2(T) for _ in range(UNROLL)]
        th2 = [w2(EI) for _ in range(UNROLL)]
        act2 = [w2(EI) for _ in range(UNROLL)]
        act2T = [w2(EI) for _ in range(UNROLL)]
        ysb = [w2(T) for _ in range(UNROLL)]
        w2s = lambda n: carve(w_shared, "2s", n)
        code = w2s(4 * T).rearrange("p (o i) -> p o i", o=4)
        picked = w2s(4 * T).rearrange("p (o i) -> p o i", o=4)
        codes = w2s(CODES)
        bits = picked.rearrange("p o i -> p (o i)").bitcast(I32).rearrange("p (o w s) -> p o w s", o=4, w=16)
        w3 = lambda n: carve(w_exp.rearrange("p e n -> p (e n)"), 3, n)
        wl = work[:, WORK - 4 * T:WORK].rearrange("p (o i) -> p o i", o=4)
        assert used[2] <= WORK - 4 * T, used
        wlT = w3(4 * T).rearrange("p (k o) -> p k o", k=4)
        yg = [w3(T) for _ in range(2)]
        qT = w3(T)
        kT = w3(T)
        vv = [w3(T) for _ in range(2)]
        pr = w3(T)
        prT = w3(T)
        xh = w3(T)
        xf = w3(T)
        xfT = w3(T)
        obuf = w3(T)
        m3 = w3(8)
        s3 = w3(8)
        r3 = w3(8)
        bqk = w3(2 * P).rearrange("p (a o) -> p a o", a=2)
        brow = w3(T)
        orow = w3(P)

        x2_rows = nc.dram_tensor("x2_rows", [B * C, T], F32, kind="Internal").ap()
        ids_dram = nc.dram_tensor("ids_dram", [SLOTS, 1], U32, kind="Internal").ap()
        y_slots = nc.dram_tensor("y_slots", [SLOTS, T], F32, kind="Internal").ap()
        ids_rows = ids_dram.rearrange("(r s) o -> r (s o)", s=SLOT_TILES)
        y_rows = y_slots.rearrange("(r s) d -> r s d", s=SLOT_TILES)
        q_dram = nc.dram_tensor("q_dram", [TILES, CHUNKS, P, CT], F32, kind="Internal").ap()
        kv_dram = [nc.dram_tensor(f"{n}_dram", [TILES, CHUNKS, P, HALO], F32, kind="Internal").ap() for n in "kv"]
        o_dram = nc.dram_tensor("o_dram", [TILES, CHUNKS, P, CT], F32, kind="Internal").ap()
        x_rows = a["x"].rearrange("b c t -> (b c) t")
        c_rows = a["ctx"].rearrange("b c t -> (b c) t")
        o_rows = a["out"].rearrange("b c t -> (b c) t")

        S = {}
        for name in """zeroed small_loaded shared_loaded iota_done ident_done gates_done gbias_done x_loaded ctx_loaded
                experts_loaded stats_ready veps_ready rstd_ready a_normed b_normed normed projected copied
                q_stored k_stored v_stored q2_loaded k2_loaded v2_loaded o_stored oT_loaded late_loaded
                d_product d_pair p_product p_pair d_summed p_summed
                diff_read exp_done prob_ready wo_done xo_ready o2_ready
                x1_ready a_link x2_stored x2_turned x2T_ready logits_done logits_read r_link routed g_done u_done
                tanh_done act_ready act_turned actT_ready down_done ffn_added
                c_link tri_ready ranked slots_ready e1_done comb_done ids_zeroed ids_scattered ids_loaded tables_loaded
                experts_known codes_ready picked_ready added
                y_col wl_turned wlT_ready const3_loaded const3_zeroed y1_gathered y2_gathered mixed qkT_done
                qk3_ready v_done pv_ready halves_ready half_mixed top_ready s3_done d_link d3_ready e3_done p3_ready pT_done av_done
                xh_ready wo3_done xo3_ready x3_ready xf_turned xfT_ready y3_done out_ready out_stored""".split():
            S[name] = sem(name)
        for u in range(UNROLL):
            for name in "gathered turned xT_ready gu_done th2_done act2_ready act2_turned act2T_ready dn_done ysb_ready y_stored col_ready".split():
                S[f"{name}{u}"] = sem(f"{name}{u}")
        s = type("Sems", (), S)

        def S_(name):
            return S[name]


        def windows(t, start, n, step, width):
            return bass.AP(t.tensor, t.offset + start, [list(t.ap[0]), [step, n], [1, width]])

        def shifted(t, w):
            return bass.AP(t.tensor, t.offset + w, [list(t.ap[0]), [1, 2], [HALO, HD], [1, CT]])

        def last_use(n, buffers, count):
            return max(m for m in range(count) if m % buffers == n % buffers) + 1 - count

        bcast_q = q2.rearrange("p (d t) -> p d t", d=HD).unsqueeze(1).broadcast_to([P, 2, HD, CT])

        def bcast_p(c):
            return diff.rearrange("p (w t) -> p w t", t=CT)[:, 2 * c:2 * c + 2, :].unsqueeze(2).broadcast_to([P, 2, HD, CT])

        def halves(z, qk):
            if qk:
                v = z.rearrange("p (w h n) -> p w h n", w=2, h=2)
                return v[:, :, 0, :], v[:, :, 1, :]
            return z[:, 0:HD * CT], z[:, HD * CT:]

        def lo_out(t, qk):
            return t.rearrange("p (w n) -> p w n", w=2) if qk else t

        def by_rows(dram, i, width):
            return dram[bass.ds(i, 1)].squeeze(0).rearrange("c (g d) t -> (c g) d t", d=HD)

        N_SM = 2 * 9 + 2 * 8 + 2
        block = ctx.enter_context(nc.Block())

        @block.sync
        def _(sp):
            small = 0

            def load(dst, src, sm=s.small_loaded):
                sp.dma_start(dst, src).then_inc(sm, 16)

            load(X[:, 0, :], x_rows[0:P, :], s.x_loaded)
            load(ctx_t[:, :], c_rows[0:P, :], s.ctx_loaded)
            sp.wait_ge(s.zeroed, 1)
            mats = ["wq0", "wk0", "wv0", "wo0", "wq1", "wk1", "wv1", "wv1", "wo1"]
            for n, name in enumerate(mats):
                for h in range(2):
                    c = (1 - h) if n == 7 else h
                    load(w_att[h * C:(h + 1) * C, n, c * C:(c + 1) * C], a[name])
                    small += 1
            for n, name in enumerate(["bq0", "bk0", "bv0", "bo0", "bq1", "bk1", "bv1", "bo1"]):
                for h in range(2):
                    load(bias_att[h * C:(h + 1) * C, n:n + 1], a[name].rearrange("(c o) -> c o", o=1))
                    small += 1
            load(gates[:, 0:4], a["gate4"].partition_broadcast(P))
            load(w_router, a["w_router"])
            small += 2
            assert small == N_SM
            load(w_sgu, a["w_sgu"], s.shared_loaded)
            load(w_sdn, a["w_sdn"], s.shared_loaded)

            def store_qkv(i):
                sp.wait_ge(s.copied, 3 * i + 3)
                sp.dma_start(q_dram[bass.ds(i, 1)].squeeze(0).rearrange("c r t -> r c t"),
                             q.rearrange("p (c t) -> p c t", t=CT)).then_inc(s.q_stored, 16)
                for n, (pad, done) in enumerate(((k_pad, s.k_stored), (v_pad, s.v_stored))):
                    sp.dma_start(kv_dram[n][bass.ds(i, 1)].squeeze(0).rearrange("c r t -> r c t"),
                                 windows(pad, 0, CHUNKS, CT, HALO)).then_inc(done, 16)

            def load_qk(i):
                if later(i):
                    sp.wait_ge(s.p_product, N_POOL * (i - 1) + len(QK_POOL))
                sp.wait_ge(s.q_stored, 16 * (i + 1))
                if later(i):
                    sp.wait_ge(s.d_product, N_DVE * (i - 1) + len(QK_DVE))
                sp.dma_start(q2.rearrange("p (d t) -> p d t", d=HD), by_rows(q_dram, i, CT)).then_inc(s.q2_loaded, 16)
                sp.wait_ge(s.k_stored, 16 * (i + 1))
                sp.dma_start(k2.rearrange("p (d t) -> p d t", d=HD), by_rows(kv_dram[0], i, HALO)).then_inc(s.k2_loaded, 16)

            def load_v(i):
                sp.wait_ge(s.v_stored, 16 * (i + 1))
                sp.dma_start(v2.rearrange("p (d t) -> p d t", d=HD), by_rows(kv_dram[1], i, HALO)).then_inc(s.v2_loaded, 16)

            def load_x(i):
                sp.wait_ge(s.x_loaded, 16 * i)
                sp.dma_start(X[:, bass.ds(i, 1), :], x_rows[bass.ds(i * P, P), :]).then_inc(s.x_loaded, 16)

            def load_ctx(i):
                sp.wait_ge(s.projected, 3 * i)
                sp.dma_start(ctx_t[:, :], c_rows[bass.ds(i * P, P), :]).then_inc(s.ctx_loaded, 16)

            def load_expert(e, done=s.experts_loaded):
                sp.dma_start(w_exp[:, bass.ds(e, 1), 0:TC * 2 * EI], a["w_gu"][bass.ds(e * P, P), :]).then_inc(done, 16)
                sp.dma_start(w_exp[:, bass.ds(e, 1), TC * 2 * EI:], a["w_dn"][bass.ds(e * P, P), :]).then_inc(done, 16)

            def store_x2(i):
                sp.wait_ge(s.b_normed, i + 1)
                sp.dma_start(x2_rows[bass.ds(i * P, P), :], x2).then_inc(s.x2_stored, 16)

            def turn_o(i):
                sp.wait_ge(s.o2_ready, i + 1)
                sp.dma_start(o_dram[bass.ds(i, 1)].squeeze(0).rearrange("c r t -> (c r t)").rearrange("(p n) -> p n", p=P),
                             o2).then_inc(s.o_stored, 16)
                sp.wait_ge(s.o_stored, 16 * (i + 1))
                sp.dma_start(oT.rearrange("p (c t) -> p c t", t=CT),
                             o_dram[bass.ds(i, 1)].squeeze(0).rearrange("c r t -> r c t")).then_inc(s.oT_loaded, 16)

            def turn(i, before=True, after=True, expert=True):
                load_v(i)
                if expert:
                    load_expert(i)
                if after:
                    store_qkv(i + 1)
                    load_qk(i + 1)
                if before:
                    store_x2(i - 1)
                if after and not (isinstance(i, int) and i == TILES - 2):
                    load_ctx(i + 2)
                    load_x(i + 2)
                turn_o(i)

            load_x(1)
            store_qkv(0)
            load_qk(0)
            load_ctx(1)
            turn(0, before=False)
            with sp.Fori(1, EXPERTS - LATE_EXPERTS) as i:
                turn(i)
            with sp.Fori(EXPERTS - LATE_EXPERTS, TILES - 2) as i:
                turn(i, expert=False)
            last = TILES - 1
            turn(TILES - 2, expert=False)
            turn(last, after=False, expert=False)
            store_x2(last)
            sp.wait_ge(s.projected, 3 * TILES)
            sp.dma_start(ctx_t[:, :], c_rows[0:P, :]).then_inc(s.ctx_loaded, 16)
            sp.wait_ge(s.d_summed, N_DVE * TILES)
            sp.wait_ge(s.p_summed, N_POOL * TILES)
            for e in range(EXPERTS - LATE_EXPERTS, EXPERTS):
                load_expert(e, s.late_loaded)
            sp.wait_ge(s.ffn_added, TILES)
            load(lut, a["lut4"], s.tables_loaded)
            load(words, a["words"], s.tables_loaded)
            sp.wait_ge(s.tri_ready, 5)
            load(ids_rows, zeros48, s.ids_zeroed)
            sp.wait_ge(s.ids_scattered, 16 * 2 * TILES)
            load(ids, ids_rows, s.ids_loaded)
            with sp.Fori(0, SLOT_TILES // UNROLL) as it:
                for u in range(UNROLL):
                    sp.wait_ge(S_(f"ysb_ready{u}"), it + 1)
                    sp.dma_start(y_rows[:, bass.ds(UNROLL * it + u, 1), :], ysb[u]).then_inc(S_(f"y_stored{u}"), 16)
            sp.wait_ge(s.const3_zeroed, 1)
            for h in range(2):
                for n, name in enumerate(["bq1", "bk1"]):
                    load(bqk[:, n, h * C:(h + 1) * C], a[name].partition_broadcast(P), s.const3_loaded)
            load(brow[0:1, :], a["bias"].rearrange("(r o) -> r o", r=1), s.const3_loaded)

            def out_tile(i):
                sp.wait_ge(s.out_ready, i + 1)
                sp.dma_start(o_rows[bass.ds(i * P, P), :], obuf).then_inc(s.out_stored, 16)

            with sp.Fori(0, TILES - 1) as i:
                sp.wait_ge(s.qkT_done, 2 * (i + 1))
                sp.wait_ge(s.v_done, 2 * (i + 1))
                sp.dma_start(ctx_t[:, :], c_rows[bass.ds((i + 1) * P, P), :]).then_inc(s.ctx_loaded, 16)
                out_tile(i)
            out_tile(last)
            sp.wait_ge(s.out_stored, 16 * TILES)
            sp.wait_ge(s.x2_stored, 16 * TILES)

        @block.gpsimd
        def _(pool):
            pool.memset(w_att[:, :, :], 0.0).then_inc(s.zeroed, 1)
            pool.memset(consts[:, 0:1], -0.5).then_inc(s.iota_done, 1)
            pool.memset(k_pad, 0.0).then_inc(s.iota_done, 1)
            pool.memset(v_pad, 0.0).then_inc(s.iota_done, 1)
            pool.memset(onehot[:, TILES, :, :], 0.0).then_inc(s.iota_done, 1)
            pool.iota(iota16, pattern=[[1, EXPERTS]], base=0, channel_multiplier=0,
                      allow_small_or_imprecise_dtypes=True).then_inc(s.iota_done, 1)
            pool.memset(ident[:, :], 0.0).then_inc(s.ident_done, 1)
            pool.wait_ge(s.ident_done, 1)
            pool.affine_select(out=ident[:, :], in_=ident[:, :], compare_op=ALU.not_equal, fill=1.0, base=0,
                               pattern=[[-1, P]], channel_multiplier=1).then_inc(s.ident_done, 1)

            def root():
                pool.wait_ge(s.stats_ready, 1)
                pool.sem_clear(s.stats_ready)
                pool.tensor_scalar(veps[:, :], mv[:, 1:2], EPS, None, ALU.add).then_inc(s.veps_ready, 1)
                pool.wait_ge(s.veps_ready, 1)
                pool.sem_clear(s.veps_ready)
                pool.tensor_tensor(rstd[:, :], veps[:, :], consts[:, 0:1], ALU.pow).then_inc(s.rstd_ready, 1)

            def product(i, n, in0, in1):
                if n >= NZ:
                    pool.wait_ge(s.p_pair, N_POOL * i + n - NZ + 1)
                elif later(i):
                    pool.wait_ge(s.p_pair, N_POOL * i + last_use(n, NZ, N_POOL))
                pool.tensor_tensor(zp[n % NZ].rearrange("p (w d t) -> p w d t", w=2, d=HD), in0, in1,
                                   ALU.mult).then_inc(s.p_product, 1)

            def pair(i, n, qk):
                pool.wait_ge(s.p_product, N_POOL * i + n + 1)
                if n >= SP_:
                    pool.wait_ge(s.p_summed, N_POOL * i + n - SP_ + 1)
                elif later(i):
                    pool.wait_ge(s.p_summed, N_POOL * i + last_use(n, SP_, N_POOL))
                lo, hi = halves(zp[n % NZ], qk)
                pool.tensor_tensor(lo_out(sp_[n % SP_], qk), lo, hi, ALU.add).then_inc(s.p_pair, 1)

            def turn(i, before=True, after=True):
                if after:
                    root()
                pool.wait_ge(s.q2_loaded, 16 * (i + 1))
                pool.wait_ge(s.k2_loaded, 16 * (i + 1))
                for n, c in enumerate(QK_POOL):
                    product(i, n, bcast_q, shifted(k2, 2 * c))
                    if n:
                        pair(i, n - 1, True)
                pair(i, len(QK_POOL) - 1, True)
                if before:
                    root()
                pool.wait_ge(s.v2_loaded, 16 * (i + 1))
                pool.wait_ge(s.prob_ready, i + 1)
                for m, c in enumerate(AV_POOL):
                    n = len(QK_POOL) + m
                    product(i, n, bcast_p(c), shifted(v2, 2 * c))
                    if m:
                        pair(i, n - 1, False)
                pair(i, N_POOL - 1, False)

            root()
            turn(0, before=False)
            with pool.Fori(1, TILES - 1) as i:
                turn(i)
            turn(TILES - 1, after=False)
            root()

            pool.wait_ge(s.ffn_added, TILES)
            pool.wait_ge(s.x2_stored, 16 * TILES)
            pool.memset(ones, 1.0).then_inc(s.tri_ready, 1)
            pool.memset(tri, 1.0).then_inc(s.tri_ready, 1)
            pool.iota(token, pattern=[[P, TILES]], base=0, channel_multiplier=1).then_inc(s.tri_ready, 1)
            pool.iota(slot_no, pattern=[[1, SLOT_TILES]], base=0, channel_multiplier=0,
                      allow_small_or_imprecise_dtypes=True).then_inc(s.tri_ready, 1)
            pool.memset(zeros48, 0).then_inc(s.tri_ready, 1)
            pool.iota(codes, pattern=[[1, CODES]], base=0, channel_multiplier=0,
                      allow_small_or_imprecise_dtypes=True).then_inc(s.tri_ready, 1)
            pool.wait_ge(s.tri_ready, 6)
            pool.affine_select(out=tri, in_=tri, compare_op=ALU.is_ge, fill=0.0, base=-1,
                               pattern=[[1, P]], channel_multiplier=-1).then_inc(s.tri_ready, 1)
            pool.wait_ge(s.slots_ready, 1)
            pool.wait_ge(s.ids_zeroed, 16)
            for i in range(TILES):
                for k in range(2):
                    pool.indirect_dma_start(out=ids_dram, out_offset=bass.IndirectOffsetOnAxis(ap=slot_of[:, i, k:k + 1], axis=0),
                                            in_=token[:, i:i + 1], in_offset=None).then_inc(s.ids_scattered, 16)
            pool.memset(wl, 0.0).then_inc(s.added, 1)
            pool.wait_ge(s.ids_loaded, 16)
            def expert_turn(it):
                for u in range(UNROLL):
                    if later(it):
                        pool.wait_ge(S_(f"gathered{u}"), 16 * it)
                    if later(it):
                        pool.wait_ge(S_(f"turned{u}"), it)
                    pool.tensor_copy(cols[:, u:u + 1], ids[:, bass.ds(UNROLL * it + u, 1)]).then_inc(S_(f"col_ready{u}"), 1)
                    pool.wait_ge(S_(f"col_ready{u}"), 1)
                    pool.sem_clear(S_(f"col_ready{u}"))
                    pool.indirect_dma_start(out=xg[u], out_offset=None, in_=x2_rows,
                                            in_offset=bass.IndirectOffsetOnAxis(ap=cols[:, u:u + 1], axis=0)
                                            ).then_inc(S_(f"gathered{u}"), 16)
                pool.wait_ge(s.picked_ready, it + 1)
                pool.wait_ge(s.added, it + 1)
                pool.tensor_tensor(wl, wl, picked, ALU.add).then_inc(s.added, 1)

            expert_turn(0)
            with pool.Fori(1, SLOT_TILES // UNROLL) as it:
                expert_turn(it)
            for u in range(UNROLL):
                pool.wait_ge(S_(f"y_stored{u}"), 16 * (SLOT_TILES // UNROLL))
                pool.wait_ge(S_(f"dn_done{u}"), SLOT_TILES // UNROLL)
            pool.memset(orow[0:1, :], 1.0).then_inc(s.const3_zeroed, 1)

            def gather_tile(i):
                for k in range(2):
                    gathered = (s.y1_gathered, s.y2_gathered)[k]
                    if later(i):
                        pool.wait_ge(gathered, 16 * i)
                    if later(i):
                        pool.wait_ge(s.normed, 2 * i)
                    pool.tensor_copy(cols[:, k:k + 1], slot_of[:, bass.ds(i, 1), k]).then_inc(s.y_col, 1)
                    pool.wait_ge(s.y_col, 1)
                    pool.sem_clear(s.y_col)
                    pool.indirect_dma_start(out=yg[k], out_offset=None, in_=y_slots,
                                            in_offset=bass.IndirectOffsetOnAxis(ap=cols[:, k:k + 1], axis=0)
                                            ).then_inc(gathered, 16)
                root()
                root()

            gather_tile(0)
            with pool.Fori(1, TILES) as i:
                gather_tile(i)
        @block.scalar
        def _(act_e):
            sc = act_e
            sc.wait_ge(s.small_loaded, 16 * N_SM)
            sc.activation(gates[:, :], gates[:, :], ACT.Tanh).then_inc(s.gates_done, 1)

            def turned(i):
                if later(i):
                    sc.wait_ge(s.down_done, i)
                sc.wait_ge(s.x2_turned, i + 1)
                sc.activation(x2T, ps[:, 7, :], ACT.Copy).then_inc(s.x2T_ready, 1)

            def copy_qkv(i):
                if later(i):
                    sc.wait_ge(s.q_stored, 16 * i)
                    sc.wait_ge(s.k_stored, 16 * i)
                    sc.wait_ge(s.v_stored, 16 * i)
                for n, dst in enumerate((q, k_pad[:, LEFT:LEFT + T], v_pad[:, LEFT:LEFT + T])):
                    sc.wait_ge(s.projected, 3 * i + n + 1)
                    sc.activation(dst, ps[:, (4, 5, 4)[n], :], ACT.Identity,
                                  bias=bias_att[:, n:n + 1]).then_inc(s.copied, 1)

            def gate(i):
                sc.wait_ge(s.g_done, i + 1)
                sc.activation(th, ps[:, 2, :], ACT.Tanh, scale=0.5).then_inc(s.tanh_done, 1)

            def act_copy(i):
                sc.wait_ge(s.act_turned, i + 1)
                sc.activation(actT, ps[:, 7, :], ACT.Copy).then_inc(s.actT_ready, 1)

            def exps(i):
                sc.wait_ge(s.diff_read, i + 1)
                sc.activation(diff, diff, ACT.Exp, scale=HD ** -0.5).then_inc(s.exp_done, 1)

            def copy_o(i):
                sc.wait_ge(s.d_summed, N_DVE * (i + 1))
                sc.wait_ge(s.p_summed, N_POOL * (i + 1))
                if later(i):
                    sc.wait_ge(s.o_stored, 16 * i)
                sc.activation(o2, ps[:, 6, :], ACT.Copy).then_inc(s.o2_ready, 1)

            def gate_attention(i):
                sc.wait_ge(s.wo_done, i + 1)
                sc.activation(xo[:, :], ps[:, 5, :], ACT.Identity, bias=gbias[:, 0:1],
                              scale=gates[:, 0:1]).then_inc(s.xo_ready, 1)

            def turn(i, before=True, after=True):
                if after:
                    copy_qkv(i + 1)
                if before:
                    gate_attention(i - 1)
                exps(i)
                if before:
                    turned(i - 1)
                    gate(i - 1)
                    act_copy(i - 1)
                copy_o(i)

            sc.wait_ge(s.iota_done, 5)
            sc.wait_ge(s.gbias_done, 1)
            copy_qkv(0)
            turn(0, before=False)
            with sc.Fori(1, TILES - 1) as i:
                turn(i)
            turn(TILES - 1, after=False)
            gate_attention(TILES - 1)
            turned(TILES - 1)
            gate(TILES - 1)
            act_copy(TILES - 1)
            sc.wait_ge(s.slots_ready, 1)
            sc.activation(e1, margin[:, :], ACT.Exp).then_inc(s.e1_done, 1)
            def expert_turn(it):
                for u in range(UNROLL):
                    sc.wait_ge(S_(f"turned{u}"), it + 1)
                    sc.activation(xT[u], ps[:, u, :], ACT.Copy).then_inc(S_(f"xT_ready{u}"), 1)
                for u in range(UNROLL):
                    sc.wait_ge(S_(f"gu_done{u}"), it + 1)
                    sc.activation(th2[u], ps[:, u, 0:EI], ACT.Tanh, scale=0.5).then_inc(S_(f"th2_done{u}"), 1)
                for u in range(UNROLL):
                    sc.wait_ge(S_(f"act2_turned{u}"), it + 1)
                    sc.activation(act2T[u], ps[:, u, 0:EI], ACT.Copy).then_inc(S_(f"act2T_ready{u}"), 1)
                for u in range(UNROLL):
                    sc.wait_ge(S_(f"dn_done{u}"), it + 1)
                    if later(it):
                        sc.wait_ge(S_(f"y_stored{u}"), 16 * it)
                    sc.activation(ysb[u], ps[:, 3 + u, :], ACT.Copy).then_inc(S_(f"ysb_ready{u}"), 1)

            expert_turn(0)
            with sc.Fori(1, SLOT_TILES // UNROLL) as it:
                expert_turn(it)
            for k in range(4):
                sc.wait_ge(s.wl_turned, k + 1)
                sc.activation(wlT[:, k, :], ps[:, k, :], ACT.Copy).then_inc(s.wlT_ready, 1)

            def attend(i):
                for n in range(2):
                    sc.wait_ge(s.v_done, 2 * i + n + 1)
                    sc.activation(vv[n], ps[:, 2 + n, :], ACT.Identity, bias=bias_att[:, 6:7]).then_inc(s.pv_ready, 1)
                sc.wait_ge(s.d3_ready, i + 1)
                sc.activation(pr, pr, ACT.Exp, scale=LH ** -0.5).then_inc(s.e3_done, 1)
                sc.wait_ge(s.pT_done, i + 1)
                sc.activation(prT, ps[:, 4, :], ACT.Copy).then_inc(s.pv_ready, 1)
                sc.wait_ge(s.av_done, i + 1)
                sc.activation(xh.rearrange("p (j f t) -> p f j t", f=2, t=LH),
                              ps[:, 2:4, 0:4 * LH].rearrange("p f (j t) -> p f j t", t=LH), ACT.Copy).then_inc(s.xh_ready, 1)
                sc.wait_ge(s.wo3_done, i + 1)
                sc.activation(xo[:, :], ps[:, 5, :], ACT.Identity, bias=gbias[:, 1:2],
                              scale=gates[:, 1:2]).then_inc(s.xo3_ready, 1)

            def ffn_turn(i):
                sc.wait_ge(s.xf_turned, i + 1)
                sc.activation(xfT, ps[:, 6, :], ACT.Copy).then_inc(s.xfT_ready, 1)

            attend(0)
            with sc.Fori(1, TILES) as i:
                ffn_turn(i - 1)
                attend(i)
            ffn_turn(TILES - 1)

        @block.vector
        def _(dve):
            dve.wait_ge(s.gates_done, 1)
            for n in range(2):
                dve.tensor_tensor(gbias[:, n:n + 1], bias_att[:, 4 * n + 3:4 * n + 4], gates[:, n:n + 1],
                                  ALU.mult).then_inc(s.gbias_done, 1) if n else \
                    dve.tensor_tensor(gbias[:, 0:1], bias_att[:, 3:4], gates[:, 0:1], ALU.mult)

            def statistics(src):
                dve.bn_stats(stats[:, :], src).then_inc(s.halves_ready, 1)
                dve.wait_ge(s.halves_ready, 1)
                dve.sem_clear(s.halves_ready)
                dve.bn_aggr(mv[:, :], stats[:, :]).then_inc(s.stats_ready, 1)

            def root_in():
                dve.wait_ge(s.rstd_ready, 1)
                dve.sem_clear(s.rstd_ready)

            def normalise(src, out, done):
                dve.tensor_scalar(out, src, mv[:, 0:1], rstd[:, :], ALU.subtract, ALU.mult).then_inc(done, 1)

            def row_tile(i):
                return X[:, bass.ds(i, 1), :].squeeze(1)

            sv = ps[:, 0:2, :].rearrange("p b (w t) -> p (b w) t", t=CT)
            dv = diff.rearrange("p (w t) -> p w t", t=CT)

            def per_window(t):
                return t.unsqueeze(1).broadcast_to([P, WINDOW, CT])

            def product(i, n, in0, in1):
                if n >= NZ:
                    dve.wait_ge(s.d_pair, N_DVE * i + n - NZ + 1)
                elif later(i):
                    dve.wait_ge(s.d_pair, N_DVE * i + last_use(n, NZ, N_DVE))
                dve.tensor_tensor(zd[n % NZ].rearrange("p (w d t) -> p w d t", w=2, d=HD), in0, in1,
                                  ALU.mult).then_inc(s.d_product, 1)

            def pair(i, n, qk):
                dve.wait_ge(s.d_product, N_DVE * i + n + 1)
                if n >= SD:
                    dve.wait_ge(s.d_summed, N_DVE * i + n - SD + 1)
                elif later(i):
                    dve.wait_ge(s.d_summed, N_DVE * i + last_use(n, SD, N_DVE))
                lo, hi = halves(zd[n % NZ], qk)
                dve.tensor_tensor(lo_out(sd[n % SD], qk), lo, hi, ALU.add).then_inc(s.d_pair, 1)

            def qk_products(i, after):
                if after:
                    start(i + 1)
                dve.wait_ge(s.q2_loaded, 16 * (i + 1))
                dve.wait_ge(s.k2_loaded, 16 * (i + 1))
                for n, c in enumerate(QK_DVE):
                    product(i, n, bcast_q, shifted(k2, 2 * c))
                    if n == 0 and after:
                        finish_start(i + 1)
                    if n:
                        pair(i, n - 1, True)
                pair(i, len(QK_DVE) - 1, True)

            def scores_max(i):
                dve.wait_ge(s.d_summed, N_DVE * i + len(QK_DVE))
                dve.wait_ge(s.p_summed, N_POOL * i + len(QK_POOL))
                dve.tensor_reduce(smax, sv.rearrange("p w t -> p t w"), AX.X, ALU.max).then_inc(s.a_link, 1)
                dve.wait_ge(s.a_link, A_LINKS * i + 1)
                dve.tensor_tensor(dv, sv, per_window(smax), ALU.subtract).then_inc(s.diff_read, 1)

            def sum_exps(i):
                dve.wait_ge(s.exp_done, i + 1)
                dve.tensor_reduce(ssum, dv.rearrange("p w t -> p t w"), AX.X, ALU.add).then_inc(s.a_link, 1)

            def probabilities(i):
                dve.wait_ge(s.a_link, A_LINKS * i + 2)
                dve.reciprocal(srec, ssum).then_inc(s.a_link, 1)
                dve.wait_ge(s.a_link, A_LINKS * i + 3)
                dve.tensor_tensor(dv, dv, per_window(srec), ALU.mult).then_inc(s.prob_ready, 1)

            def av_products(i, gate_at=None):
                dve.wait_ge(s.v2_loaded, 16 * (i + 1))
                dve.wait_ge(s.prob_ready, i + 1)
                for m, c in enumerate(AV_DVE):
                    n = len(QK_DVE) + m
                    product(i, n, bcast_p(c), shifted(v2, 2 * c))
                    if m:
                        pair(i, n - 1, False)
                    if m == gate_at:
                        gating(i - 1)
                pair(i, N_DVE - 1, False)

            def residual(i, meanwhile=lambda: None):
                dve.wait_ge(s.xo_ready, i + 1)
                dve.tensor_tensor(X[:, bass.ds(i, 1), :], X[:, bass.ds(i, 1), :], xo[:, :].unsqueeze(1),
                                  ALU.add).then_inc(s.x1_ready, 1)
                dve.wait_ge(s.x1_ready, 1)
                dve.sem_clear(s.x1_ready)
                statistics(row_tile(i))
                meanwhile()
                root_in()
                if later(i):
                    dve.wait_ge(s.x2_stored, 16 * i)
                    dve.wait_ge(s.x2_turned, i)
                normalise(row_tile(i), x2, s.b_normed)

            def start(i):
                dve.wait_ge(s.x_loaded, 16 * (i + 1))
                dve.tensor_copy(held[:, :], consts[:, 0:1])
                statistics(row_tile(i))

            def finish_start(i):
                root_in()
                if later(i):
                    dve.wait_ge(s.projected, 3 * i)
                normalise(row_tile(i), xn[:, :], s.a_normed)

            def router(i):
                n = R_LINKS * i
                dve.wait_ge(s.logits_done, i + 1)
                dve.tensor_copy(lg, ps[:, 7, 0:EXPERTS]).then_inc(s.logits_read, 1)
                dve.wait_ge(s.logits_read, i + 1)
                dve.tensor_copy(held[:, :], lg[:, 0:1])
                dve.max(top, lg).then_inc(s.top_ready, 1)
                dve.wait_ge(s.top_ready, 1)
                dve.sem_clear(s.top_ready)
                dve.max_index(topi, top, lg).then_inc(s.r_link, 1)
                dve.wait_ge(s.r_link, n + 1)
                dve.tensor_copy(topf, topi[:, 0:2]).then_inc(s.r_link, 1)
                dve.tensor_tensor(margin[:, bass.ds(i, 1)], top[:, 1:2], top[:, 0:1], ALU.subtract).then_inc(s.r_link, 1)
                dve.wait_ge(s.r_link, n + 3)
                for k in range(2):
                    dve.tensor_scalar(onehot[:, bass.ds(i, 1), k, :].squeeze(1), iota16, topf[:, k:k + 1], None,
                                      ALU.is_equal).then_inc(s.r_link if k else s.routed, 1)

            def gating(i):
                dve.wait_ge(s.tanh_done, i + 1)
                dve.scalar_tensor_tensor(th, th, 1.0, ps[:, 2, :], ALU.add, ALU.mult).then_inc(s.u_done, 1)
                dve.wait_ge(s.u_done, 2 * (i + 1))
                dve.scalar_tensor_tensor(act, th, 0.5, ps[:, 3, :], ALU.mult, ALU.mult).then_inc(s.act_ready, 1)

            def add_ffn(i):
                dve.wait_ge(s.down_done, i + 1)
                dve.scalar_tensor_tensor(X[:, bass.ds(i, 1), :], ps[:, 3:4, :], gates[:, 2:3], X[:, bass.ds(i, 1), :],
                                         ALU.mult, ALU.add).then_inc(s.ffn_added, 1)

            dve.wait_ge(s.iota_done, 5)
            def turn(i, before2=True, before=True, after=True):
                qk_products(i, after)
                scores_max(i)
                if before:
                    residual(i - 1, lambda: sum_exps(i))
                else:
                    sum_exps(i)
                probabilities(i)
                if before2:
                    add_ffn(i - 2)
                if before:
                    router(i - 1)
                av_products(i, 3 if before else None)

            start(0)
            finish_start(0)
            turn(0, before2=False, before=False)
            turn(1, before2=False)
            with dve.Fori(2, TILES - 1) as i:
                turn(i)
            turn(TILES - 1, after=False)
            residual(TILES - 1)
            add_ffn(TILES - 2)
            router(TILES - 1)
            gating(TILES - 1)
            add_ffn(TILES - 1)

            links = [0]

            def link(ins):
                links[0] += 1
                ins.then_inc(s.c_link, 1)
                dve.wait_ge(s.c_link, links[0])

            dve.wait_ge(s.r_link, R_LINKS * TILES)
            dve.wait_ge(s.routed, TILES)
            dve.wait_ge(s.tri_ready, 7)
            link(dve.tensor_tensor(chosen, onehot[:, :, 0, :], onehot[:, :, 1, :], ALU.add))
            dve.wait_ge(s.ranked, 1)
            rank = ps[:, 0, 0:(TILES + 1) * EXPERTS].rearrange("p (i e) -> p i e", e=EXPERTS)
            link(dve.tensor_scalar(cnt, rank[:, TILES, :], float(P - 1), None, ALU.add))
            link(dve.tensor_copy(cnti, cnt))
            link(dve.tensor_scalar(cnti, cnti, 7, None, ALU.logical_shift_right))
            link(dve.tensor_copy(ntile, cnti))
            src = ntile
            for n, d in enumerate((1, 2, 4, 8)):
                dst = cum[n % 2]
                dve.tensor_copy(dst[:, 0:d], src[:, 0:d])
                link(dve.tensor_tensor(dst[:, d:], src[:, d:], src[:, 0:EXPERTS - d], ALU.add))
                src = dst
            link(dve.tensor_tensor(first, src, ntile, ALU.subtract))
            link(dve.tensor_tensor(prod, onehot[:, 0:TILES, :, :],
                                   rank[:, 0:TILES, :].unsqueeze(2).broadcast_to([P, TILES, 2, EXPERTS]), ALU.mult))
            link(dve.tensor_reduce(pos, prod, AX.X, ALU.add))
            link(dve.tensor_tensor(prod, onehot[:, 0:TILES, :, :].rearrange("p i k e -> p (i k) e"),
                                   first.unsqueeze(1).broadcast_to([P, 2 * TILES, EXPERTS]), ALU.mult))
            link(dve.tensor_reduce(base, prod, AX.X, ALU.add))
            link(dve.tensor_copy(posi, pos))
            dve.tensor_scalar(rowi, posi, P - 1, None, ALU.bitwise_and)
            link(dve.tensor_scalar(tili, posi, 7, None, ALU.logical_shift_right))
            dve.tensor_copy(rowf, rowi)
            link(dve.tensor_copy(tilf, tili))
            link(dve.tensor_tensor(base, base, tilf, ALU.add))
            dve.scalar_tensor_tensor(slot_of[:, :, :].rearrange("p i k -> p (i k)"), rowf, float(SLOT_TILES), base,
                                     ALU.mult, ALU.add).then_inc(s.slots_ready, 1)
            am = at_most[:, 0:SLOT_TILES // 2 * EXPERTS].rearrange("p (s e) -> p s e", e=EXPERTS)
            half = 24
            for n in range(2):
                hs = slice(n * half, (n + 1) * half)
                am = at_most[:, 0:half * EXPERTS].rearrange("p (s e) -> p s e", e=EXPERTS)
                link(dve.tensor_tensor(am, first[0:1, :].unsqueeze(1).broadcast_to([1, half, EXPERTS]),
                                       slot_no[0:1, hs].unsqueeze(2).broadcast_to([1, half, EXPERTS]), ALU.is_le))
                link(dve.tensor_reduce(exp_of[0:1, hs], am, AX.X, ALU.add))
            dve.tensor_scalar(exp_id[0:1, :], exp_of[0:1, :], -1.0, None, ALU.add).then_inc(s.experts_known, 1)
            dve.wait_ge(s.e1_done, 1)
            link(dve.tensor_scalar(den, e1, 1.0, None, ALU.add))
            link(dve.reciprocal(den, den))
            dve.tensor_scalar(comb[:, 0, :], den, gates[:, 2:3], None, ALU.mult)
            link(dve.scalar_tensor_tensor(comb[:, 1, :], e1, gates[:, 2:3], den, ALU.mult, ALU.mult))
            dve.wait_ge(s.tables_loaded, 32)
            for b in range(4):
                for sh in range(32):
                    ins = dve.tensor_scalar(bits[:, :, :, sh], words[:, b, :, :], sh, 1, ALU.logical_shift_right, ALU.bitwise_and)
                link(ins)
                flat = bits.rearrange("p o w s -> p (o w s)")
                cf = code.rearrange("p o i -> p (o i)")
                if b == 0:
                    link(dve.tensor_copy(cf, flat))
                else:
                    link(dve.scalar_tensor_tensor(cf, flat, float(1 << b), cf, ALU.mult, ALU.add))

            def expert_turn(it):
                for u in range(UNROLL):
                    dve.wait_ge(S_(f"th2_done{u}"), it + 1)
                    dve.scalar_tensor_tensor(th2[u], th2[u], 1.0, ps[:, u, 0:EI], ALU.add, ALU.mult).then_inc(S_(f"act2_ready{u}"), 1)
                    dve.wait_ge(S_(f"act2_ready{u}"), 2 * it + 1)
                    dve.scalar_tensor_tensor(act2[u], th2[u], 0.5, ps[:, u, EI:2 * EI], ALU.mult, ALU.mult).then_inc(S_(f"act2_ready{u}"), 1)
                dve.wait_ge(s.added, it + 1)
                dve.scalar_tensor_tensor(picked, code, codes[:, bass.ds(it, 1)],
                                         lut[:, :, bass.ds(it, 1)].broadcast_to([P, 4, T]),
                                         ALU.is_equal, ALU.mult).then_inc(s.picked_ready, 1)

            expert_turn(0)
            with dve.Fori(1, SLOT_TILES // UNROLL) as it:
                expert_turn(it)
            dve.wait_ge(s.const3_loaded, 16 * 5)

            def mix(i):
                for k in range(2):
                    if k:
                        dve.wait_ge(s.half_mixed, 1)
                        dve.sem_clear(s.half_mixed)
                    dve.wait_ge((s.y1_gathered, s.y2_gathered)[k], 16 * (i + 1))
                    dve.scalar_tensor_tensor(X[:, bass.ds(i, 1), :], yg[k].unsqueeze(1), comb[:, k, bass.ds(i, 1)],
                                             X[:, bass.ds(i, 1), :], ALU.mult, ALU.add).then_inc(s.half_mixed, 1)
                dve.wait_ge(s.half_mixed, 1)
                dve.sem_clear(s.half_mixed)
                statistics(row_tile(i))
                root_in()
                normalise(row_tile(i), xn[:, :], s.normed)

            def attend(i):
                n = 3 * i
                for m, dst in enumerate((qT, kT)):
                    dve.wait_ge(s.qkT_done, 2 * i + m + 1)
                    dve.tensor_tensor(dst.rearrange("p (j o) -> p j o", j=TC), ps[:, m, :].rearrange("p (j o) -> p j o", j=TC),
                                      bqk[:, m, :].unsqueeze(1).broadcast_to([P, TC, P]), ALU.add).then_inc(s.qk3_ready, 1)
                s3v = ps[:, 0:2, 0:4 * C].rearrange("p f (j e) -> p f j e", e=C)
                d3v = pr.rearrange("p (j f e) -> p f j e", f=2, e=C)
                bc = lambda t: t.rearrange("p (f j) -> p f j", f=2).unsqueeze(3).broadcast_to([P, 2, 4, C])
                dve.wait_ge(s.s3_done, i + 1)
                dve.tensor_reduce(m3, s3v, AX.X, ALU.max).then_inc(s.d_link, 1)
                dve.wait_ge(s.d_link, n + 1)
                dve.tensor_tensor(d3v, s3v, bc(m3), ALU.subtract).then_inc(s.d3_ready, 1)
                dve.wait_ge(s.e3_done, i + 1)
                dve.tensor_reduce(s3, d3v, AX.X, ALU.add).then_inc(s.d_link, 1)
                dve.wait_ge(s.d_link, n + 2)
                dve.reciprocal(r3, s3).then_inc(s.d_link, 1)
                dve.wait_ge(s.d_link, n + 3)
                dve.tensor_tensor(d3v, d3v, bc(r3), ALU.mult).then_inc(s.p3_ready, 1)

            def residual3(i):
                dve.wait_ge(s.xo3_ready, i + 1)
                dve.tensor_tensor(X[:, bass.ds(i, 1), :], X[:, bass.ds(i, 1), :], xo[:, :].unsqueeze(1),
                                  ALU.add).then_inc(s.x1_ready, 1)
                dve.wait_ge(s.x1_ready, 1)
                dve.sem_clear(s.x1_ready)
                statistics(row_tile(i))
                root_in()
                if later(i):
                    dve.wait_ge(s.xf_turned, i)
                normalise(row_tile(i), xf, s.normed)

            def finish(i):
                dve.wait_ge(s.y3_done, i + 1)
                if later(i):
                    dve.wait_ge(s.out_stored, 16 * i)
                dve.scalar_tensor_tensor(obuf.unsqueeze(1), ps[:, 7:8, :], gates[:, 3:4], X[:, bass.ds(i, 1), :],
                                         ALU.mult, ALU.add).then_inc(s.out_ready, 1)

            mix(0)
            attend(0)
            residual3(0)
            mix(1)
            attend(1)
            finish(0)
            residual3(1)
            with dve.Fori(2, TILES) as i:
                mix(i)
                attend(i)
                finish(i - 1)
                residual3(i)
            finish(TILES - 1)

        @block.tensor
        def _(pe):
            def mm(out, lhsT, rhs, start=True, stop=True, **kw):
                return pe.matmul(out, lhsT, rhs, start=start, stop=stop, **kw)

            def turn4(out, src, done):
                for j in range(4):
                    ins = pe.transpose(out[:, j * P:(j + 1) * P], src[:, j * P:(j + 1) * P], ident[:, :])
                ins.then_inc(done, 1)

            def project(i, n):
                if n == 0:
                    pe.wait_ge(s.a_normed, i + 1)
                    if later(i):
                        pe.wait_ge(s.copied, 3 * i)
                    mm(ps[:, 4, :], w_att[:, 0, :], xn[:, :]).then_inc(s.projected, 1)
                    pe.wait_ge(s.ctx_loaded, 16 * (i + 1))
                    mm(ps[:, 5, :], w_att[:, 1, :], ctx_t[:, :]).then_inc(s.projected, 1)
                else:
                    pe.wait_ge(s.copied, 3 * i + 1)
                    mm(ps[:, 4, :], w_att[:, 2, :], ctx_t[:, :]).then_inc(s.projected, 1)

            def add_pair(i, c, pools, dves, base_p, base_d):
                if c in pools:
                    n = base_p + pools.index(c)
                    pe.wait_ge(s.p_pair, N_POOL * i + n + 1)
                    return sp_[n % SP_], s.p_summed
                n = base_d + dves.index(c)
                pe.wait_ge(s.d_pair, N_DVE * i + n + 1)
                return sd[n % SD], s.d_summed

            def scores(i, after):
                if after:
                    project(i + 1, 0)
                for c in range(PAIRS):
                    if c == 2 and after:
                        project(i + 1, 1)
                    zz, done = add_pair(i, c, QK_POOL, QK_DVE, 0, 0)
                    if c == 0 and later(i):
                        pe.wait_ge(s.diff_read, i)
                    zz = zz.rearrange("p (w d t) -> p w d t", w=2, t=CT)
                    for d in range(HD // 2):
                        ins = mm(ps[:, c // 4, c % 4 * 2 * CT:(c % 4 + 1) * 2 * CT], ident[:, :], zz[:, :, d, :],
                                 d == 0, d == HD // 2 - 1)
                    ins.then_inc(done, 1)

            def outputs(i, c):
                zz, done = add_pair(i, c, AV_POOL, AV_DVE, len(QK_POOL), len(QK_DVE))
                if c == 0 and later(i):
                    pe.wait_ge(s.o2_ready, i)
                mm(ps[:, 6, :], ident[:, :], zz, c == 0, c == PAIRS - 1).then_inc(done, 1)

            def wo(i, after):
                pe.wait_ge(s.copied, 3 * (i + 2) + 2 if after else 3 * TILES)
                pe.wait_ge(s.oT_loaded, 16 * (i + 1))
                mm(ps[:, 5, :], w_att[:, 3, :], oT).then_inc(s.wo_done, 1)

            def turn_x2(i):
                pe.wait_ge(s.b_normed, i + 1)
                turn4(ps[:, 7, :], x2, s.x2_turned)

            def route(i):
                pe.wait_ge(s.x2T_ready, i + 1)
                for k in range(TC):
                    ins = mm(ps[:, 7, 0:EXPERTS], x2T[:, k * P:(k + 1) * P], w_router[:, k, :], k == 0, k == TC - 1)
                ins.then_inc(s.logits_done, 1)

            def gate_up(i, n):
                half, k = divmod(n, TC)
                if n == TC and later(i):
                    pe.wait_ge(s.ffn_added, i)
                ins = mm(ps[:, 2 + half, :], x2T[:, k * P:(k + 1) * P], w_sgu[:, k, half * SI:(half + 1) * SI], k == 0, k == TC - 1)
                if k == TC - 1:
                    ins.then_inc(s.u_done if half else s.g_done, 1)

            def turn_act(i):
                pe.wait_ge(s.act_ready, i + 1)
                pe.wait_ge(s.logits_read, i + 1)
                turn4(ps[:, 7, :], act, s.act_turned)

            def down(i):
                pe.wait_ge(s.actT_ready, i + 1)
                for k in range(4):
                    ins = mm(ps[:, 3, :], actT[:, k * P:(k + 1) * P], w_sdn[:, k, :], k == 0, k == 3)
                ins.then_inc(s.down_done, 1)

            pe.wait_ge(s.small_loaded, 16 * N_SM)
            pe.wait_ge(s.ident_done, 2)
            def turn(i, before2=True, before=True, after=True):
                scores(i, after)
                if before:
                    wo(i - 1, after)
                if before2:
                    down(i - 2)
                if before:
                    turn_x2(i - 1)
                    route(i - 1)
                    for n in range(2 * TC):
                        gate_up(i - 1, n)
                for c in range(PAIRS):
                    outputs(i, c)
                    if before and c == 5:
                        turn_act(i - 1)

            project(0, 0)
            project(0, 1)
            pe.wait_ge(s.shared_loaded, 32)
            turn(0, before2=False, before=False)
            turn(1, before2=False)
            with pe.Fori(2, TILES - 1) as i:
                turn(i)
            turn(TILES - 1, after=False)
            wo(TILES - 1, False)
            down(TILES - 2)
            turn_x2(TILES - 1)
            route(TILES - 1)
            for n in range(2 * TC):
                gate_up(TILES - 1, n)
            turn_act(TILES - 1)
            down(TILES - 1)

            pe.wait_ge(s.tri_ready, 7)
            pe.wait_ge(s.c_link, 1)
            flat = chosen.rearrange("p i e -> p (i e)")
            mm(ps[:, 0, 0:(TILES + 1) * EXPERTS], tri, flat, True, False)
            for i in range(TILES):
                ins = mm(ps[:, 0, (i + 1) * EXPERTS:(TILES + 1) * EXPERTS], ones,
                         chosen[:, i:i + 1, :].broadcast_to([P, TILES - i, EXPERTS]), False, i == TILES - 1)
            ins.then_inc(s.ranked, 1)
            pe.wait_ge(s.experts_known, 1)
            pe.wait_ge(s.experts_loaded, 16 * 2 * (EXPERTS - LATE_EXPERTS))
            pe.wait_ge(s.late_loaded, 16 * 2 * LATE_EXPERTS)
            def expert_turn(it):
                for u in range(UNROLL):
                    pe.wait_ge(S_(f"gathered{u}"), 16 * (it + 1))
                    if later(it):
                        pe.wait_ge(S_(f"act2T_ready{u}"), it)
                    turn4(ps[:, u, :], xg[u], S_(f"turned{u}"))
                e = []
                for u in range(UNROLL):
                    e.append(pe.value_load(exp_id[0:1, bass.ds(UNROLL * it + u, 1)], min_val=0, max_val=EXPERTS - 1))
                    pe.wait_ge(S_(f"xT_ready{u}"), it + 1)
                    for k in range(TC):
                        ins = mm(ps[:, u, 0:2 * EI], xT[u][:, k * P:(k + 1) * P],
                                 w_gu[:, bass.ds(e[u], 1), k, :], k == 0, k == TC - 1)
                    ins.then_inc(S_(f"gu_done{u}"), 1)
                for u in range(UNROLL):
                    pe.wait_ge(S_(f"act2_ready{u}"), 2 * it + 2)
                    pe.transpose(ps[:, u, 0:EI], act2[u], ident[:, :]).then_inc(S_(f"act2_turned{u}"), 1)
                for u in range(UNROLL):
                    pe.wait_ge(S_(f"act2T_ready{u}"), it + 1)
                    if later(it):
                        pe.wait_ge(S_(f"ysb_ready{u}"), it)
                    mm(ps[:, 3 + u, :], act2T[u], w_dn[:, bass.ds(e[u], 1), :]).then_inc(S_(f"dn_done{u}"), 1)

            expert_turn(0)
            with pe.Fori(1, SLOT_TILES // UNROLL) as it:
                expert_turn(it)
            pe.wait_ge(s.added, 1 + CODES)
            pe.wait_ge(S_("ysb_ready0"), SLOT_TILES // UNROLL)
            for k in range(4):
                for o in range(4):
                    ins = pe.transpose(ps[:, k, o * P:(o + 1) * P], wl[:, o, k * P:(k + 1) * P], ident[:, :])
                ins.then_inc(s.wl_turned, 1)
            pe.wait_ge(s.wlT_ready, 4)
            pe.wait_ge(s.const3_loaded, 16 * 5)

            def qkv(i):
                pe.wait_ge(s.normed, 2 * i + 1)
                if later(i):
                    pe.wait_ge(s.d3_ready, i)
                for j in range(TC):
                    ins = mm(ps[:, 0, j * P:(j + 1) * P], xn[:, j * P:(j + 1) * P], w_att[:, 4, :])
                ins.then_inc(s.qkT_done, 1)
                pe.wait_ge(s.ctx_loaded, 16 * (TILES + 1 + i))
                for j in range(TC):
                    ins = mm(ps[:, 1, j * P:(j + 1) * P], ctx_t[:, j * P:(j + 1) * P], w_att[:, 5, :])
                ins.then_inc(s.qkT_done, 1)
                if later(i):
                    pe.wait_ge(s.xh_ready, i)
                for n in range(2):
                    mm(ps[:, 2 + n, :], w_att[:, 6 + n, :], ctx_t[:, :]).then_inc(s.v_done, 1)

            def scores(i):
                pe.wait_ge(s.qk3_ready, 2)
                pe.sem_clear(s.qk3_ready)
                for f in range(2):
                    rows = slice(f * LH, (f + 1) * LH)
                    for b in range(2):
                        for j in range(TC):
                            at = slice(j * P + b * C, j * P + (b + 1) * C)
                            ins = mm(ps[b * C:(b + 1) * C, f, j * C:(j + 1) * C], qT[rows, at], kT[rows, at])
                ins.then_inc(s.s3_done, 1)

            def weighted(i):
                pe.wait_ge(s.p3_ready, i + 1)
                turn4(ps[:, 4, :], pr, s.pT_done)
                pe.wait_ge(s.pv_ready, 3)
                pe.sem_clear(s.pv_ready)
                for f in range(2):
                    rows = slice(f * C, (f + 1) * C)
                    for b in range(2):
                        v = vv[0 if b == f else 1]
                        for j in range(TC):
                            ins = mm(ps[b * C:(b + 1) * C, 2 + f, j * LH:(j + 1) * LH],
                                     prT[rows, j * P + b * C:j * P + (b + 1) * C],
                                     v[rows, (2 * j + f) * LH:(2 * j + f + 1) * LH])
                ins.then_inc(s.av_done, 1)
                pe.wait_ge(s.xh_ready, i + 1)
                if later(i):
                    pe.wait_ge(s.xo3_ready, i)
                mm(ps[:, 5, :], w_att[:, 8, :], xh).then_inc(s.wo3_done, 1)

            def turn_xf(i):
                pe.wait_ge(s.normed, 2 * i + 2)
                turn4(ps[:, 6, :], xf, s.xf_turned)

            def linear(i):
                pe.wait_ge(s.xfT_ready, i + 1)
                mm(ps[:, 7, :], orow[0:1, :], brow[0:1, :], True, False)
                for k in range(4):
                    ins = mm(ps[:, 7, :], xfT[:, k * P:(k + 1) * P], wlT[:, k, :], False, k == 3)
                ins.then_inc(s.y3_done, 1)

            qkv(0)
            scores(0)
            weighted(0)
            with pe.Fori(1, TILES) as i:
                turn_xf(i - 1)
                qkv(i)
                scores(i)
                linear(i - 1)
                weighted(i)
            turn_xf(TILES - 1)
            linear(TILES - 1)


_NAMES = ["x", "ctx", "gate4", "wq0", "wk0", "wv0", "wo0", "wq1", "wk1", "wv1", "wo1", "bq0", "bk0", "bv0", "bo0",
          "bq1", "bk1", "bv1", "bo1", "w_router", "w_sgu", "w_sdn", "w_gu", "w_dn", "lut4", "words", "bias"]


def kernel(**inputs):
    import numpy as np
    import concourse.bacc as bacc
    from concourse.bass_utils import run_bass_kernel_spmd as run

    v = {k: np.asarray(t) for k, t in inputs.items()}

    def by_rows(w, chunks):
        return w.T.reshape(chunks, P, w.shape[0]).transpose(1, 0, 2)

    laid = {"x": v["x"], "ctx": v["ctx_4096"], "gate4": np.concatenate([v["g_xattn"], v["g_ffn"]])}
    for layer in range(2):
        for m in "qkvo":
            laid[f"w{m}{layer}"] = v[f"L{layer}_xattn_W{m}"].T
            laid[f"b{m}{layer}"] = v[f"L{layer}_xattn_b{m}"]
    laid["w_router"] = by_rows(v["L0_ffn_gate_w"], TC)
    laid["w_sgu"] = by_rows(v["L0_ffn_shared_w_gate_up"], TC)
    laid["w_sdn"] = by_rows(v["L0_ffn_shared_w_down"], 4)
    gu = v["L0_ffn_w_gate_up"].transpose(0, 2, 1).reshape(EXPERTS, TC, P, 2 * EI).transpose(0, 2, 1, 3)
    laid["w_gu"] = gu.reshape(EXPERTS * P, TC * 2 * EI)
    laid["w_dn"] = v["L0_ffn_w_down"].transpose(0, 2, 1).reshape(EXPERTS * P, T)
    laid["lut4"] = v["L1_ffn_lut4"].reshape(4, P, CODES).transpose(1, 0, 2)
    laid["words"] = v["L1_ffn_qweight"][0:4].reshape(4, 4, P, T // 32).transpose(2, 0, 1, 3)
    laid["bias"] = v["L1_ffn_bias"]

    nc = bacc.Bacc("TRN2", target_bir_lowering=False, num_devices=1)
    arrays, aps = {}, {}
    for name in _NAMES:
        t = np.ascontiguousarray(laid[name])
        arrays[f"in_{name}"] = t
        aps[name] = nc.dram_tensor(f"in_{name}", t.shape, mybir.dt.from_np(t.dtype), kind="ExternalInput").ap()
    aps["out"] = nc.dram_tensor("out_0", (B, C, T), F32, kind="ExternalOutput").ap()
    build(nc, aps)
    r = run(nc, [arrays], core_ids=[0])
    return r.results[0]["out_0"]
```

```python
from contextlib import ExitStack

import concourse.bass as bass
from concourse import mybir

P = 128
B, C, T = 32, 64, 512
TILES = B * C // P
TC = T // P
HEADS0, WINDOW = 8, 16
HD = C // HEADS0
GROUPS = 2 * HEADS0
LEFT = WINDOW // 2
PADDED = T + WINDOW - 1
HEADS1 = 8
LH = T // HEADS1
EXPERTS, EI, SI = 16, 128, 512
SLOT_TILES = 48
SLOTS = SLOT_TILES * P
UNROLL = 3
TURNS = SLOT_TILES // UNROLL
POOL_CHOICES = tuple(range(1, 2 * TILES, 2))
WL_BANKS = 0, 1, 6, 7
CODES = 16
EPS = 1e-5
WORK = 10750

ALU = mybir.AluOpType
ACT = mybir.ActivationFunctionType
AX = mybir.AxisListType
F32, F16, I32, U32 = mybir.dt.float32, mybir.dt.float16, mybir.dt.int32, mybir.dt.uint32

CT = 64
CHUNKS = T // CT
HALO = CT + WINDOW - 1
PAIRS = WINDOW // 2
QK_POOL, AV_POOL = (2, 5), (2, 5, 7)
QK_DVE = tuple(c for c in range(PAIRS) if c not in QK_POOL)
AV_DVE = tuple(c for c in range(PAIRS) if c not in AV_POOL)
N_DVE, N_POOL = len(QK_DVE) + len(AV_DVE), len(QK_POOL) + len(AV_POOL)
SD, SP_ = 3, 2
NZ = 3
A_LINKS = 3
R_LINKS = 4
LATE_EXPERTS = 5


def later(i, first=1):
    return not (isinstance(i, int) and i < first)


def follows(i, n):
    return not (isinstance(i, int) and i + n >= TILES)


def build(nc, a):
    ctx = ExitStack()
    with ctx:
        def sb(name, shape, dt=F32):
            return ctx.enter_context(nc.sbuf_tensor(name, shape, dt))

        def sem(name):
            return ctx.enter_context(nc.semaphore(name))

        X = sb("X", [P, TILES, T])
        w_att = sb("w_att", [P, 8, P])
        bias_att = sb("bias_att", [P, 8])
        ident = sb("ident", [P, P])
        gates = sb("gates", [P, 4])
        gbias = sb("gbias", [P, 2])
        consts = sb("consts", [P, 1])
        stats = sb("stats", [P, 6])
        mv = sb("mv", [P, 2])
        veps = sb("veps", [P, 1])
        held = sb("held", [P, 1])
        rstd = sb("rstd", [P, 1])
        ctx_t = sb("ctx_t", [P, T])
        xn = sb("xn", [P, T])
        xo = sb("xo", [P, T])
        onehot = sb("onehot", [P, TILES, 2, EXPERTS])
        margin = sb("margin", [P, TILES])
        comb = sb("comb", [P, 2, TILES])
        slot_of = sb("slot_of", [P, TILES, 2], U32)
        cols = sb("cols", [P, 4], U32)
        w_exp = sb("w_exp", [P, EXPERTS, TC * 2 * EI + T])
        w_gu = w_exp[:, :, 0:TC * 2 * EI].rearrange("p e (k n) -> p e k n", k=TC)
        w_dn = w_exp[:, :, TC * 2 * EI:]
        work = sb("work", [P, WORK])
        ps = ctx.enter_context(nc.psum_tensor("ps", [P, 8, 512], F32))

        used = {}

        def carve(area, key, n):
            at = used.get(key, 0)
            used[key] = at + n
            assert used[key] <= area.shape[1], (key, used[key])
            return area[:, at:at + n]

        w_shared = sb("w_shared", [P, TC * 2 * SI + 4 * T])
        w_sgu = w_shared[:, 0:TC * 2 * SI].rearrange("p (k n) -> p k n", k=TC)
        w_sdn = w_shared[:, TC * 2 * SI:].rearrange("p (k n) -> p k n", k=4)

        w1 = lambda n: carve(work, 1, n)
        late = w_exp[:, EXPERTS - LATE_EXPERTS:, :].rearrange("p e n -> p (e n)")
        w1l = lambda n: carve(late, "1l", n)
        q = w1(T)
        k_pad = w1(PADDED + 1)
        v_pad = w1(PADDED + 1)
        q2 = w1(HD * CT)
        k2 = w1(HD * HALO)
        v2 = w1(HD * HALO)
        diff = w1(WINDOW * CT)
        attended = used[1]
        x2 = w1(T)
        x2T = w1(T)
        th = w1(T)
        act = th
        w_router = w1(TC * EXPERTS).rearrange("p (k e) -> p k e", k=TC)
        iota16 = w1(EXPERTS)
        smax = w1(CT)
        ssum = w1(CT)
        srec = w1(CT)
        lg = w1(EXPERTS)
        top = w1(8)
        topi = w1(8).bitcast(U32)
        topf = w1(2)
        actT = x2T
        o2 = w1(T)
        oT = w1(T)
        xffn = w1(T)
        zd = [w1l(2 * HD * CT) for _ in range(NZ)]
        sd = [w1l(HD * CT) for _ in range(SD)]
        zp = [w1l(2 * HD * CT) for _ in range(NZ)]
        sp_ = [w1(HD * CT) for _ in range(SP_)]

        w2 = lambda n: carve(work, 2, n)
        tri = w2(P)
        ones = w2(P)
        chosen = w2(TILES * EXPERTS).rearrange("p (i e) -> p i e", e=EXPERTS)
        prod = w2(TILES * 2 * EXPERTS).rearrange("p (i k e) -> p i k e", k=2, e=EXPERTS)
        pos = w2(TILES * 2)
        base = w2(TILES * 2)
        posi = w2(TILES * 2).bitcast(I32)
        rowi = w2(TILES * 2).bitcast(I32)
        tili = w2(TILES * 2).bitcast(I32)
        rowf = w2(TILES * 2)
        tilf = w2(TILES * 2)
        cnt = w2(EXPERTS)
        cnti = w2(EXPERTS).bitcast(I32)
        cum = [w2(EXPERTS) for _ in range(2)]
        scan = [w2((TILES + 1) * EXPERTS) for _ in range(2)]
        ntile = w2(EXPERTS)
        first = w2(EXPERTS)
        token = w2(TILES)
        ids = w2(SLOT_TILES).bitcast(U32)
        row_no = w2(P)
        row_no16 = w2(P // 2).bitcast(F16)
        slot_no16 = w2(SLOT_TILES // 2).bitcast(F16)
        slot_no = w2(SLOT_TILES)
        exp_of = w2(SLOT_TILES)
        exp_id = w2(SLOT_TILES).bitcast(I32)
        at_most = prod[0:1].rearrange("p i k e -> p (i k e)")
        e1 = w2(TILES)
        den = w2(TILES)
        lut = w2(4 * CODES).rearrange("p (o c) -> p o c", o=4)
        words = w2(4 * 4 * 16).bitcast(I32).rearrange("p (b o w) -> p b o w", b=4, o=4)
        codes = w2(CODES)
        low_bits = w2(1).bitcast(I32)
        assert used[2] <= attended
        to_row = work[:, used[2]:used[2] + TILES * P].bitcast(F16).rearrange("p (c r) -> p c r", r=P)
        xg = [w2(T) for _ in range(UNROLL)]
        xT = [w2(T) for _ in range(UNROLL)]
        th2 = [w2(EI) for _ in range(UNROLL)]
        act2 = [w2(EI) for _ in range(UNROLL)]
        act2T = [w2(EI) for _ in range(UNROLL)]
        ysb = [w2(T) for _ in range(UNROLL)]
        w2s = lambda n: carve(w_shared, "2s", n)
        code = w2s(4 * T).rearrange("p (o i) -> p o i", o=4)
        picked = w2s(4 * T).rearrange("p (o i) -> p o i", o=4)
        to_tile = w2s(TILES * SLOT_TILES).bitcast(F16).rearrange("p (c s) -> p c s", s=SLOT_TILES)
        bits = picked.rearrange("p o i -> p (o i)").bitcast(I32).rearrange("p (b m n) -> p b m n", b=4, n=8)
        w3 = lambda n: carve(w_exp.rearrange("p e n -> p (e n)"), 3, n)
        wl = work[:, WORK - 4 * T:WORK].rearrange("p (o i) -> p o i", o=4)
        assert used[2] <= WORK - 4 * T, used
        wlT = w3(4 * T).rearrange("p (k o) -> p k o", k=4)
        yg = [w3(T) for _ in range(2)]
        qT = w3(T)
        kT = w3(T)
        vv = [w3(T) for _ in range(2)]
        pr = w3(T)
        prT = w3(T)
        xh = w3(T)
        xf = w3(T)
        xfT = w3(T)
        obuf = w3(T)
        m3 = w3(8)
        s3 = w3(8)
        r3 = w3(8)
        bqk = w3(2 * P).rearrange("p (a o) -> p a o", a=2)
        bias_ffn = w3(T)

        x2_rows = nc.dram_tensor("x2_rows", [B * C, T], F32, kind="Internal").ap()
        y_slots = nc.dram_tensor("y_slots", [SLOTS, T], F32, kind="Internal").ap()
        y_rows = y_slots.rearrange("(r s) d -> r s d", s=SLOT_TILES)
        q_dram = nc.dram_tensor("q_dram", [TILES, CHUNKS, P, CT], F32, kind="Internal").ap()
        kv_dram = [nc.dram_tensor(f"{n}_dram", [TILES, CHUNKS, P, HALO], F32, kind="Internal").ap() for n in "kv"]
        o_dram = nc.dram_tensor("o_dram", [TILES, CHUNKS, P, CT], F32, kind="Internal").ap()
        x_rows = a["x"].rearrange("b c t -> (b c) t")
        c_rows = a["ctx"].rearrange("b c t -> (b c) t")
        o_rows = a["out"].rearrange("b c t -> (b c) t")

        S = {}
        for name in """zeroed small_loaded layer1_loaded shared_loaded iota_done ident_done gates_done gbias_done x_loaded ctx_loaded
                experts_loaded stats_ready veps_ready rstd_ready a_normed b_normed normed projected copied
                q_stored k_stored v_stored q2_loaded k2_loaded v2_loaded o_stored oT_loaded late_loaded
                d_product d_pair p_product p_pair d_summed p_summed
                diff_read exp_done wo_done xo_ready o2_ready
                x1_ready a_link x2_stored x2_turned x2T_ready logits_done logits_read r_link routed g_done u_done
                tanh_done act_ready act_turned actT_ready down_done xffn_ready ffn_added
                c_link tri_ready numbers_ready ranked slots_ready e1_done to_row_ready d_to_tile_ready p_to_tile_ready
                ids_summed ids_ready tables_loaded
                experts_known picked_ready added
                y_col wl_turned wlT_ready const3_loaded gated_bias bias_added y1_gathered y2_gathered q3_done k3_done xn_ready
                qk3_ready v_done v3_copied prT_ready halves_ready half_mixed top_ready s3_done d_link d3_ready e3_done p3_ready pT_done av_done
                xh_ready wo3_done xo3_ready xf_turned xfT_ready y3_done out_ready out_stored""".split():
            S[name] = sem(name)
        for u in range(UNROLL):
            for name in "gathered turned xT_ready gu_done th2_done act2_ready act2_turned act2T_ready dn_done ysb_ready y_stored col_ready".split():
                S[f"{name}{u}"] = sem(f"{name}{u}")
        s = type("Sems", (), S)

        def S_(name):
            return S[name]


        def windows(t, start, n, step, width):
            return bass.AP(t.tensor, t.offset + start, [list(t.ap[0]), [step, n], [1, width]])

        def shifted(t, w):
            return bass.AP(t.tensor, t.offset + w, [list(t.ap[0]), [1, 2], [HALO, HD], [1, CT]])

        def last_use(n, buffers, count):
            return max(m for m in range(count) if m % buffers == n % buffers) + 1 - count

        bcast_q = q2.rearrange("p (d t) -> p d t", d=HD).unsqueeze(1).broadcast_to([P, 2, HD, CT])

        def bcast_p(c):
            return diff.rearrange("p (w t) -> p w t", t=CT)[:, 2 * c:2 * c + 2, :].unsqueeze(2).broadcast_to([P, 2, HD, CT])

        def halves(z, qk):
            if qk:
                v = z.rearrange("p (w h n) -> p w h n", w=2, h=2)
                return v[:, :, 0, :], v[:, :, 1, :]
            return z[:, 0:HD * CT], z[:, HD * CT:]

        def lo_out(t, qk):
            return t.rearrange("p (w n) -> p w n", w=2) if qk else t

        def by_rows(dram, i, width):
            return dram[bass.ds(i, 1)].squeeze(0).rearrange("c (g d) t -> (c g) d t", d=HD)

        N_FIRST = 2 + 2 + 1
        N_LAYER1 = 2
        block = ctx.enter_context(nc.Block())

        @block.sync
        def _(sp):
            def load(dst, src, sm=s.small_loaded):
                sp.dma_start(dst, src).then_inc(sm, 16)

            load(X[:, 0, :], x_rows[0:P, :], s.x_loaded)
            load(ctx_t[:, :], c_rows[0:P, :], s.ctx_loaded)
            sp.wait_ge(s.zeroed, 1)
            for h in range(2):
                rows = slice(h * C, (h + 1) * C)
                load(w_att[rows, 0:4, rows], a["w_att0"])

            def store_qkv(i):
                for n, (pad, done) in enumerate(((q, s.q_stored), (k_pad, s.k_stored), (v_pad, s.v_stored))):
                    sp.wait_ge(s.copied, 3 * i + n + 1)
                    rows = (q_dram, *kv_dram)[n][bass.ds(i, 1)].squeeze(0).rearrange("c r t -> r c t")
                    sp.dma_start(rows, windows(pad, 0, CHUNKS, CT, HALO) if n else
                                 q.rearrange("p (c t) -> p c t", t=CT)).then_inc(done, 16)

            def load_qk(i):
                if later(i):
                    sp.wait_ge(s.p_product, N_POOL * (i - 1) + len(QK_POOL))
                sp.wait_ge(s.q_stored, 16 * (i + 1))
                if later(i):
                    sp.wait_ge(s.d_product, N_DVE * (i - 1) + len(QK_DVE))
                sp.dma_start(q2.rearrange("p (d t) -> p d t", d=HD), by_rows(q_dram, i, CT)).then_inc(s.q2_loaded, 16)
                sp.wait_ge(s.k_stored, 16 * (i + 1))
                sp.dma_start(k2.rearrange("p (d t) -> p d t", d=HD), by_rows(kv_dram[0], i, HALO)).then_inc(s.k2_loaded, 16)

            def load_v(i):
                sp.wait_ge(s.v_stored, 16 * (i + 1))
                sp.dma_start(v2.rearrange("p (d t) -> p d t", d=HD), by_rows(kv_dram[1], i, HALO)).then_inc(s.v2_loaded, 16)

            def load_x(i):
                sp.wait_ge(s.x_loaded, 16 * i)
                sp.dma_start(X[:, bass.ds(i, 1), :], x_rows[bass.ds(i * P, P), :]).then_inc(s.x_loaded, 16)

            def load_ctx(i):
                sp.wait_ge(s.projected, 3 * i)
                sp.dma_start(ctx_t[:, :], c_rows[bass.ds(i * P, P), :]).then_inc(s.ctx_loaded, 16)

            def load_expert(e, done=s.experts_loaded):
                sp.dma_start(w_exp[:, bass.ds(e, 1), 0:TC * 2 * EI], a["w_gu"][bass.ds(e * P, P), :]).then_inc(done, 16)
                sp.dma_start(w_exp[:, bass.ds(e, 1), TC * 2 * EI:], a["w_dn"][bass.ds(e * P, P), :]).then_inc(done, 16)

            def store_x2(i):
                sp.wait_ge(s.b_normed, i + 1)
                sp.dma_start(x2_rows[bass.ds(i * P, P), :], x2).then_inc(s.x2_stored, 16)

            def turn_o(i):
                sp.wait_ge(s.o2_ready, i + 1)
                sp.dma_start(o_dram[bass.ds(i, 1)].squeeze(0).rearrange("c r t -> (c r t)").rearrange("(p n) -> p n", p=P),
                             o2).then_inc(s.o_stored, 16)
                sp.wait_ge(s.o_stored, 16 * (i + 1))
                sp.dma_start(oT.rearrange("p (c t) -> p c t", t=CT),
                             o_dram[bass.ds(i, 1)].squeeze(0).rearrange("c r t -> r c t")).then_inc(s.oT_loaded, 16)

            def turn(i, before=True, after=True, expert=True):
                load_v(i)
                if expert:
                    load_expert(i)
                if after:
                    store_qkv(i + 1)
                    load_qk(i + 1)
                if before:
                    store_x2(i - 1)
                if after and not (isinstance(i, int) and i == TILES - 2):
                    load_ctx(i + 2)
                    load_x(i + 2)
                turn_o(i)

            load_x(1)
            store_qkv(0)
            load_qk(0)
            load_ctx(1)
            load(w_router, a["w_router"], s.shared_loaded)
            load(w_sgu, a["w_sgu"], s.shared_loaded)
            load(w_sdn, a["w_sdn"], s.shared_loaded)
            for h in range(2):
                rows = slice(h * C, (h + 1) * C)
                load(w_att[rows, 4:8, rows], a["w_att1"], s.layer1_loaded)
            turn(0, before=False)
            with sp.Fori(1, EXPERTS - LATE_EXPERTS) as i:
                turn(i)
            with sp.Fori(EXPERTS - LATE_EXPERTS, TILES - 2) as i:
                turn(i, expert=False)
            last = TILES - 1
            turn(TILES - 2, expert=False)
            turn(last, after=False, expert=False)
            store_x2(last)
            sp.wait_ge(s.projected, 3 * TILES)
            sp.dma_start(ctx_t[:, :], c_rows[0:P, :]).then_inc(s.ctx_loaded, 16)
            sp.wait_ge(s.d_summed, N_DVE * TILES)
            sp.wait_ge(s.p_summed, N_POOL * TILES)
            load(lut, a["lut4"], s.tables_loaded)
            load(words, a["words"], s.tables_loaded)
            for e in range(EXPERTS - LATE_EXPERTS, EXPERTS):
                load_expert(e, s.late_loaded)
            with sp.Fori(0, TURNS) as it:
                for u in range(UNROLL):
                    sp.wait_ge(S_(f"ysb_ready{u}"), it + 1)
                    sp.dma_start(y_rows[:, bass.ds(UNROLL * it + u, 1), :], ysb[u]).then_inc(S_(f"y_stored{u}"), 16)
            for u in range(UNROLL):
                sp.wait_ge(S_(f"dn_done{u}"), TURNS)
            for h in range(2):
                for n, name in enumerate(["bq1", "bk1"]):
                    load(bqk[:, n, h * C:(h + 1) * C], a[name].partition_broadcast(P), s.const3_loaded)
            load(bias_ffn, a["bias"].partition_broadcast(P), s.const3_loaded)

            def out_tile(i):
                sp.wait_ge(s.out_ready, i + 1)
                sp.dma_start(o_rows[bass.ds(i * P, P), :], obuf).then_inc(s.out_stored, 16)

            def next_ctx(i):
                sp.wait_ge(s.v_done, i)
                sp.dma_start(ctx_t[:, :], c_rows[bass.ds(i * P, P), :]).then_inc(s.ctx_loaded, 16)

            for i in range(1, 4):
                next_ctx(i)
            with sp.Fori(0, TILES - 4) as i:
                next_ctx(i + 4)
                out_tile(i)
            out_tile(TILES - 4)
            out_tile(TILES - 3)
            out_tile(TILES - 2)
            out_tile(last)
            sp.wait_ge(s.out_stored, 16 * TILES)
            sp.wait_ge(s.x2_stored, 16 * TILES)

        @block.gpsimd
        def _(pool):
            pool.memset(w_att[:, :, :], 0.0).then_inc(s.zeroed, 1)
            pool.memset(consts[:, 0:1], -0.5).then_inc(s.iota_done, 1)
            pool.memset(k_pad, 0.0).then_inc(s.iota_done, 1)
            pool.memset(v_pad, 0.0).then_inc(s.iota_done, 1)
            pool.iota(iota16, pattern=[[1, EXPERTS]], base=0, channel_multiplier=0,
                      allow_small_or_imprecise_dtypes=True).then_inc(s.iota_done, 1)
            pool.memset(ident[:, :], 0.0).then_inc(s.ident_done, 1)
            pool.wait_ge(s.ident_done, 1)
            pool.affine_select(out=ident[:, :], in_=ident[:, :], compare_op=ALU.not_equal, fill=1.0, base=0,
                               pattern=[[-1, P]], channel_multiplier=1).then_inc(s.ident_done, 1)

            def root():
                pool.wait_ge(s.stats_ready, 1)
                pool.sem_clear(s.stats_ready)
                pool.tensor_scalar(veps[:, :], mv[:, 1:2], EPS, None, ALU.add).then_inc(s.veps_ready, 1)
                pool.wait_ge(s.veps_ready, 1)
                pool.sem_clear(s.veps_ready)
                pool.tensor_tensor(rstd[:, :], veps[:, :], consts[:, 0:1], ALU.pow).then_inc(s.rstd_ready, 1)

            def product(i, n, in0, in1):
                if n >= NZ:
                    pool.wait_ge(s.p_pair, N_POOL * i + n - NZ + 1)
                elif later(i):
                    pool.wait_ge(s.p_pair, N_POOL * i + last_use(n, NZ, N_POOL))
                pool.tensor_tensor(zp[n % NZ].rearrange("p (w d t) -> p w d t", w=2, d=HD), in0, in1,
                                   ALU.mult).then_inc(s.p_product, 1)

            def pair(i, n, qk):
                pool.wait_ge(s.p_product, N_POOL * i + n + 1)
                if n >= SP_:
                    pool.wait_ge(s.p_summed, N_POOL * i + n - SP_ + 1)
                elif later(i):
                    pool.wait_ge(s.p_summed, N_POOL * i + last_use(n, SP_, N_POOL))
                lo, hi = halves(zp[n % NZ], qk)
                pool.tensor_tensor(lo_out(sp_[n % SP_], qk), lo, hi, ALU.add).then_inc(s.p_pair, 1)

            def add_ffn(i):
                pool.wait_ge(s.xffn_ready, i + 1)
                pool.tensor_tensor(X[:, bass.ds(i, 1), :], X[:, bass.ds(i, 1), :], xffn.unsqueeze(1),
                                   ALU.add).then_inc(s.ffn_added, 1)

            def turn(i, before2=True, before=True, after=True):
                pool.wait_ge(s.q2_loaded, 16 * (i + 1))
                pool.wait_ge(s.k2_loaded, 16 * (i + 1))
                for n, c in enumerate(QK_POOL):
                    product(i, n, bcast_q, shifted(k2, 2 * c))
                    if n:
                        pair(i, n - 1, True)
                pair(i, len(QK_POOL) - 1, True)
                if after:
                    root()
                if before:
                    root()
                if before2:
                    add_ffn(i - 2)
                pool.wait_ge(s.v2_loaded, 16 * (i + 1))
                pool.wait_ge(s.exp_done, i + 1)
                for m, c in enumerate(AV_POOL):
                    n = len(QK_POOL) + m
                    product(i, n, bcast_p(c), shifted(v2, 2 * c))
                    if m:
                        pair(i, n - 1, False)
                pair(i, N_POOL - 1, False)

            root()
            turn(0, before2=False, before=False)
            turn(1, before2=False)
            with pool.Fori(2, TILES - 1) as i:
                turn(i)
            turn(TILES - 1, after=False)

            pool.wait_ge(s.d_summed, N_DVE * TILES)
            pool.wait_ge(s.p_summed, N_POOL * TILES)
            pool.memset(ones, 1.0).then_inc(s.tri_ready, 1)
            pool.memset(tri, 1.0).then_inc(s.tri_ready, 1)
            pool.iota(token, pattern=[[P, TILES]], base=0, channel_multiplier=1,
                      allow_small_or_imprecise_dtypes=True).then_inc(s.tri_ready, 1)
            pool.iota(slot_no, pattern=[[1, SLOT_TILES]], base=0, channel_multiplier=0,
                      allow_small_or_imprecise_dtypes=True).then_inc(s.tri_ready, 1)
            pool.iota(row_no, pattern=[[1, P]], base=0, channel_multiplier=0,
                      allow_small_or_imprecise_dtypes=True).then_inc(s.tri_ready, 1)
            pool.iota(codes, pattern=[[1, CODES]], base=0, channel_multiplier=0,
                      allow_small_or_imprecise_dtypes=True).then_inc(s.tri_ready, 1)
            pool.memset(low_bits.bitcast(mybir.dt.uint8), 1).then_inc(s.tri_ready, 1)
            pool.wait_ge(s.tri_ready, 7)
            pool.affine_select(out=tri, in_=tri, compare_op=ALU.is_ge, fill=0.0, base=-1,
                               pattern=[[1, P]], channel_multiplier=-1).then_inc(s.tri_ready, 1)
            root()
            add_ffn(TILES - 2)
            pool.wait_ge(s.slots_ready, 1)
            add_ffn(TILES - 1)
            pool.wait_ge(s.ffn_added, TILES)
            pool.wait_ge(s.x2_stored, 16 * TILES)
            for c in POOL_CHOICES:
                pool.tensor_scalar(to_tile[:, c, :], slot_no, base[:, c:c + 1], token[:, c // 2:c // 2 + 1],
                                   ALU.is_equal, ALU.mult).then_inc(s.p_to_tile_ready, 1)
            pool.memset(wl, 0.0).then_inc(s.added, 1)
            pool.wait_ge(s.ids_ready, 1)

            def gather_slots(it):
                for u in range(UNROLL):
                    if later(it):
                        pool.wait_ge(S_(f"gathered{u}"), 16 * it)
                        pool.wait_ge(S_(f"turned{u}"), it)
                    pool.tensor_copy(cols[:, u:u + 1], ids[:, bass.ds(UNROLL * it + u, 1)]).then_inc(S_(f"col_ready{u}"), 1)
                    pool.wait_ge(S_(f"col_ready{u}"), 1)
                    pool.sem_clear(S_(f"col_ready{u}"))
                    pool.indirect_dma_start(out=xg[u], out_offset=None, in_=x2_rows,
                                            in_offset=bass.IndirectOffsetOnAxis(ap=cols[:, u:u + 1], axis=0)
                                            ).then_inc(S_(f"gathered{u}"), 16)

            gather_slots(0)
            with pool.Fori(1, TURNS) as it:
                gather_slots(it)
            for u in range(UNROLL):
                pool.wait_ge(S_(f"y_stored{u}"), 16 * (TURNS))
                pool.wait_ge(S_(f"dn_done{u}"), TURNS)

            def gather(i):
                for k in range(2):
                    gathered = (s.y1_gathered, s.y2_gathered)[k]
                    if later(i):
                        pool.wait_ge(gathered, 16 * i)
                        pool.wait_ge(s.xn_ready, i)
                    pool.tensor_copy(cols[:, k:k + 1], slot_of[:, bass.ds(i, 1), k]).then_inc(s.y_col, 1)
                    pool.wait_ge(s.y_col, 1)
                    pool.sem_clear(s.y_col)
                    pool.indirect_dma_start(out=yg[k], out_offset=None, in_=y_slots,
                                            in_offset=bass.IndirectOffsetOnAxis(ap=cols[:, k:k + 1], axis=0)
                                            ).then_inc(gathered, 16)

            def add_bias(i):
                pool.wait_ge(s.normed, i + 1)
                pool.tensor_tensor(X[:, bass.ds(i, 1), :], X[:, bass.ds(i, 1), :], bias_ffn.unsqueeze(1),
                                   ALU.add).then_inc(s.bias_added, 1)

            def turn3(i):
                if later(i):
                    root()
                    add_bias(i - 1)
                if follows(i, 2):
                    root()
                if follows(i, 3):
                    gather(i + 3)

            gather(0)
            root()
            gather(1)
            root()
            gather(2)
            pool.wait_ge(s.gated_bias, 1)
            turn3(0)
            with pool.Fori(1, TILES - 3) as i:
                turn3(i)
            for i in range(TILES - 3, TILES):
                turn3(i)
            root()
            add_bias(TILES - 1)

        @block.scalar
        def _(act_e):
            sc = act_e
            sc.dma_start(gates[:, 0:4], a["gate4"].partition_broadcast(P)).then_inc(s.small_loaded, 16)
            for h in range(2):
                sc.dma_start(bias_att[h * C:(h + 1) * C, :], a["b_att"]).then_inc(s.small_loaded, 16)
            sc.wait_ge(s.small_loaded, 16 * N_FIRST)
            sc.activation(gates[:, :], gates[:, :], ACT.Tanh).then_inc(s.gates_done, 1)

            def turned(i):
                if later(i):
                    sc.wait_ge(s.down_done, i)
                sc.wait_ge(s.x2_turned, i + 1)
                sc.activation(x2T, ps[:, 7, :], ACT.Copy).then_inc(s.x2T_ready, 1)

            def copy_projected(i, n):
                dst = (q, k_pad[:, LEFT:LEFT + T], v_pad[:, LEFT:LEFT + T])[n]
                if later(i):
                    sc.wait_ge((s.q_stored, s.k_stored, s.v_stored)[n], 16 * i)
                sc.wait_ge(s.projected, 3 * i + n + 1)
                sc.activation(dst, ps[:, (4, 5, 4)[n], :], ACT.Identity,
                              bias=bias_att[:, n:n + 1]).then_inc(s.copied, 1)

            def gate(i):
                sc.wait_ge(s.g_done, i + 1)
                sc.activation(th, ps[:, 2, :], ACT.Tanh, scale=0.5).then_inc(s.tanh_done, 1)

            def act_copy(i):
                sc.wait_ge(s.act_turned, i + 1)
                sc.activation(actT, ps[:, 7, :], ACT.Copy).then_inc(s.actT_ready, 1)

            def exps(i):
                sc.wait_ge(s.diff_read, i + 1)
                sc.activation(diff, diff, ACT.Exp, scale=HD ** -0.5).then_inc(s.exp_done, 1)

            def gate_ffn(i):
                sc.wait_ge(s.down_done, i + 1)
                if later(i):
                    sc.wait_ge(s.ffn_added, i)
                sc.activation(xffn, ps[:, 3, :], ACT.Copy, scale=gates[:, 2:3]).then_inc(s.xffn_ready, 1)

            def gate_attention(i):
                sc.wait_ge(s.wo_done, i + 1)
                sc.activation(xo[:, :], ps[:, 5, :], ACT.Identity, bias=gbias[:, 0:1],
                              scale=gates[:, 0:1]).then_inc(s.xo_ready, 1)

            def turn(i, before2=True, before=True, after=True):
                if before:
                    gate_attention(i - 1)
                exps(i)
                if before2:
                    gate_ffn(i - 2)
                if after:
                    copy_projected(i + 1, 0)
                    copy_projected(i + 1, 1)
                if before:
                    turned(i - 1)
                if after:
                    copy_projected(i + 1, 2)
                if before:
                    gate(i - 1)
                    act_copy(i - 1)

            sc.wait_ge(s.iota_done, 4)
            for n in range(3):
                copy_projected(0, n)
            turn(0, before2=False, before=False)
            sc.wait_ge(s.gbias_done, 2)
            turn(1, before2=False)
            with sc.Fori(2, TILES - 1) as i:
                turn(i)
            turn(TILES - 1, after=False)
            gate_attention(TILES - 1)
            gate_ffn(TILES - 2)
            turned(TILES - 1)
            gate(TILES - 1)
            act_copy(TILES - 1)
            gate_ffn(TILES - 1)
            sc.wait_ge(s.slots_ready, 1)
            sc.activation(e1, margin[:, :], ACT.Exp).then_inc(s.e1_done, 1)

            def copy_xT(it, u):
                sc.wait_ge(S_(f"turned{u}"), it + 1)
                sc.activation(xT[u], ps[:, u % 2, :], ACT.Copy).then_inc(S_(f"xT_ready{u}"), 1)

            def copy_act2(it):
                for u in range(UNROLL):
                    sc.wait_ge(S_(f"act2_turned{u}"), it + 1)
                    sc.activation(act2T[u], ps[:, 2 + u, 0:EI], ACT.Copy).then_inc(S_(f"act2T_ready{u}"), 1)

            def copy_y(it):
                for u in range(UNROLL):
                    sc.wait_ge(S_(f"dn_done{u}"), it + 1)
                    if later(it):
                        sc.wait_ge(S_(f"y_stored{u}"), 16 * it)
                    sc.activation(ysb[u], ps[:, 5 + u, :], ACT.Copy).then_inc(S_(f"ysb_ready{u}"), 1)

            def expert_turn(it):
                copy_xT(it, 0)
                copy_xT(it, 1)
                if later(it):
                    copy_act2(it - 1)
                copy_xT(it, 2)
                if later(it):
                    copy_y(it - 1)
                for u in range(UNROLL):
                    sc.wait_ge(S_(f"gu_done{u}"), it + 1)
                    sc.activation(th2[u], ps[:, 2 + u, 0:EI], ACT.Tanh, scale=0.5).then_inc(S_(f"th2_done{u}"), 1)

            expert_turn(0)
            expert_turn(1)
            with sc.Fori(2, TURNS) as it:
                expert_turn(it)
            copy_act2(TURNS - 1)
            copy_y(TURNS - 1)

            def copy_v(i):
                sc.wait_ge(s.v_done, i + 1)
                sc.activation(vv[0], ps[:, 4, :], ACT.Identity, bias=bias_att[:, 6:7]).then_inc(s.v3_copied, 1)
                for h in range(2):
                    rows, other = slice(h * C, (h + 1) * C), slice((1 - h) * C, (2 - h) * C)
                    sc.activation(vv[1][other], ps[rows, 4, :], ACT.Identity,
                                  bias=bias_att[rows, 6:7]).then_inc(s.v3_copied, 1)

            def copy_xf(i):
                sc.wait_ge(s.xf_turned, i + 1)
                sc.activation(xfT, ps[:, 5, :], ACT.Copy).then_inc(s.xfT_ready, 1)

            def turn3(i):
                sc.wait_ge(s.d3_ready, i + 1)
                sc.activation(pr, pr, ACT.Exp, scale=LH ** -0.5).then_inc(s.e3_done, 1)
                sc.wait_ge(s.pT_done, i + 1)
                sc.activation(prT, ps[:, 6, :], ACT.Copy).then_inc(s.prT_ready, 1)
                sc.wait_ge(s.av_done, i + 1)
                sc.activation(xh.rearrange("p (j f t) -> p f j t", f=2, t=LH),
                              ps[:, 0:2, 0:4 * LH].rearrange("p f (j t) -> p f j t", t=LH), ACT.Copy).then_inc(s.xh_ready, 1)
                if later(i):
                    copy_xf(i - 1)
                sc.wait_ge(s.wo3_done, i + 1)
                sc.activation(xo[:, :], ps[:, 6, :], ACT.Identity, bias=gbias[:, 1:2],
                              scale=gates[:, 1:2]).then_inc(s.xo3_ready, 1)
                if follows(i, 1):
                    copy_v(i + 1)

            sc.wait_ge(s.layer1_loaded, 16 * N_LAYER1)
            copy_v(0)
            for k in range(4):
                sc.wait_ge(s.wl_turned, k + 1)
                sc.activation(wlT[:, k, :], ps[:, WL_BANKS[k], :], ACT.Copy).then_inc(s.wlT_ready, 1)
            turn3(0)
            with sc.Fori(1, TILES - 1) as i:
                turn3(i)
            turn3(TILES - 1)
            copy_xf(TILES - 1)

        @block.vector
        def _(dve):
            def part_statistics(src):
                dve.bn_stats(stats[:, :], src).then_inc(s.halves_ready, 1)

            def aggregate():
                dve.wait_ge(s.halves_ready, 1)
                dve.sem_clear(s.halves_ready)
                dve.bn_aggr(mv[:, :], stats[:, :]).then_inc(s.stats_ready, 1)

            def statistics(src):
                part_statistics(src)
                aggregate()

            def root_in():
                dve.wait_ge(s.rstd_ready, 1)
                dve.sem_clear(s.rstd_ready)

            def normalise(src, out, done):
                dve.tensor_scalar(out, src, mv[:, 0:1], rstd[:, :], ALU.subtract, ALU.mult).then_inc(done, 1)

            def row_tile(i):
                return X[:, bass.ds(i, 1), :].squeeze(1)

            sv = ps[:, 0:2, :].rearrange("p b (w t) -> p (b w) t", t=CT)
            dv = diff.rearrange("p (w t) -> p w t", t=CT)

            def per_window(t):
                return t.unsqueeze(1).broadcast_to([P, WINDOW, CT])

            def product(i, n, in0, in1):
                if n >= NZ:
                    dve.wait_ge(s.d_pair, N_DVE * i + n - NZ + 1)
                elif later(i):
                    dve.wait_ge(s.d_pair, N_DVE * i + last_use(n, NZ, N_DVE))
                dve.tensor_tensor(zd[n % NZ].rearrange("p (w d t) -> p w d t", w=2, d=HD), in0, in1,
                                  ALU.mult).then_inc(s.d_product, 1)

            def pair(i, n, qk):
                dve.wait_ge(s.d_product, N_DVE * i + n + 1)
                if n >= SD:
                    dve.wait_ge(s.d_summed, N_DVE * i + n - SD + 1)
                elif later(i):
                    dve.wait_ge(s.d_summed, N_DVE * i + last_use(n, SD, N_DVE))
                lo, hi = halves(zd[n % NZ], qk)
                dve.tensor_tensor(lo_out(sd[n % SD], qk), lo, hi, ALU.add).then_inc(s.d_pair, 1)

            def qk_products(i, after):
                dve.wait_ge(s.q2_loaded, 16 * (i + 1))
                dve.wait_ge(s.k2_loaded, 16 * (i + 1))
                for n, c in enumerate(QK_DVE):
                    product(i, n, bcast_q, shifted(k2, 2 * c))
                    if n == 3 and later(i):
                        scale_o(i - 1)
                    if n:
                        pair(i, n - 1, True)
                pair(i, len(QK_DVE) - 1, True)

            def scores_max(i):
                dve.wait_ge(s.d_summed, N_DVE * i + len(QK_DVE))
                dve.wait_ge(s.p_summed, N_POOL * i + len(QK_POOL))
                dve.tensor_reduce(smax, sv.rearrange("p w t -> p t w"), AX.X, ALU.max).then_inc(s.a_link, 1)
                dve.wait_ge(s.a_link, A_LINKS * i + 1)
                dve.tensor_tensor(dv, sv, per_window(smax), ALU.subtract).then_inc(s.diff_read, 1)

            def sum_exps(i):
                dve.wait_ge(s.exp_done, i + 1)
                dve.tensor_reduce(ssum, dv.rearrange("p w t -> p t w"), AX.X, ALU.add).then_inc(s.a_link, 1)

            def invert_sums(i):
                dve.wait_ge(s.a_link, A_LINKS * i + 2)
                dve.reciprocal(srec, ssum).then_inc(s.a_link, 1)

            def scale_o(i):
                dve.wait_ge(s.a_link, A_LINKS * (i + 1))
                dve.wait_ge(s.d_summed, N_DVE * (i + 1))
                dve.wait_ge(s.p_summed, N_POOL * (i + 1))
                if later(i):
                    dve.wait_ge(s.o_stored, 16 * i)
                dve.tensor_tensor(o2.rearrange("p (d t) -> p d t", d=HD), ps[:, 6, :].rearrange("p (d t) -> p d t", d=HD),
                                  srec.unsqueeze(1).broadcast_to([P, HD, CT]), ALU.mult).then_inc(s.o2_ready, 1)

            def av_products(i, before):
                dve.wait_ge(s.v2_loaded, 16 * (i + 1))
                dve.wait_ge(s.exp_done, i + 1)
                for m, c in enumerate(AV_DVE):
                    n = len(QK_DVE) + m
                    product(i, n, bcast_p(c), shifted(v2, 2 * c))
                    if m == 2 and before:
                        top_logits(i - 1)
                    if m == 3 and before:
                        expert_numbers(i - 1)
                    if m:
                        pair(i, n - 1, False)
                    if m == 1 and before:
                        copy_logits(i - 1)
                    if m == 2 and before:
                        top_experts(i - 1)
                    if m == 3 and before:
                        mark_experts(i - 1)
                        gating(i - 1)
                pair(i, N_DVE - 1, False)

            def residual(i, meanwhile=lambda: None):
                dve.wait_ge(s.xo_ready, i + 1)
                dve.tensor_tensor(X[:, bass.ds(i, 1), :], X[:, bass.ds(i, 1), :], xo[:, :].unsqueeze(1),
                                  ALU.add).then_inc(s.x1_ready, 1)
                dve.wait_ge(s.x1_ready, 1)
                dve.sem_clear(s.x1_ready)
                statistics(row_tile(i))
                meanwhile()
                root_in()
                if later(i):
                    dve.wait_ge(s.x2_stored, 16 * i)
                    dve.wait_ge(s.x2_turned, i)
                normalise(row_tile(i), x2, s.b_normed)

            def start(i):
                dve.wait_ge(s.x_loaded, 16 * (i + 1))
                dve.tensor_copy(held[:, :], consts[:, 0:1])
                part_statistics(row_tile(i))

            def finish_start(i):
                root_in()
                if later(i):
                    dve.wait_ge(s.projected, 3 * i)
                normalise(row_tile(i), xn[:, :], s.a_normed)

            def copy_logits(i):
                dve.wait_ge(s.logits_done, i + 1)
                dve.tensor_copy(lg, ps[:, 7, 0:EXPERTS]).then_inc(s.logits_read, 1)

            def top_logits(i):
                dve.wait_ge(s.logits_read, i + 1)
                dve.tensor_copy(held[:, :], lg[:, 0:1])
                dve.max(top, lg).then_inc(s.top_ready, 1)

            def top_experts(i):
                dve.wait_ge(s.top_ready, 1)
                dve.sem_clear(s.top_ready)
                dve.max_index(topi, top, lg).then_inc(s.r_link, 1)
                dve.tensor_tensor(margin[:, bass.ds(i, 1)], top[:, 1:2], top[:, 0:1], ALU.subtract).then_inc(s.r_link, 1)

            def expert_numbers(i):
                dve.wait_ge(s.r_link, R_LINKS * i + 2)
                dve.tensor_copy(topf, topi[:, 0:2]).then_inc(s.r_link, 1)

            def mark_experts(i):
                dve.wait_ge(s.r_link, R_LINKS * i + 3)
                for k in range(2):
                    dve.tensor_scalar(onehot[:, bass.ds(i, 1), k, :].squeeze(1), iota16, topf[:, k:k + 1], None,
                                      ALU.is_equal).then_inc(s.r_link if k else s.routed, 1)

            def gating(i):
                dve.wait_ge(s.tanh_done, i + 1)
                dve.scalar_tensor_tensor(th, th, 1.0, ps[:, 2, :], ALU.add, ALU.mult).then_inc(s.u_done, 1)
                dve.wait_ge(s.u_done, 2 * (i + 1))
                dve.scalar_tensor_tensor(act, th, 0.5, ps[:, 3, :], ALU.mult, ALU.mult).then_inc(s.act_ready, 1)

            dve.wait_ge(s.iota_done, 4)
            def turn(i, before=True, after=True):
                qk_products(i, after)
                if after:
                    start(i + 1)
                    aggregate()
                scores_max(i)
                if after:
                    finish_start(i + 1)
                if before:
                    residual(i - 1, lambda: sum_exps(i))
                else:
                    sum_exps(i)
                invert_sums(i)
                av_products(i, before)

            start(0)
            aggregate()
            finish_start(0)
            dve.wait_ge(s.gates_done, 1)
            for n in range(2):
                dve.tensor_tensor(gbias[:, n:n + 1], bias_att[:, 4 * n + 3:4 * n + 4], gates[:, n:n + 1],
                                  ALU.mult).then_inc(s.gbias_done, 1)
            turn(0, before=False)
            with dve.Fori(1, TILES - 1) as i:
                turn(i)
            turn(TILES - 1, after=False)
            scale_o(TILES - 1)
            residual(TILES - 1)
            for step in (copy_logits, top_logits, top_experts, expert_numbers, mark_experts):
                step(TILES - 1)

            links = [0]

            def link(ins):
                links[0] += 1
                ins.then_inc(s.c_link, 1)
                dve.wait_ge(s.c_link, links[0])

            dve.wait_ge(s.r_link, R_LINKS * TILES)
            dve.wait_ge(s.routed, TILES)
            dve.wait_ge(s.tri_ready, 8)
            dve.tensor_copy(row_no16, row_no).then_inc(s.numbers_ready, 1)
            dve.tensor_copy(slot_no16, slot_no).then_inc(s.numbers_ready, 1)
            link(dve.tensor_tensor(chosen, onehot[:, :, 0, :], onehot[:, :, 1, :], ALU.add))
            dve.wait_ge(s.ranked, 1)
            n_rank = TILES * EXPERTS
            dve.memset(scan[0][:, 0:EXPERTS], 0.0)
            link(dve.tensor_copy(scan[0][:, EXPERTS:], ps[:, 1, 0:n_rank]))
            src = scan[0]
            for n, d in enumerate((1, 2, 4, 8)):
                dst = scan[(n + 1) % 2]
                w = d * EXPERTS
                dve.tensor_copy(dst[:, 0:w], src[:, 0:w])
                link(dve.tensor_tensor(dst[:, w:], src[:, w:], src[:, 0:n_rank + EXPERTS - w], ALU.add))
                src = dst
            link(dve.tensor_tensor(src[:, 0:n_rank], src[:, 0:n_rank], ps[:, 0, 0:n_rank], ALU.add))
            rank = src.rearrange("p (i e) -> p i e", e=EXPERTS)
            link(dve.tensor_scalar(cnt, rank[:, TILES, :], float(P - 1), None, ALU.add))
            link(dve.tensor_copy(cnti, cnt))
            link(dve.tensor_scalar(cnti, cnti, 7, None, ALU.logical_shift_right))
            link(dve.tensor_copy(ntile, cnti))
            src = ntile
            for n, d in enumerate((1, 2, 4, 8)):
                dst = cum[n % 2]
                dve.tensor_copy(dst[:, 0:d], src[:, 0:d])
                link(dve.tensor_tensor(dst[:, d:], src[:, d:], src[:, 0:EXPERTS - d], ALU.add))
                src = dst
            link(dve.tensor_tensor(first, src, ntile, ALU.subtract))
            gating(TILES - 1)
            link(dve.tensor_tensor(prod, onehot[:, :, :, :],
                                   rank[:, 0:TILES, :].unsqueeze(2).broadcast_to([P, TILES, 2, EXPERTS]), ALU.mult))
            link(dve.tensor_reduce(pos, prod, AX.X, ALU.add))
            link(dve.tensor_tensor(prod, onehot[:, :, :, :].rearrange("p i k e -> p (i k) e"),
                                   first.unsqueeze(1).broadcast_to([P, 2 * TILES, EXPERTS]), ALU.mult))
            link(dve.tensor_reduce(base, prod, AX.X, ALU.add))
            link(dve.tensor_copy(posi, pos))
            dve.tensor_scalar(rowi, posi, P - 1, None, ALU.bitwise_and)
            link(dve.tensor_scalar(tili, posi, 7, None, ALU.logical_shift_right))
            dve.tensor_copy(rowf, rowi)
            link(dve.tensor_copy(tilf, tili))
            link(dve.tensor_tensor(base, base, tilf, ALU.add))
            dve.scalar_tensor_tensor(slot_of[:, :, :].rearrange("p i k -> p (i k)"), rowf, float(SLOT_TILES), base,
                                     ALU.mult, ALU.add).then_inc(s.slots_ready, 1)
            am = at_most[:, 0:SLOT_TILES // 2 * EXPERTS].rearrange("p (s e) -> p s e", e=EXPERTS)
            half = 24
            for n in range(2):
                hs = slice(n * half, (n + 1) * half)
                am = at_most[:, 0:half * EXPERTS].rearrange("p (s e) -> p s e", e=EXPERTS)
                link(dve.tensor_tensor(am, first[0:1, :].unsqueeze(1).broadcast_to([1, half, EXPERTS]),
                                       slot_no[0:1, hs].unsqueeze(2).broadcast_to([1, half, EXPERTS]), ALU.is_le))
                link(dve.tensor_reduce(exp_of[0:1, hs], am, AX.X, ALU.add))
            dve.tensor_scalar(exp_id[0:1, :], exp_of[0:1, :], -1.0, None, ALU.add).then_inc(s.experts_known, 1)
            dve.wait_ge(s.ffn_added, TILES)
            dve.wait_ge(s.x2_stored, 16 * TILES)
            dve.wait_ge(s.numbers_ready, 2)
            for c in range(2 * TILES):
                dve.tensor_scalar(to_row[:, c, :], row_no16, rowf[:, c:c + 1], None, ALU.is_equal).then_inc(s.to_row_ready, 1)
                if c not in POOL_CHOICES:
                    dve.tensor_scalar(to_tile[:, c, :], slot_no16, base[:, c:c + 1], token[:, c // 2:c // 2 + 1],
                                      ALU.is_equal, ALU.mult).then_inc(s.d_to_tile_ready, 1)
            dve.wait_ge(s.e1_done, 1)
            link(dve.tensor_scalar(den, e1, 1.0, None, ALU.add))
            link(dve.reciprocal(den, den))
            dve.tensor_scalar(comb[:, 0, :], den, gates[:, 2:3], None, ALU.mult)
            link(dve.scalar_tensor_tensor(comb[:, 1, :], e1, gates[:, 2:3], den, ALU.mult, ALU.mult))
            dve.wait_ge(s.ids_summed, 1)
            dve.tensor_copy(ids, ps[:, 1, 0:SLOT_TILES]).then_inc(s.ids_ready, 1)
            dve.wait_ge(s.tables_loaded, 32)
            flat_words = words.rearrange("p b o w -> p (b o w)")
            for sh in range(8):
                ins = dve.scalar_tensor_tensor(bits[:, :, :, sh].rearrange("p b m -> p (b m)"), flat_words, sh,
                                               low_bits.broadcast_to([P, 4 * 4 * 16]),
                                               ALU.logical_shift_right, ALU.bitwise_and)
            link(ins)
            for b in range(1, 4):
                link(dve.scalar_tensor_tensor(bits[:, 0], bits[:, b], b, bits[:, 0],
                                              ALU.logical_shift_left, ALU.bitwise_or))
            link(dve.tensor_copy(code.rearrange("p o (w j n) -> p (o w) n j", j=4, n=8),
                                 bits[:, 0].rearrange("p m n -> p (m n)").bitcast(mybir.dt.uint8)
                                 .rearrange("p (m n j) -> p m n j", n=8, j=4)))

            def expert_turn(it):
                for u in range(UNROLL):
                    dve.wait_ge(S_(f"th2_done{u}"), it + 1)
                    dve.scalar_tensor_tensor(th2[u], th2[u], 1.0, ps[:, 2 + u, 0:EI], ALU.add, ALU.mult).then_inc(S_(f"act2_ready{u}"), 1)
                    dve.wait_ge(S_(f"act2_ready{u}"), 2 * it + 1)
                    dve.scalar_tensor_tensor(act2[u], th2[u], 0.5, ps[:, 2 + u, EI:2 * EI], ALU.mult, ALU.mult).then_inc(S_(f"act2_ready{u}"), 1)
                dve.wait_ge(s.added, it + 1)
                dve.scalar_tensor_tensor(picked, code, codes[:, bass.ds(it, 1)],
                                         lut[:, :, bass.ds(it, 1)].broadcast_to([P, 4, T]),
                                         ALU.is_equal, ALU.mult).then_inc(s.picked_ready, 1)
                dve.wait_ge(s.picked_ready, it + 1)
                dve.tensor_tensor(wl, wl, picked, ALU.add).then_inc(s.added, 1)

            expert_turn(0)
            with dve.Fori(1, TURNS) as it:
                expert_turn(it)
            dve.wait_ge(s.const3_loaded, 16 * 5)
            dve.tensor_scalar(bias_ffn, bias_ffn, gates[:, 3:4], None, ALU.mult).then_inc(s.gated_bias, 1)

            def mix(i):
                for k in range(2):
                    if k:
                        dve.wait_ge(s.half_mixed, 1)
                        dve.sem_clear(s.half_mixed)
                    dve.wait_ge((s.y1_gathered, s.y2_gathered)[k], 16 * (i + 1))
                    dve.scalar_tensor_tensor(X[:, bass.ds(i, 1), :], yg[k].unsqueeze(1), comb[:, k, bass.ds(i, 1)],
                                             X[:, bass.ds(i, 1), :], ALU.mult, ALU.add).then_inc(s.half_mixed, 1)
                dve.wait_ge(s.half_mixed, 1)
                dve.sem_clear(s.half_mixed)
                statistics(row_tile(i))
                root_in()
                normalise(row_tile(i), xn[:, :], s.xn_ready)

            def copy_qk(i, m):
                dve.wait_ge((s.q3_done, s.k3_done)[m], i + 1)
                dve.tensor_tensor((qT, kT)[m].rearrange("p (j o) -> p j o", j=TC),
                                  ps[:, 2 + m, :].rearrange("p (j o) -> p j o", j=TC),
                                  bqk[:, m, :].unsqueeze(1).broadcast_to([P, TC, P]), ALU.add).then_inc(s.qk3_ready, 1)

            s3v = ps[:, 0:2, 0:4 * C].rearrange("p f (j e) -> p f j e", e=C)
            d3v = pr.rearrange("p (j f e) -> p f j e", f=2, e=C)

            def per_head(t):
                return t.rearrange("p (f j) -> p f j", f=2).unsqueeze(3).broadcast_to([P, 2, 4, C])

            def finish(i):
                dve.wait_ge(s.bias_added, i + 1)
                dve.wait_ge(s.y3_done, i + 1)
                if later(i):
                    dve.wait_ge(s.out_stored, 16 * i)
                dve.scalar_tensor_tensor(obuf.unsqueeze(1), ps[:, 7:8, :], gates[:, 3:4], X[:, bass.ds(i, 1), :],
                                         ALU.mult, ALU.add).then_inc(s.out_ready, 1)

            def residual3(i):
                dve.wait_ge(s.xo3_ready, i + 1)
                dve.tensor_tensor(X[:, bass.ds(i, 1), :], X[:, bass.ds(i, 1), :], xo[:, :].unsqueeze(1),
                                  ALU.add).then_inc(s.x1_ready, 1)
                dve.wait_ge(s.x1_ready, 1)
                dve.sem_clear(s.x1_ready)
                statistics(row_tile(i))

            def finish_residual3(i):
                root_in()
                if later(i):
                    dve.wait_ge(s.xf_turned, i)
                normalise(row_tile(i), xf, s.normed)

            def turn3(i):
                dve.wait_ge(s.s3_done, i + 1)
                dve.tensor_reduce(m3, s3v, AX.X, ALU.max).then_inc(s.d_link, 1)
                dve.wait_ge(s.d_link, 3 * i + 1)
                dve.tensor_tensor(d3v, s3v, per_head(m3), ALU.subtract).then_inc(s.d3_ready, 1)
                if later(i):
                    residual3(i - 1)
                dve.wait_ge(s.e3_done, i + 1)
                dve.tensor_reduce(s3, d3v, AX.X, ALU.add).then_inc(s.d_link, 1)
                dve.wait_ge(s.d_link, 3 * i + 2)
                dve.reciprocal(r3, s3).then_inc(s.d_link, 1)
                dve.wait_ge(s.d_link, 3 * i + 3)
                dve.tensor_tensor(d3v, d3v, per_head(r3), ALU.mult).then_inc(s.p3_ready, 1)
                if later(i):
                    finish_residual3(i - 1)
                if follows(i, 1):
                    copy_qk(i + 1, 0)
                    copy_qk(i + 1, 1)
                if follows(i, 2):
                    mix(i + 2)
                if later(i, 2):
                    finish(i - 2)

            mix(0)
            for m in range(2):
                copy_qk(0, m)
            mix(1)
            turn3(0)
            turn3(1)
            with dve.Fori(2, TILES - 2) as i:
                turn3(i)
            for i in range(TILES - 2, TILES):
                turn3(i)
            residual3(TILES - 1)
            finish_residual3(TILES - 1)
            finish(TILES - 2)
            finish(TILES - 1)

        @block.tensor
        def _(pe):
            def mm(out, lhsT, rhs, start=True, stop=True, **kw):
                return pe.matmul(out, lhsT, rhs, start=start, stop=stop, **kw)

            def turn4(out, src, done):
                for j in range(4):
                    ins = pe.transpose(out[:, j * P:(j + 1) * P], src[:, j * P:(j + 1) * P], ident[:, :])
                ins.then_inc(done, 1)

            def project(i, n):
                if n == 0:
                    pe.wait_ge(s.a_normed, i + 1)
                    if later(i):
                        pe.wait_ge(s.copied, 3 * i)
                    mm(ps[:, 4, :], w_att[:, 0, :], xn[:, :]).then_inc(s.projected, 1)
                elif n == 1:
                    pe.wait_ge(s.ctx_loaded, 16 * (i + 1))
                    if later(i, 2):
                        pe.wait_ge(s.xo_ready, i - 1)
                    mm(ps[:, 5, :], w_att[:, 1, :], ctx_t[:, :]).then_inc(s.projected, 1)
                else:
                    pe.wait_ge(s.copied, 3 * i + 1)
                    mm(ps[:, 4, :], w_att[:, 2, :], ctx_t[:, :]).then_inc(s.projected, 1)

            def add_pair(i, c, pools, dves, base_p, base_d):
                if c in pools:
                    n = base_p + pools.index(c)
                    pe.wait_ge(s.p_pair, N_POOL * i + n + 1)
                    return sp_[n % SP_], s.p_summed
                n = base_d + dves.index(c)
                pe.wait_ge(s.d_pair, N_DVE * i + n + 1)
                return sd[n % SD], s.d_summed

            def scores(i):
                for c in range(PAIRS):
                    zz, done = add_pair(i, c, QK_POOL, QK_DVE, 0, 0)
                    if c == 0 and later(i):
                        pe.wait_ge(s.diff_read, i)
                    zz = zz.rearrange("p (w d t) -> p w d t", w=2, t=CT)
                    for d in range(HD // 2):
                        ins = mm(ps[:, c // 4, c % 4 * 2 * CT:(c % 4 + 1) * 2 * CT], ident[:, :], zz[:, :, d, :],
                                 d == 0, d == HD // 2 - 1)
                    ins.then_inc(done, 1)

            def outputs(i, c):
                zz, done = add_pair(i, c, AV_POOL, AV_DVE, len(QK_POOL), len(QK_DVE))
                if c == 0 and later(i):
                    pe.wait_ge(s.o2_ready, i)
                mm(ps[:, 6, :], ident[:, :], zz, c == 0, c == PAIRS - 1).then_inc(done, 1)

            def wo(i):
                pe.wait_ge(s.oT_loaded, 16 * (i + 1))
                mm(ps[:, 5, :], w_att[:, 3, :], oT).then_inc(s.wo_done, 1)

            def turn_x2(i):
                pe.wait_ge(s.b_normed, i + 1)
                turn4(ps[:, 7, :], x2, s.x2_turned)

            def route(i):
                pe.wait_ge(s.x2T_ready, i + 1)
                for k in range(TC):
                    ins = mm(ps[:, 7, 0:EXPERTS], x2T[:, k * P:(k + 1) * P], w_router[:, k, :], k == 0, k == TC - 1)
                ins.then_inc(s.logits_done, 1)

            def gate_up(i, n):
                half, k = divmod(n, TC)
                if n == TC and later(i):
                    pe.wait_ge(s.xffn_ready, i)
                ins = mm(ps[:, 2 + half, :], x2T[:, k * P:(k + 1) * P], w_sgu[:, k, half * SI:(half + 1) * SI], k == 0, k == TC - 1)
                if k == TC - 1:
                    ins.then_inc(s.u_done if half else s.g_done, 1)

            def turn_act(i):
                pe.wait_ge(s.act_ready, i + 1)
                pe.wait_ge(s.logits_read, i + 1)
                turn4(ps[:, 7, :], act, s.act_turned)

            def down(i):
                pe.wait_ge(s.actT_ready, i + 1)
                for k in range(4):
                    ins = mm(ps[:, 3, :], actT[:, k * P:(k + 1) * P], w_sdn[:, k, :], k == 0, k == 3)
                ins.then_inc(s.down_done, 1)

            pe.wait_ge(s.small_loaded, 16 * N_FIRST)
            pe.wait_ge(s.ident_done, 2)
            def turn(i, before2=True, before=True, after=True):
                scores(i)
                if before:
                    wo(i - 1)
                if before2:
                    down(i - 2)
                if after:
                    project(i + 1, 0)
                    project(i + 1, 1)
                if before:
                    turn_x2(i - 1)
                if after:
                    project(i + 1, 2)
                if before:
                    route(i - 1)
                    for n in range(2 * TC):
                        gate_up(i - 1, n)
                for c in range(PAIRS):
                    outputs(i, c)
                    if before and c == 5:
                        turn_act(i - 1)

            for n in range(3):
                project(0, n)
            turn(0, before2=False, before=False)
            pe.wait_ge(s.shared_loaded, 16 * 3)
            turn(1, before2=False)
            with pe.Fori(2, TILES - 1) as i:
                turn(i)
            turn(TILES - 1, after=False)
            wo(TILES - 1)
            down(TILES - 2)
            turn_x2(TILES - 1)
            route(TILES - 1)
            for n in range(TC):
                gate_up(TILES - 1, n)
            pe.wait_ge(s.tri_ready, 8)
            pe.wait_ge(s.c_link, 1)
            flat = chosen.rearrange("p i e -> p (i e)")
            mm(ps[:, 0, 0:TILES * EXPERTS], tri, flat)
            mm(ps[:, 1, 0:TILES * EXPERTS], ones, flat).then_inc(s.ranked, 1)
            for n in range(TC, 2 * TC):
                gate_up(TILES - 1, n)
            turn_act(TILES - 1)
            down(TILES - 1)
            for c in range(2 * TILES):
                pe.wait_ge(s.to_row_ready, c + 1)
                by_pool = sum(n <= c for n in POOL_CHOICES)
                if c in POOL_CHOICES:
                    pe.wait_ge(s.p_to_tile_ready, by_pool)
                else:
                    pe.wait_ge(s.d_to_tile_ready, c + 1 - by_pool)
                ins = mm(ps[:, 1, 0:SLOT_TILES], to_row[:, c, :], to_tile[:, c, :], c == 0, c == 2 * TILES - 1)
            ins.then_inc(s.ids_summed, 1)
            pe.wait_ge(s.experts_known, 1)
            pe.wait_ge(s.ids_ready, 1)
            pe.wait_ge(s.experts_loaded, 16 * 2 * (EXPERTS - LATE_EXPERTS))
            pe.wait_ge(s.late_loaded, 16 * 2 * LATE_EXPERTS)

            def expert_of(it, u):
                return pe.value_load(exp_id[0:1, bass.ds(UNROLL * it + u, 1)], min_val=0, max_val=EXPERTS - 1)

            def turn_xg(it, u):
                pe.wait_ge(S_(f"gathered{u}"), 16 * (it + 1))
                turn4(ps[:, u % 2, :], xg[u], S_(f"turned{u}"))

            def turn_act2(it):
                for u in range(UNROLL):
                    pe.wait_ge(S_(f"act2_ready{u}"), 2 * it + 2)
                    pe.transpose(ps[:, 2 + u, 0:EI], act2[u], ident[:, :]).then_inc(S_(f"act2_turned{u}"), 1)

            def expert_down(it):
                for u in range(UNROLL):
                    e = expert_of(it, u)
                    pe.wait_ge(S_(f"act2T_ready{u}"), it + 1)
                    if later(it):
                        pe.wait_ge(S_(f"ysb_ready{u}"), it)
                    mm(ps[:, 5 + u, :], act2T[u], w_dn[:, bass.ds(e, 1), :]).then_inc(S_(f"dn_done{u}"), 1)

            def expert_turn(it):
                turn_xg(it, 0)
                turn_xg(it, 1)
                if later(it):
                    turn_act2(it - 1)
                pe.wait_ge(s.xT_ready0, it + 1)
                turn_xg(it, 2)
                if later(it):
                    expert_down(it - 1)
                for u in range(UNROLL):
                    e = expert_of(it, u)
                    pe.wait_ge(S_(f"xT_ready{u}"), it + 1)
                    for k in range(TC):
                        ins = mm(ps[:, 2 + u, 0:2 * EI], xT[u][:, k * P:(k + 1) * P],
                                 w_gu[:, bass.ds(e, 1), k, :], k == 0, k == TC - 1)
                    ins.then_inc(S_(f"gu_done{u}"), 1)

            expert_turn(0)
            expert_turn(1)
            with pe.Fori(2, TURNS) as it:
                expert_turn(it)
            turn_act2(TURNS - 1)
            expert_down(TURNS - 1)

            def q3(i):
                pe.wait_ge(s.xn_ready, i + 1)
                for j in range(TC):
                    ins = mm(ps[:, 2, j * P:(j + 1) * P], xn[:, j * P:(j + 1) * P], w_att[:, 4, :])
                ins.then_inc(s.q3_done, 1)

            def k3(i):
                pe.wait_ge(s.ctx_loaded, 16 * (TILES + 1 + i))
                for j in range(TC):
                    ins = mm(ps[:, 3, j * P:(j + 1) * P], ctx_t[:, j * P:(j + 1) * P], w_att[:, 5, :])
                ins.then_inc(s.k3_done, 1)

            def v3(i):
                if later(i):
                    pe.wait_ge(s.v3_copied, 3 * i)
                mm(ps[:, 4, :], w_att[:, 6, :], ctx_t[:, :]).then_inc(s.v_done, 1)

            def scores(i):
                pe.wait_ge(s.qk3_ready, 2)
                pe.sem_clear(s.qk3_ready)
                for f in range(2):
                    rows = slice(f * LH, (f + 1) * LH)
                    for b in range(2):
                        for j in range(TC):
                            at = slice(j * P + b * C, j * P + (b + 1) * C)
                            ins = mm(ps[b * C:(b + 1) * C, f, j * C:(j + 1) * C], qT[rows, at], kT[rows, at])
                ins.then_inc(s.s3_done, 1)

            def turn_p(i):
                pe.wait_ge(s.p3_ready, i + 1)
                turn4(ps[:, 6, :], pr, s.pT_done)

            def weighted(i):
                if not follows(i, 1):
                    pe.wait_ge(s.v3_copied, 3 * TILES)
                pe.wait_ge(s.prT_ready, 1)
                pe.sem_clear(s.prT_ready)
                for f in range(2):
                    rows = slice(f * C, (f + 1) * C)
                    for b in range(2):
                        v = vv[0 if b == f else 1]
                        for j in range(TC):
                            ins = mm(ps[b * C:(b + 1) * C, f, j * LH:(j + 1) * LH],
                                     prT[rows, j * P + b * C:j * P + (b + 1) * C],
                                     v[rows, (2 * j + f) * LH:(2 * j + f + 1) * LH])
                ins.then_inc(s.av_done, 1)

            def wo3(i):
                pe.wait_ge(s.xh_ready, i + 1)
                mm(ps[:, 6, :], w_att[:, 7, :], xh).then_inc(s.wo3_done, 1)

            def turn_xf(i):
                pe.wait_ge(s.normed, i + 1)
                turn4(ps[:, 5, :], xf, s.xf_turned)

            def linear(i, k):
                if k == 0:
                    pe.wait_ge(s.xfT_ready, i + 1)
                    if later(i):
                        pe.wait_ge(s.out_ready, i)
                ins = mm(ps[:, 7, :], xfT[:, k * P:(k + 1) * P], wlT[:, k, :], k == 0, k == 3)
                if k == 3:
                    ins.then_inc(s.y3_done, 1)

            def turn3(i):
                scores(i)
                if follows(i, 1):
                    q3(i + 1)
                    k3(i + 1)
                    v3(i + 1)
                if later(i, 2):
                    for k in range(3):
                        linear(i - 2, k)
                turn_p(i)
                if later(i, 2):
                    linear(i - 2, 3)
                weighted(i)
                if later(i):
                    turn_xf(i - 1)
                wo3(i)

            pe.wait_ge(s.layer1_loaded, 16 * N_LAYER1)
            k3(0)
            pe.wait_ge(s.ysb_ready0, TURNS)
            v3(0)
            pe.wait_ge(s.ysb_ready1, TURNS)
            pe.wait_ge(s.ysb_ready2, TURNS)
            pe.wait_ge(s.added, 1 + CODES)
            for k in range(4):
                for o in range(4):
                    ins = pe.transpose(ps[:, WL_BANKS[k], o * P:(o + 1) * P], wl[:, o, k * P:(k + 1) * P], ident[:, :])
                ins.then_inc(s.wl_turned, 1)
            q3(0)
            pe.wait_ge(s.wlT_ready, 4)
            turn3(0)
            turn3(1)
            with pe.Fori(2, TILES - 1) as i:
                turn3(i)
            turn3(TILES - 1)
            for k in range(4):
                linear(TILES - 2, k)
            turn_xf(TILES - 1)
            for k in range(4):
                linear(TILES - 1, k)


_NAMES = ["x", "ctx", "gate4", "w_att0", "w_att1", "b_att", "bq1", "bk1", "w_router", "w_sgu", "w_sdn",
          "w_gu", "w_dn", "lut4", "words", "bias"]


def kernel(**inputs):
    import numpy as np
    import concourse.bacc as bacc
    from concourse.bass_utils import run_bass_kernel_spmd as run

    v = {k: np.asarray(t) for k, t in inputs.items()}

    def by_rows(w, chunks):
        return w.T.reshape(chunks, P, w.shape[0]).transpose(1, 0, 2)

    laid = {"x": v["x"], "ctx": v["ctx_4096"], "gate4": np.concatenate([v["g_xattn"], v["g_ffn"]])}
    for layer in range(2):
        laid[f"w_att{layer}"] = np.stack([v[f"L{layer}_xattn_W{m}"].T for m in "qkvo"], axis=1)
    laid["b_att"] = np.stack([v[f"L{layer}_xattn_b{m}"] for layer in range(2) for m in "qkvo"], axis=1)
    laid["bq1"], laid["bk1"] = v["L1_xattn_bq"], v["L1_xattn_bk"]
    laid["w_router"] = by_rows(v["L0_ffn_gate_w"], TC)
    laid["w_sgu"] = by_rows(v["L0_ffn_shared_w_gate_up"], TC)
    laid["w_sdn"] = by_rows(v["L0_ffn_shared_w_down"], 4)
    gu = v["L0_ffn_w_gate_up"].transpose(0, 2, 1).reshape(EXPERTS, TC, P, 2 * EI).transpose(0, 2, 1, 3)
    laid["w_gu"] = gu.reshape(EXPERTS * P, TC * 2 * EI)
    laid["w_dn"] = v["L0_ffn_w_down"].transpose(0, 2, 1).reshape(EXPERTS * P, T)
    laid["lut4"] = v["L1_ffn_lut4"].reshape(4, P, CODES).transpose(1, 0, 2)
    laid["words"] = v["L1_ffn_qweight"][0:4].reshape(4, 4, P, T // 32).transpose(2, 0, 1, 3)
    laid["bias"] = v["L1_ffn_bias"]

    nc = bacc.Bacc("TRN2", target_bir_lowering=False, num_devices=1)
    arrays, aps = {}, {}
    for name in _NAMES:
        t = np.ascontiguousarray(laid[name])
        arrays[f"in_{name}"] = t
        aps[name] = nc.dram_tensor(f"in_{name}", t.shape, mybir.dt.from_np(t.dtype), kind="ExternalInput").ap()
    aps["out"] = nc.dram_tensor("out_0", (B, C, T), F32, kind="ExternalOutput").ap()
    build(nc, aps)
    r = run(nc, [arrays], core_ids=[0])
    return r.results[0]["out_0"]
```
